# Optimizing a Trainium2 kernel written in Bass

```python
import numpy as np
import jax
import jax.numpy as jnp

def _softmax(x, axis=-1):
    return jax.nn.softmax(x, axis=axis)

def _gelu(x):
    return jax.nn.gelu(x, approximate=True)

def _silu(x):
    return jax.nn.silu(x)

def _sigmoid(x):
    return jax.nn.sigmoid(x)

def _layernorm(x, axis=-1, eps=1e-05):
    m = jnp.mean(x, axis=axis, keepdims=True)
    v = jnp.var(x, axis=axis, keepdims=True)
    return (x - m) / jnp.sqrt(v + eps)

def _scatter_add(tgt, idx, src, axis=0):
    return tgt.at[idx].add(src)

def _segment_sum(src, seg, n):
    return jax.ops.segment_sum(src, seg, n)
kernel_name = 'mk_recurrent_d2_jaxref_r8_1f73c6'

def setup_inputs(seed: int=0):
    np.random.seed(seed)
    _w = jnp.asarray

    def _L0_attn_setup():
        import jax, jax.numpy as jnp
        import numpy as np
        DIM = 128
        HEADS = 16
        DIM_HEAD = DIM // HEADS
        LATENT = DIM // 4
        SCALE = DIM_HEAD ** (-0.5)
        key = jax.random.key(seed)
        ks = jax.random.split(key, 8)
        B, S = (2, 256)
        init = lambda k, shape, fan_in: jax.random.normal(k, shape, jnp.float32) * fan_in ** (-0.5)
        return {'x': jax.random.normal(ks[0], (B, S, DIM), jnp.float32), 'Wq': init(ks[1], (DIM, DIM), DIM), 'bq': jnp.zeros((DIM,), jnp.float32), 'Wl': init(ks[2], (DIM, LATENT), DIM), 'bl': jnp.zeros((LATENT,), jnp.float32), 'Wk': init(ks[3], (LATENT, DIM), LATENT), 'bk': jnp.zeros((DIM,), jnp.float32), 'Wv': init(ks[4], (LATENT, DIM), LATENT), 'bv': jnp.zeros((DIM,), jnp.float32), 'Wo': init(ks[5], (DIM, DIM), DIM), 'bo': jnp.zeros((DIM,), jnp.float32)}
    _L0_attn_in = _L0_attn_setup()

    def _L0_ffn_setup():
        import jax, jax.numpy as jnp
        import numpy as np
        DIM = 128
        DEPTH = 2
        HEADS = 8
        DIM_HEAD = 64
        WINDOW = 64
        INNER = HEADS * DIM_HEAD
        HID = int(DIM * 4 * 2 / 3)
        B, N = (2, 1024)
        QK_SCALE = 8.0

        def shift_token(t):
            t1, t2 = jnp.split(t, 2, axis=-1)
            t2 = jnp.pad(t2, ((0, 0), (1, 0), (0, 0)))[:, :-1]
            return jnp.concatenate([t1, t2], axis=-1)

        def l2norm(t):
            return t / jnp.clip(jnp.linalg.norm(t, axis=-1, keepdims=True), 1e-12)

        def rotate_half(x):
            x1, x2 = jnp.split(x, 2, axis=-1)
            return jnp.concatenate([-x2, x1], axis=-1)

        def rotary_xpos(q, k):
            n = q.shape[-2]
            half_idx = jnp.arange(0, DIM_HEAD, 2, dtype=jnp.float32)
            inv_freq = 1.0 / 10000.0 ** (half_idx / DIM_HEAD)
            t = jnp.arange(n, dtype=jnp.float32)
            freqs = t[:, None] * inv_freq[None, :]
            freqs = jnp.concatenate([freqs, freqs], axis=-1)
            base = (half_idx + 0.4 * DIM_HEAD) / (1.4 * DIM_HEAD)
            power = (t - n // 2) / float(WINDOW // 2)
            scale = base[None, :] ** power[:, None]
            scale = jnp.concatenate([scale, scale], axis=-1)
            cos, sin = (jnp.cos(freqs), jnp.sin(freqs))
            q = q * cos * scale + rotate_half(q) * sin * scale
            k = k * cos / scale + rotate_half(k) * sin / scale
            return (q, k)

        def local_attention(q, k, v):
            b, h, n, d = q.shape
            w = n // WINDOW
            bq = q.reshape(b, h, w, WINDOW, d) * QK_SCALE
            bk = k.reshape(b, h, w, WINDOW, d)
            bv = v.reshape(b, h, w, WINDOW, d)

            def look_around(t):
                p = jnp.pad(t, ((0, 0), (0, 0), (1, 0), (0, 0), (0, 0)))
                return jnp.concatenate([p[:, :, :w], p[:, :, 1:]], axis=3)
            bk, bv = (look_around(bk), look_around(bv))
            bt = jnp.arange(n).reshape(w, WINDOW)
            btp = jnp.pad(bt, ((1, 0), (0, 0)), constant_values=-1)
            btk = jnp.concatenate([btp[:w], btp[1:]], axis=1)
            sim = jnp.einsum('bhwid,bhwjd->bhwij', bq, bk)
            i = bt[:, :, None]
            j = btk[:, None, :]
            mask = (i < j) | (i > j + WINDOW) | (j == -1)
            sim = jnp.where(mask, -jnp.finfo(sim.dtype).max, sim)
            attn = jax.nn.softmax(sim, axis=-1)
            out = jnp.einsum('bhwij,bhwjd->bhwid', attn, bv)
            return out.reshape(b, h, n, d)

        def _layer(x, wqkv, qs, ksc, wo, lg, lb, w1, b1, w2, b2):
            b, n, _ = x.shape
            h = shift_token(x)
            qkv = h @ wqkv
            q, k, v = jnp.split(qkv, 3, axis=-1)
            to_heads = lambda t: t.reshape(b, n, HEADS, DIM_HEAD).transpose(0, 2, 1, 3)
            q, k, v = (to_heads(q), to_heads(k), to_heads(v))
            q = l2norm(q) * qs
            k = l2norm(k) * ksc
            q, k = rotary_xpos(q, k)
            o = local_attention(q, k, v)
            o = o.transpose(0, 2, 1, 3).reshape(b, n, INNER)
            x = x + o @ wo
            h = shift_token(x)
            mu = h.mean(-1, keepdims=True)
            var = h.var(-1, keepdims=True)
            h = (h - mu) / jnp.sqrt(var + 1e-05) * lg + lb
            h = h @ w1 + b1
            a, g = jnp.split(h, 2, axis=-1)
            h = a * jax.nn.gelu(g, approximate=False)
            x = x + h @ w2 + b2
            return x
        key = jax.random.key(seed)
        ks = jax.random.split(key, 6)
        return {'x': jax.random.normal(ks[0], (B, N, DIM), jnp.float32), 'wqkv': jax.random.normal(ks[1], (DEPTH, DIM, 3 * INNER), jnp.float32) * 0.02, 'q_scale': jnp.ones((DEPTH, DIM_HEAD), jnp.float32), 'k_scale': jnp.ones((DEPTH, DIM_HEAD), jnp.float32), 'wo': jax.random.normal(ks[2], (DEPTH, INNER, DIM), jnp.float32) * 0.02, 'ln_g': jnp.ones((DEPTH, DIM), jnp.float32), 'ln_b': jnp.zeros((DEPTH, DIM), jnp.float32), 'w1': jax.random.normal(ks[3], (DEPTH, DIM, 2 * HID), jnp.float32) * 0.02, 'b1': jnp.zeros((DEPTH, 2 * HID), jnp.float32), 'w2': jax.random.normal(ks[4], (DEPTH, HID, DIM), jnp.float32) * 0.02, 'b2': jnp.zeros((DEPTH, DIM), jnp.float32)}
    _L0_ffn_in = _L0_ffn_setup()

    def _L1_attn_setup():
        import jax, jax.numpy as jnp
        import numpy as np
        from jax import lax
        D_MODEL, D_STATE, D_CONV, EXPAND, HEADDIM = (128, 128, 4, 2, 64)
        D_INNER = EXPAND * D_MODEL
        NHEADS = D_INNER // HEADDIM
        CONV_DIM = D_INNER + 2 * D_STATE
        D_IN_PROJ = 2 * D_INNER + 2 * D_STATE + NHEADS

        def _mamba2(x, in_proj_w, conv_w, conv_b, dt_bias, A_log, D, norm_w, out_proj_w):
            b, l, _ = x.shape
            zxbcdt = x @ in_proj_w.T
            z = zxbcdt[..., :D_INNER]
            xBC = zxbcdt[..., D_INNER:D_INNER + CONV_DIM]
            dt = zxbcdt[..., D_INNER + CONV_DIM:]
            xBC_pad = jnp.pad(xBC, ((0, 0), (D_CONV - 1, 0), (0, 0)))
            windows = jnp.stack([xBC_pad[:, k:k + l, :] for k in range(D_CONV)], axis=-1)
            xBC = jax.nn.silu(jnp.einsum('blck,ck->blc', windows, conv_w) + conv_b)
            xs = xBC[..., :D_INNER]
            B = xBC[..., D_INNER:D_INNER + D_STATE]
            C = xBC[..., D_INNER + D_STATE:]
            xh = xs.reshape(b, l, NHEADS, HEADDIM)
            dt = jax.nn.softplus(dt + dt_bias)
            A = -jnp.exp(A_log)
            dA = jnp.exp(dt * A)
            xdt = xh * dt[..., None]

            def step(S, inp):
                dA_t, xdt_t, B_t, C_t = inp
                S = dA_t[:, :, None, None] * S + xdt_t[..., None] * B_t[:, None, None, :]
                y_t = jnp.einsum('bhpn,bn->bhp', S, C_t)
                return (S, y_t)
            S0 = jnp.zeros((b, NHEADS, HEADDIM, D_STATE), x.dtype)
            _, y = lax.scan(step, S0, (dA.transpose(1, 0, 2), xdt.transpose(1, 0, 2, 3), B.transpose(1, 0, 2), C.transpose(1, 0, 2)))
            y = y.transpose(1, 0, 2, 3) + D[None, None, :, None] * xh
            y = y.reshape(b, l, D_INNER)
            y = y * jax.nn.silu(z)
            y = y * lax.rsqrt(jnp.mean(y * y, axis=-1, keepdims=True) + 1e-05) * norm_w
            return y @ out_proj_w.T
        key = jax.random.key(seed)
        ks = jax.random.split(key, 9)
        b, l = (2, 256)
        x = jax.random.normal(ks[0], (b, l, D_MODEL), jnp.float32)
        in_proj_w = jax.random.normal(ks[1], (D_IN_PROJ, D_MODEL), jnp.float32) * 0.02
        conv_w = jax.random.normal(ks[2], (CONV_DIM, D_CONV), jnp.float32) * 0.2
        conv_b = jax.random.normal(ks[3], (CONV_DIM,), jnp.float32) * 0.02
        dt_bias = jnp.log(jnp.expm1(jax.random.uniform(ks[4], (NHEADS,), jnp.float32, 0.001, 0.1)))
        A_log = jnp.log(jax.random.uniform(ks[5], (NHEADS,), jnp.float32, 1.0, 16.0))
        D = jax.random.normal(ks[6], (NHEADS,), jnp.float32)
        norm_w = jnp.ones((D_INNER,), jnp.float32)
        out_proj_w = jax.random.normal(ks[7], (D_MODEL, D_INNER), jnp.float32) * 0.02
        return {'x': x, 'in_proj_w': in_proj_w, 'conv_w': conv_w, 'conv_b': conv_b, 'dt_bias': dt_bias, 'A_log': A_log, 'D': D, 'norm_w': norm_w, 'out_proj_w': out_proj_w}
    _L1_attn_in = _L1_attn_setup()

    def _L1_ffn_setup():
        import jax, jax.numpy as jnp
        import numpy as np
        NEG_INF = -1e+30
        K = 2
        key = jax.random.key(seed)
        ks = jax.random.split(key, 5)
        B, S, D, O, E = (8, 256, 128, 128, 8)
        scale = 1.0 / np.sqrt(D)
        return {'x': jax.random.normal(ks[0], (B, S, D), dtype=jnp.float32), 'gate_w': jax.random.normal(ks[1], (E, D), dtype=jnp.float32) * scale, 'gate_b': jnp.zeros((E,), dtype=jnp.float32), 'expert_w': jax.random.normal(ks[2], (E, O, D), dtype=jnp.float32) * scale, 'expert_b': jnp.zeros((E, O), dtype=jnp.float32)}
    _L1_ffn_in = _L1_ffn_setup()
    _d = {'L0_attn_x': _L0_attn_in['x'], 'L0_attn_Wq': _L0_attn_in['Wq'], 'L0_attn_bq': _L0_attn_in['bq'], 'L0_attn_Wl': _L0_attn_in['Wl'], 'L0_attn_bl': _L0_attn_in['bl'], 'L0_attn_Wk': _L0_attn_in['Wk'], 'L0_attn_bk': _L0_attn_in['bk'], 'L0_attn_Wv': _L0_attn_in['Wv'], 'L0_attn_bv': _L0_attn_in['bv'], 'L0_attn_Wo': _L0_attn_in['Wo'], 'L0_attn_bo': _L0_attn_in['bo'], 'L0_ffn_wqkv': _L0_ffn_in['wqkv'], 'L0_ffn_q_scale': _L0_ffn_in['q_scale'], 'L0_ffn_k_scale': _L0_ffn_in['k_scale'], 'L0_ffn_wo': _L0_ffn_in['wo'], 'L0_ffn_ln_g': _L0_ffn_in['ln_g'], 'L0_ffn_ln_b': _L0_ffn_in['ln_b'], 'L0_ffn_w1': _L0_ffn_in['w1'], 'L0_ffn_b1': _L0_ffn_in['b1'], 'L0_ffn_w2': _L0_ffn_in['w2'], 'L0_ffn_b2': _L0_ffn_in['b2'], 'L1_attn_in_proj_w': _L1_attn_in['in_proj_w'], 'L1_attn_conv_w': _L1_attn_in['conv_w'], 'L1_attn_conv_b': _L1_attn_in['conv_b'], 'L1_attn_dt_bias': _L1_attn_in['dt_bias'], 'L1_attn_A_log': _L1_attn_in['A_log'], 'L1_attn_D': _L1_attn_in['D'], 'L1_attn_norm_w': _L1_attn_in['norm_w'], 'L1_attn_out_proj_w': _L1_attn_in['out_proj_w'], 'L1_ffn_gate_w': _L1_ffn_in['gate_w'], 'L1_ffn_gate_b': _L1_ffn_in['gate_b'], 'L1_ffn_expert_w': _L1_ffn_in['expert_w'], 'L1_ffn_expert_b': _L1_ffn_in['expert_b']}
    _x0 = _d['L0_attn_x']
    _d['L0_attn_x'] = jax.random.normal(jax.random.fold_in(jax.random.key(seed), 1), (16, 256, 128), dtype=_x0.dtype)
    del _x0
    return _d

def reference(L0_attn_x, L0_attn_Wq, L0_attn_bq, L0_attn_Wl, L0_attn_bl, L0_attn_Wk, L0_attn_bk, L0_attn_Wv, L0_attn_bv, L0_attn_Wo, L0_attn_bo, L0_ffn_wqkv, L0_ffn_q_scale, L0_ffn_k_scale, L0_ffn_wo, L0_ffn_ln_g, L0_ffn_ln_b, L0_ffn_w1, L0_ffn_b1, L0_ffn_w2, L0_ffn_b2, L1_attn_in_proj_w, L1_attn_conv_w, L1_attn_conv_b, L1_attn_dt_bias, L1_attn_A_log, L1_attn_D, L1_attn_norm_w, L1_attn_out_proj_w, L1_ffn_gate_w, L1_ffn_gate_b, L1_ffn_expert_w, L1_ffn_expert_b):

    def _L0_attn_ref(x, Wq, bq, Wl, bl, Wk, bk, Wv, bv, Wo, bo):
        import jax, jax.numpy as jnp
        import numpy as np
        DIM = 128
        HEADS = 16
        DIM_HEAD = DIM // HEADS
        LATENT = DIM // 4
        SCALE = DIM_HEAD ** (-0.5)
        B, S, D = x.shape
        H, Dh = (HEADS, DIM_HEAD)
        q = (x @ Wq + bq).reshape(B, S, H, Dh)
        latent = x @ Wl + bl
        k = (latent @ Wk + bk).reshape(B, S, H, Dh)
        v = (latent @ Wv + bv).reshape(B, S, H, Dh)
        scores = jnp.einsum('bihd,bjhd->bhij', q, k) * SCALE
        attn = jax.nn.softmax(scores, axis=-1)
        out = jnp.einsum('bhij,bjhd->bihd', attn, v).reshape(B, S, D)
        out = out @ Wo + bo
        return out

    def _L0_ffn_ref(x, wqkv, q_scale, k_scale, wo, ln_g, ln_b, w1, b1, w2, b2):
        import jax, jax.numpy as jnp
        import numpy as np
        DIM = 128
        DEPTH = 2
        HEADS = 8
        DIM_HEAD = 64
        WINDOW = 64
        INNER = HEADS * DIM_HEAD
        HID = int(DIM * 4 * 2 / 3)
        B, N = (2, 1024)
        QK_SCALE = 8.0

        def shift_token(t):
            t1, t2 = jnp.split(t, 2, axis=-1)
            t2 = jnp.pad(t2, ((0, 0), (1, 0), (0, 0)))[:, :-1]
            return jnp.concatenate([t1, t2], axis=-1)

        def l2norm(t):
            return t / jnp.clip(jnp.linalg.norm(t, axis=-1, keepdims=True), 1e-12)

        def rotate_half(x):
            x1, x2 = jnp.split(x, 2, axis=-1)
            return jnp.concatenate([-x2, x1], axis=-1)

        def rotary_xpos(q, k):
            n = q.shape[-2]
            half_idx = jnp.arange(0, DIM_HEAD, 2, dtype=jnp.float32)
            inv_freq = 1.0 / 10000.0 ** (half_idx / DIM_HEAD)
            t = jnp.arange(n, dtype=jnp.float32)
            freqs = t[:, None] * inv_freq[None, :]
            freqs = jnp.concatenate([freqs, freqs], axis=-1)
            base = (half_idx + 0.4 * DIM_HEAD) / (1.4 * DIM_HEAD)
            power = (t - n // 2) / float(WINDOW // 2)
            scale = base[None, :] ** power[:, None]
            scale = jnp.concatenate([scale, scale], axis=-1)
            cos, sin = (jnp.cos(freqs), jnp.sin(freqs))
            q = q * cos * scale + rotate_half(q) * sin * scale
            k = k * cos / scale + rotate_half(k) * sin / scale
            return (q, k)

        def local_attention(q, k, v):
            b, h, n, d = q.shape
            w = n // WINDOW
            bq = q.reshape(b, h, w, WINDOW, d) * QK_SCALE
            bk = k.reshape(b, h, w, WINDOW, d)
            bv = v.reshape(b, h, w, WINDOW, d)

            def look_around(t):
                p = jnp.pad(t, ((0, 0), (0, 0), (1, 0), (0, 0), (0, 0)))
                return jnp.concatenate([p[:, :, :w], p[:, :, 1:]], axis=3)
            bk, bv = (look_around(bk), look_around(bv))
            bt = jnp.arange(n).reshape(w, WINDOW)
            btp = jnp.pad(bt, ((1, 0), (0, 0)), constant_values=-1)
            btk = jnp.concatenate([btp[:w], btp[1:]], axis=1)
            sim = jnp.einsum('bhwid,bhwjd->bhwij', bq, bk)
            i = bt[:, :, None]
            j = btk[:, None, :]
            mask = (i < j) | (i > j + WINDOW) | (j == -1)
            sim = jnp.where(mask, -jnp.finfo(sim.dtype).max, sim)
            attn = jax.nn.softmax(sim, axis=-1)
            out = jnp.einsum('bhwij,bhwjd->bhwid', attn, bv)
            return out.reshape(b, h, n, d)

        def _layer(x, wqkv, qs, ksc, wo, lg, lb, w1, b1, w2, b2):
            b, n, _ = x.shape
            h = shift_token(x)
            qkv = h @ wqkv
            q, k, v = jnp.split(qkv, 3, axis=-1)
            to_heads = lambda t: t.reshape(b, n, HEADS, DIM_HEAD).transpose(0, 2, 1, 3)
            q, k, v = (to_heads(q), to_heads(k), to_heads(v))
            q = l2norm(q) * qs
            k = l2norm(k) * ksc
            q, k = rotary_xpos(q, k)
            o = local_attention(q, k, v)
            o = o.transpose(0, 2, 1, 3).reshape(b, n, INNER)
            x = x + o @ wo
            h = shift_token(x)
            mu = h.mean(-1, keepdims=True)
            var = h.var(-1, keepdims=True)
            h = (h - mu) / jnp.sqrt(var + 1e-05) * lg + lb
            h = h @ w1 + b1
            a, g = jnp.split(h, 2, axis=-1)
            h = a * jax.nn.gelu(g, approximate=False)
            x = x + h @ w2 + b2
            return x
        for l in range(DEPTH):
            x = _layer(x, wqkv[l], q_scale[l], k_scale[l], wo[l], ln_g[l], ln_b[l], w1[l], b1[l], w2[l], b2[l])
        return x

    def _L1_attn_ref(x, in_proj_w, conv_w, conv_b, dt_bias, A_log, D, norm_w, out_proj_w):
        import jax, jax.numpy as jnp
        import numpy as np
        from jax import lax
        D_MODEL, D_STATE, D_CONV, EXPAND, HEADDIM = (128, 128, 4, 2, 64)
        D_INNER = EXPAND * D_MODEL
        NHEADS = D_INNER // HEADDIM
        CONV_DIM = D_INNER + 2 * D_STATE
        D_IN_PROJ = 2 * D_INNER + 2 * D_STATE + NHEADS

        def _mamba2(x, in_proj_w, conv_w, conv_b, dt_bias, A_log, D, norm_w, out_proj_w):
            b, l, _ = x.shape
            zxbcdt = x @ in_proj_w.T
            z = zxbcdt[..., :D_INNER]
            xBC = zxbcdt[..., D_INNER:D_INNER + CONV_DIM]
            dt = zxbcdt[..., D_INNER + CONV_DIM:]
            xBC_pad = jnp.pad(xBC, ((0, 0), (D_CONV - 1, 0), (0, 0)))
            windows = jnp.stack([xBC_pad[:, k:k + l, :] for k in range(D_CONV)], axis=-1)
            xBC = jax.nn.silu(jnp.einsum('blck,ck->blc', windows, conv_w) + conv_b)
            xs = xBC[..., :D_INNER]
            B = xBC[..., D_INNER:D_INNER + D_STATE]
            C = xBC[..., D_INNER + D_STATE:]
            xh = xs.reshape(b, l, NHEADS, HEADDIM)
            dt = jax.nn.softplus(dt + dt_bias)
            A = -jnp.exp(A_log)
            dA = jnp.exp(dt * A)
            xdt = xh * dt[..., None]

            def step(S, inp):
                dA_t, xdt_t, B_t, C_t = inp
                S = dA_t[:, :, None, None] * S + xdt_t[..., None] * B_t[:, None, None, :]
                y_t = jnp.einsum('bhpn,bn->bhp', S, C_t)
                return (S, y_t)
            S0 = jnp.zeros((b, NHEADS, HEADDIM, D_STATE), x.dtype)
            _, y = lax.scan(step, S0, (dA.transpose(1, 0, 2), xdt.transpose(1, 0, 2, 3), B.transpose(1, 0, 2), C.transpose(1, 0, 2)))
            y = y.transpose(1, 0, 2, 3) + D[None, None, :, None] * xh
            y = y.reshape(b, l, D_INNER)
            y = y * jax.nn.silu(z)
            y = y * lax.rsqrt(jnp.mean(y * y, axis=-1, keepdims=True) + 1e-05) * norm_w
            return y @ out_proj_w.T
        return x + _mamba2(x, in_proj_w, conv_w, conv_b, dt_bias, A_log, D, norm_w, out_proj_w)

    def _L1_ffn_ref(x, gate_w, gate_b, expert_w, expert_b):
        import jax, jax.numpy as jnp
        import numpy as np
        NEG_INF = -1e+30
        K = 2
        pooled = x.mean(axis=1)
        logits = pooled @ gate_w.T + gate_b
        topk_vals, _ = jax.lax.top_k(logits, K)
        min_topk = topk_vals[:, -1:]
        masked = jnp.where(logits < min_topk, -jnp.inf, logits)
        gates = jax.nn.softmax(masked, axis=-1)
        expert_out = jax.nn.gelu(jnp.einsum('bsd,eod->beso', x, expert_w) + expert_b[None, :, None, :], approximate=False)
        return jnp.einsum('be,beso->bso', gates, expert_out)
    x = L0_attn_x
    xn = _layernorm(x, axis=-1)
    s = _L0_attn_ref(xn, L0_attn_Wq, L0_attn_bq, L0_attn_Wl, L0_attn_bl, L0_attn_Wk, L0_attn_bk, L0_attn_Wv, L0_attn_bv, L0_attn_Wo, L0_attn_bo)
    g = _silu(_L0_ffn_ref(xn, L0_ffn_wqkv, L0_ffn_q_scale, L0_ffn_k_scale, L0_ffn_wo, L0_ffn_ln_g, L0_ffn_ln_b, L0_ffn_w1, L0_ffn_b1, L0_ffn_w2, L0_ffn_b2))
    x = x + s * g
    xn = _layernorm(x, axis=-1)
    s = _L1_attn_ref(xn, L1_attn_in_proj_w, L1_attn_conv_w, L1_attn_conv_b, L1_attn_dt_bias, L1_attn_A_log, L1_attn_D, L1_attn_norm_w, L1_attn_out_proj_w)
    g = _silu(_L1_ffn_ref(xn, L1_ffn_gate_w, L1_ffn_gate_b, L1_ffn_expert_w, L1_ffn_expert_b))
    x = x + s * g
    return x

_drawn_inputs = setup_inputs


def setup_inputs(seed=0):
    import zlib

    import numpy as np

    out = dict(_drawn_inputs(seed))
    spreads = {'L0_attn_bq': (0.0, 0.1),
     'L0_attn_bl': (0.0, 0.1),
     'L0_attn_bk': (0.0, 2.0),
     'L0_attn_bv': (0.0, 0.1),
     'L0_attn_bo': (0.0, 0.1),
     'L0_ffn_q_scale': (1.0, 0.6),
     'L0_ffn_k_scale': (1.0, 0.6),
     'L0_ffn_ln_g': (1.0, 0.6),
     'L0_ffn_ln_b': (0.0, 0.8),
     'L0_ffn_b1': (0.0, 0.8),
     'L0_ffn_b2': (0.0, 0.8),
     'L1_attn_norm_w': (1.0, 0.6),
     'L1_ffn_gate_b': (0.0, 0.8),
     'L1_ffn_expert_b': (0.0, 2.0)}
    factors = {'L0_ffn_wqkv': 8.0,
     'L0_ffn_wo': 8.0,
     'L0_ffn_w1': 8.0,
     'L0_ffn_w2': 8.0,
     'L1_attn_conv_b': 28.208,
     'L1_attn_dt_bias': 8.0,
     'L1_attn_A_log': 8.0,
     'L1_attn_in_proj_w': 5.965,
     'L1_attn_conv_w': 7.176,
     'L1_attn_D': 5.196,
     'L1_attn_out_proj_w': 6.074,
     'L1_ffn_gate_w': 2.738}
    for name, (base, spread) in spreads.items():
        noise = np.random.default_rng([zlib.crc32(name.encode()), seed]).standard_normal(out[name].shape)
        drawn = base * np.exp(spread * noise) if base else spread * noise
        out[name] = jnp.asarray(drawn.astype(out[name].dtype))
    for name, factor in factors.items():
        out[name] = (out[name] * factor).astype(out[name].dtype)
    return out
```

```python
import concourse.bass as bass
from concourse import mybir
from contextlib import ExitStack

F32 = mybir.dt.float32
BF16 = mybir.dt.bfloat16
ALU = mybir.AluOpType
ACT = mybir.ActivationFunctionType
AXX = mybir.AxisListType.X

D = 128
SEQ = 256
NB = 2
TOK = NB * SEQ
NT = TOK // 128
BATCH = 16
NG = BATCH // NB
AH, ADH, LATENT = 16, 8, 32
AP = AH // 2
NPART = 3
Q_PART = [0, 0, 0, 1, 1, 2]
K_PART = [0, 1, 2, 0, 1, 0]
QROWS = ADH * len(Q_PART)
MROWS = QROWS + NPART
DEPTH, FH, FDH, WIN = 2, 8, 64, 64
INNER = FH * FDH
FP = INNER // 128
HID = D * 4 * 2 // 3
HC = 3
HCW = -(-HID // HC)
HCN = [min(HCW, HID - c * HCW) for c in range(HC)]
SW = 128 + 192
DI, NS, MH, MDH, TAPS = 256, 128, 4, 64, 4
XBC = (DI + 2 * NS) // 128
NE = 8

NORM_SHIFT = 2.0 ** 20
LN_SHIFT = 20 * 0.6931471805599453
LN_8 = 3 * 0.6931471805599453


def layout():
    parts = [
        [("ident", 128), ("mean", 128), ("wq", 128), ("wl", 32), ("wk", 128), ("wv", 128), ("wo", 128),
         ("bq", 1), ("bl", 1), ("bk", 1), ("bo", 1),
         ("block", 128), ("heads2", 2), ("band", SW), ("step", SEQ), ("sel", MH * 128),
         ("qs", 2), ("qsr", 2), ("ks", 2), ("ksr", 2)],
    ]
    for l in range(DEPTH):
        parts.append([(f"{n}{l}", w) for n, w in [
            ("fq", INNER), ("fqr", INNER), ("fk", INNER), ("fkr", INNER), ("fv", INNER), ("fo", FP * D),
            ("w1", 2 * HID), ("w2", HC * D), ("lg", 1), ("lb", 1), ("b1", 2 * HC), ("b2", 1)]])
    parts.append([("inp", 2 * DI + 2 * NS + MH), ("cw", XBC * TAPS), ("cb", XBC), ("dtb", MH), ("alog", MH),
                  ("dsk", 2), ("nw", 2), ("outp", 2 * D), ("gw", NE), ("gb", NE), ("ew", NE * D), ("eb", NE)])
    at, spans, place = 0, [], {}
    for part in parts:
        first = at
        for name, width in part:
            place[name] = (at, width)
            at += width
        spans.append((first, at))
    return place, spans, at


SERIES = [1.0 / n for n in (15, 13, 11, 9, 7, 5, 3)]

PER = {
    "x_loaded": 16, "x_rows_free": 1, "out_stored": 16,
    "xT": 1, "out_rows": 1,
    "ln_centered": 4, "ln_squared": 4, "ln_log": 4, "ln_rstd": 4, "ln_done": 4,
    "a_q32": 2, "a_part0": 2, "a_rest1": 2, "a_part1": 2, "a_part2": 2,
    "q_spread": 16 * 12, "k_spread": 16 * 12, "m_spread": 16 * 6,
    "latent": 1, "a_v": 1,
    "neg_max": 2 * AH, "m_part0": 1, "m_rest1": 1, "m_part1": 1, "m_part2": 1, "m_rows": 1,
    "a_exp": 2 * AH, "a_pv": 2 * AH, "a_rsum": NB, "a_norm": NB, "a_oT": 1, "attn_out": 1,
    "shifted": 2 * DEPTH,
    "q_squared": DEPTH * FP, "k_squared": DEPTH * FP, "q_cos": DEPTH * FP, "q_sin": DEPTH * FP,
    "k_cos": DEPTH * FP, "k_sin": DEPTH * FP, "q_rot": DEPTH * FP, "k_rot": DEPTH * FP,
    "k_norm2": DEPTH * FP, "k_nlog": DEPTH * FP, "k_rnorm": DEPTH * FP, "k_final": DEPTH * FP,
    "q_norm2": DEPTH, "q_nlog": DEPTH, "q_rnorm": DEPTH, "f_v": DEPTH * (NT + NB),
    "f_masked": DEPTH * NB * FH, "f_negmax": DEPTH * NB * FH, "f_exp": DEPTH * NB * FH,
    "f_rsum": DEPTH * NB * FH, "f_probs": DEPTH * NB * FH, "f_probsT": DEPTH * NB * FH,
    "f_oT": DEPTH * NB * FP, "f_res1": DEPTH, "f_affine": DEPTH,
    "f_gelu": DEPTH * HC, "f_hidden": DEPTH * HC, "f_res2": DEPTH,
    "silu": 2, "gated": 2, "x_new": 2,
    "conv_in": XBC, "conv": XBC * TAPS, "conv_silu": XBC, "z_silu": 2,
    "dt_raw": 1, "dt_abs": 1, "dt_exp": 1, "dt_step": 5 + len(SERIES), "dt": 1, "dt_a": 1, "dA": 1, "dA_rows": 1,
    "xdt": NT,
    "cb_prod": NB, "decay": NB * MH, "weights": NB * MH, "weights_used": NB * MH,
    "y_skip": NB, "y_gated": NB, "y_squared": 1, "y_log": 1, "y_rstd": 1, "mamba_out": 2,
    "pooled": 1, "pool_rows": NB, "logits": 1, "top": NB, "g_keep": NB, "g_negmax": NB, "g_exp": NB, "g_sum": NB, "g_rsum": NB,
    "gates": NB, "expert": NE, "mixed": NE,
    "pe_trip": 1, "act_trip": 1, "dve_trip": 1, "pool_trip": 1, "sp_trip": 1,
}
NBANK = 3
WORK_TILES = 200


def build(nc, x, w, tables, out):
    place, spans, width = layout()
    ctx = ExitStack()
    with ctx:
        def sb(name, shape, dt=F32):
            return ctx.enter_context(nc.sbuf_tensor(name, shape, dt))

        def sem(name):
            return ctx.enter_context(nc.semaphore(name))

        W = sb("W", [128, width])

        def wt(name, rows=128):
            a, n = place[name]
            return W[0:rows, a:a + n]

        def col(name, j=0, rows=128):
            a, _ = place[name]
            return W[0:rows, a + j:a + j + 1]

        ident = wt("ident")
        cols = sb("cols", [128, 4])
        EPS, HALF_SHIFT, HALF_SHIFT8, ONE = (cols[:, j:j + 1] for j in range(4))
        rope = sb("rope", [128, DEPTH, 4, SEQ])
        outp = wt("outp").rearrange("p (j d) -> p j d", j=2)
        neg_a = wt("alog")

        x_rows = sb("x_rows", [128, NT, D])
        xT = sb("xT_", [128, TOK])
        cen = sb("cen", [128, TOK])
        sqr = sb("sqr", [128, TOK])
        rst = sqr
        xn = sb("xn", [128, TOK])
        f32op = sb("f32op", [128, 2, TOK])
        rest = sb("rest", [128, 2, TOK])
        parts = sb("parts", [128, 2, NPART, TOK], BF16)
        QR = sb("QR", [128, FP, TOK])
        QS = QR[:, :, :].rearrange("p a t -> p (a t)").bitcast(BF16).rearrange("p (a t) -> p a t", a=AP)
        KS = sb("KS", [128, AP, TOK], BF16)
        lat = sb("lat", [LATENT + 1, TOK])
        VA = sb("VA", [128, NT, AH, ADH + 1])
        nmax = sb("nmax", [128, NT, AH])
        kn = sb("kn", [128, 2, TOK])
        mx, mrest = kn[0:AH, 0, :], kn[0:AH, 1, :]
        mparts = sb("mparts", [AH, NPART, TOK], BF16)
        NPT = 3
        ge = sb("ge", [128, HC, TOK])
        PT = ge[:, :, :].rearrange("p n (c q) -> p n c q", c=2)
        arsum = sb("arsum", [128, NB, 2, AH])
        sqk = sb("sqk", [128, 2, TOK])
        AN = sqk[:, 0, :].rearrange("p (t h d) -> p t h d", t=NT, h=AH)
        aoT = sqk[:, 1, :]
        s_out = sb("s_out", [128, TOK])

        hT = sb("hT", [128, NB, SEQ])
        KR = sb("KR", [128, FP, TOK])
        sqq = sb("sqq", [128, FP, TOK])
        cosp, sinp = f32op, rest
        qn = sb("qn", [128, NT, FH])
        V = sb("V", [128, NT, INNER])
        VH = sb("VH", [64, NB, INNER])
        MS = sb("MS", [128, NB * FH, SW])
        fmx = sb("fmx", [128, NB * FH, 2])
        fnm = sb("fnm", [128, NB * FH, 2])
        fsum = sb("fsum", [128, NB * FH, 2])
        frs = sb("frs", [128, NB * FH, 2])
        NPP = 4
        PP = parts[:, :, :, :].rearrange("p i r t -> p (i r t)").bitcast(F32).rearrange("p (n s) -> p n s", n=NPP)
        OT = sqq
        yT = sb("yT", [128, TOK])
        hn = cen
        hid = ge

        x1T = sb("x1T", [128, TOK])
        cin = sb("cin", [128, XBC, NB, SEQ + TAPS - 1])
        ms = MS[:, :, :].rearrange("p n s -> p (n s)")
        cv = QR[:, :, :].rearrange("p j (b t) -> p j b t", b=NB)
        cs = cv[:, :, :, :].rearrange("p j b t -> p j (b t)")
        zs = V[:, 0:2, :]
        dt7 = sb("dt7", [128, 8, NT, MH])
        dt_raw, dt_e, dt_w, dt_w2, dt_p, dt_pos, dt_, dt_dA = (dt7[:, k, :, :] for k in range(8))
        dA_rows = KR[0:MH, 0, :]
        xd = V[:, 2:4, :].rearrange("p a (b h d) -> p (a b) h d", b=2, h=MH)
        cbp, dec, wgt = (ms[:, a * 768:a * 768 + 768].rearrange("p (b t) -> p b t", b=2) for a in range(3))
        ym = ms[:, 2304:2304 + 1024].rearrange("p (j b t) -> p j b t", j=2, b=NB)
        ysq = zs
        pool = sb("pool", [128, NB])
        poolb = sb("poolb", [128, NB, 128])
        lg_ = sb("lg_", [128, NB, NE])
        top = sb("top", [128, NB, 8])
        gsm = sb("gsm", [128, NB, 4])
        gex = sb("gex", [128, NB, NE])
        gkp = sb("gkp", [128, NB, NE])
        gt = sb("gt", [128, NB, NE])
        eg = ms[:, 3328:3328 + 1024].rearrange("p (a t) -> p a t", a=2)
        gate = sb("gate", [128, TOK])
        mix = gate[:, :].rearrange("p (b t) -> p b t", b=NB)
        out_rows = x_rows

        banks = [ctx.enter_context(nc.psum_tensor(f"bank{i}", [128, 512], F32)) for i in range(8)]
        MAXB, EXPB, PVB, WORK = banks[0:2], banks[2:4], banks[4], banks[5:8]

        rope0 = ms[:, 0:4 * SEQ].rearrange("p (k t) -> p k t", k=4)

        S = {name: sem(name) for name in PER}
        weights_in = [sem(f"weights_in{i}") for i in range(len(spans))]
        tables_in = sem("tables_in")
        setup = sem("setup")
        consts = sem("consts")
        spacer = sem("spacer")
        work_filled = [sem(f"work_filled{b}") for b in range(NBANK)]
        work_read = [sem(f"work_read{b}") for b in range(NBANK)]
        max_filled = sem("max_filled")
        max_read = sem("max_read")
        exp_filled = sem("exp_filled")
        pv_filled = sem("pv_filled")
        work_uses = [len(range(b, WORK_TILES, NBANK)) for b in range(NBANK)]
        work_place = {}

        def upto(g, name, k):
            return g * PER[name] + k

        def bank_free(g, name):
            n = len(work_place)
            work_place[name] = n
            return work_read[n % NBANK], g * work_uses[n % NBANK] + n // NBANK + 1

        def bank_to_fill(name):
            n = work_place[name]
            return WORK[n % NBANK], work_filled[n % NBANK]

        def bank_filled(g, name):
            n = work_place[name]
            return work_filled[n % NBANK], g * work_uses[n % NBANK] + n // NBANK + 1

        def bank_to_read(name):
            n = work_place[name]
            return WORK[n % NBANK], work_read[n % NBANK]

        block = ctx.enter_context(nc.Block())

        def units():
            return [(bb, h) for bb in range(NB) for h in range(AH)]

        def fills(l):
            return [(bb, h) for bb in range(NB) for h in range(FH)]

        @block.tensor
        def _(pe):
            for i in range(len(spans)):
                pe.wait_ge(weights_in[i], 16)
            pe.wait_ge(consts, CONSTS)
            pe.wait_ge(setup, SETUP)
            pe.sem_inc(S["pe_trip"], 1)
            mm = pe.matmul

            def layer_norm(g, n, src):
                pe.wait_ge(*bank_free(g, ("mean", n)))
                t, full = bank_to_fill(("mean", n))
                mm(t[:, :], wt("mean"), src, start=True, stop=True).then_inc(full, 1)
                pe.wait_ge(S["ln_squared"], upto(g, "ln_squared", n + 1))
                pe.wait_ge(*bank_free(g, ("var", n)))
                t, full = bank_to_fill(("var", n))
                mm(t[:, :], wt("mean"), sqr[:, :], start=True, stop=True).then_inc(full, 1)

            with pe.Fori(0, NG) as g:
                pe.wait_ge(S["act_trip"], g + 1)
                pe.wait_ge(S["dve_trip"], g + 1)
                pe.wait_ge(S["pool_trip"], g + 1)
                pe.wait_ge(S["sp_trip"], g + 1)
                pe.wait_ge(S["x_loaded"], upto(g, "x_loaded", 16))
                pe.wait_ge(*bank_free(g, "xT"))
                t, full = bank_to_fill("xT")
                for j in range(NT):
                    m = pe.transpose(t[:, j * 128:j * 128 + 128], x_rows[:, j, :], ident)
                m.then_inc(full, 1)
                pe.wait_ge(S["xT"], upto(g, "xT", 1))
                layer_norm(g, 0, xT[:, :])

                pe.wait_ge(S["ln_done"], upto(g, "ln_done", 1))
                pe.wait_ge(*bank_free(g, "a_lat"))
                t, full = bank_to_fill("a_lat")
                mm(t[0:LATENT, :], wt("wl"), xn[:, :], start=True, stop=True).then_inc(full, 1)
                pe.wait_ge(*bank_free(g, ("a_proj", 0)))
                t, full = bank_to_fill(("a_proj", 0))
                mm(t[:, :], wt("wq"), xn[:, :], start=True, stop=True).then_inc(full, 1)
                pe.wait_ge(S["latent"], upto(g, "latent", 1))
                pe.wait_ge(*bank_free(g, ("a_proj", 1)))
                t, full = bank_to_fill(("a_proj", 1))
                mm(t[:, :], wt("wk", LATENT), lat[0:LATENT, :], start=True, stop=True).then_inc(full, 1)
                pe.wait_ge(*bank_free(g, "a_v"))
                t, full = bank_to_fill("a_v")
                for j in range(NT):
                    m = mm(t[:, j * 128:j * 128 + 128], lat[:, j * 128:j * 128 + 128], wt("wv", LATENT + 1),
                           start=True, stop=True)
                m.then_inc(full, 1)

                pe.wait_ge(S["q_spread"], upto(g, "q_spread", PER["q_spread"]))
                pe.wait_ge(S["k_spread"], upto(g, "k_spread", PER["k_spread"]))
                for n, (bb, h) in enumerate(units()):
                    p, lo = h // 2, 64 * (h % 2)
                    pe.wait_ge(max_read, g * 2 * AH + n + 1)
                    for qt in range(2):
                        q0 = bb * SEQ + qt * 128
                        m = mm(MAXB[n % 2][:, qt * SEQ:qt * SEQ + SEQ], QS[lo:lo + QROWS, p, q0:q0 + 128],
                               KS[lo:lo + QROWS, p, bb * SEQ:bb * SEQ + SEQ], start=True, stop=True)
                    m.then_inc(max_filled, 1)
                pe.wait_ge(S["neg_max"], upto(g, "neg_max", PER["neg_max"]))
                pe.wait_ge(*bank_free(g, "maxT"))
                t, full = bank_to_fill("maxT")
                for j in range(NT):
                    m = pe.transpose(t[0:AH, j * 128:j * 128 + 128], nmax[:, j, :], ident)
                m.then_inc(full, 1)

                pe.wait_ge(S["m_spread"], upto(g, "m_spread", PER["m_spread"]))
                pe.wait_ge(S["a_v"], upto(g, "a_v", 1))

                def shifted_scores(n, bb, h):
                    p, lo = h // 2, 64 * (h % 2)
                    if n >= 2:
                        pe.wait_ge(S["a_exp"], upto(g, "a_exp", n - 1))
                    for c in range(2):
                        k0 = bb * SEQ + c * 128
                        m = mm(EXPB[n % 2][:, c * SEQ:c * SEQ + SEQ], KS[lo:lo + MROWS, p, k0:k0 + 128],
                               QS[lo:lo + MROWS, p, bb * SEQ:bb * SEQ + SEQ], start=True, stop=True)
                    m.then_inc(exp_filled, 1)

                def probs_v(n, bb, h):
                    if h == 0 and bb > 0:
                        pe.wait_ge(S["a_norm"], upto(g, "a_norm", bb))
                    pe.wait_ge(S["a_exp"], upto(g, "a_exp", n + 1))
                    o = PVB[:, 0:2 * AH * (ADH + 1)].rearrange("p (a h d) -> p a h d", a=2, h=AH)
                    for qt in range(2):
                        for c in range(2):
                            m = mm(o[:, qt, h, :], PT[:, n % NPT, c, qt * 128:qt * 128 + 128],
                                   VA[:, 2 * bb + c, h, :], start=(c == 0), stop=(c == 1))
                    m.then_inc(S["a_pv"], 1)
                    if h == AH - 1:
                        pe.sem_inc(pv_filled, 1)

                us = units()
                for n in range(len(us) + 1):
                    if n < len(us):
                        shifted_scores(n, *us[n])
                    if n > 0:
                        probs_v(n - 1, *us[n - 1])
                pe.wait_ge(S["a_norm"], upto(g, "a_norm", NB))
                pe.wait_ge(*bank_free(g, "a_oT"))
                t, full = bank_to_fill("a_oT")
                for j in range(NT):
                    m = pe.transpose(t[:, j * 128:j * 128 + 128], AN[:, j, :, :].rearrange("p h d -> p (h d)"), ident)
                m.then_inc(full, 1)
                pe.wait_ge(S["a_oT"], upto(g, "a_oT", 1))
                pe.wait_ge(*bank_free(g, "a_out"))
                t, full = bank_to_fill("a_out")
                mm(t[:, :], wt("wo"), aoT[:, :], start=True, stop=True).then_inc(full, 1)

                for l in range(DEPTH):
                    pe.wait_ge(S["shifted"], upto(g, "shifted", 2 * l + 1))
                    h2 = hT[:, :, :].rearrange("p b t -> p (b t)")
                    for p in range(FP):
                        for name in ("fq", "fqr", "fk", "fkr"):
                            pe.wait_ge(*bank_free(g, (name, l, p)))
                            t, full = bank_to_fill((name, l, p))
                            mm(t[:, :], wt(f"{name}{l}")[:, p * 128:p * 128 + 128], h2,
                               start=True, stop=True).then_inc(full, 1)
                        pe.wait_ge(S["k_squared"], upto(g, "k_squared", l * FP + p + 1))
                        pe.wait_ge(*bank_free(g, ("k_norm", l, p)))
                        t, full = bank_to_fill(("k_norm", l, p))
                        mm(t[:, :], wt("block"), sqk[:, p % 2, :], start=True, stop=True).then_inc(full, 1)
                    pe.wait_ge(S["q_squared"], upto(g, "q_squared", (l + 1) * FP))
                    pe.wait_ge(*bank_free(g, ("q_norm", l)))
                    t, full = bank_to_fill(("q_norm", l))
                    for j in range(NT):
                        for p in range(FP):
                            m = mm(t[:, j * FH + 2 * p:j * FH + 2 * p + 2], sqq[:, p, j * 128:j * 128 + 128],
                                   wt("heads2"), start=True, stop=True)
                    m.then_inc(full, 1)
                    for j in range(NT):
                        pe.wait_ge(*bank_free(g, ("f_v", l, j)))
                        t, full = bank_to_fill(("f_v", l, j))
                        mm(t[:, :], h2[:, j * 128:j * 128 + 128], wt(f"fv{l}"), start=True,
                           stop=True).then_inc(full, 1)
                    for bb in range(NB):
                        k0 = bb * SEQ + WIN
                        pe.wait_ge(*bank_free(g, ("f_vh", l, bb)))
                        t, full = bank_to_fill(("f_vh", l, bb))
                        mm(t[0:64, :], h2[:, k0:k0 + WIN], wt(f"fv{l}"), start=True,
                           stop=True).then_inc(full, 1)
                    for n, (bb, h) in enumerate(fills(l)):
                        p, lo = h // 2, 64 * (h % 2)
                        q0 = bb * SEQ
                        if n < FH:
                            pe.wait_ge(S["q_rot"], upto(g, "q_rot", l * FP + p + 1))
                            pe.wait_ge(S["k_final"], upto(g, "k_final", l * FP + p + 1))
                        pe.wait_ge(*bank_free(g, ("f_s", l, n)))
                        t, full = bank_to_fill(("f_s", l, n))
                        mm(t[:, 0:128], QR[lo:lo + 64, p, q0:q0 + 128], KR[lo:lo + 64, p, q0:q0 + 128],
                           start=True, stop=True)
                        mm(t[:, 128:SW], QR[lo:lo + 64, p, q0 + 128:q0 + 256],
                           KR[lo:lo + 64, p, q0 + 64:q0 + 256], start=True, stop=True).then_inc(full, 1)
                    pe.wait_ge(S["f_v"], upto(g, "f_v", (l + 1) * (NT + NB)))

                    def transposes(n):
                        pe.wait_ge(S["f_probs"], upto(g, "f_probs", l * NB * FH + n + 1))
                        pe.wait_ge(*bank_free(g, ("f_pT", l, n)))
                        t, full = bank_to_fill(("f_pT", l, n))
                        pe.transpose(t[:, 0:128], MS[:, n, 0:128], ident)
                        pe.transpose(t[0:64, 128:256], MS[:, n, 128:192], ident)
                        pe.transpose(t[:, 256:384], MS[:, n, 192:320], ident).then_inc(full, 1)

                    def pv_pair(n):
                        bb, p = n // FH, (n % FH) // 2
                        pe.wait_ge(*bank_free(g, ("f_o", l, n // 2)))
                        t, full = bank_to_fill(("f_o", l, n // 2))
                        for i in range(2):
                            pe.wait_ge(S["f_probsT"], upto(g, "f_probsT", l * NB * FH + n + i + 1))
                            P, h = PP[:, (n + i) % NPP, :], 2 * p + i
                            hc = slice(h * FDH, h * FDH + FDH)
                            o = t[64 * i:64 * i + 64, :]
                            mm(o[:, 0:128], V[:, 2 * bb, hc], P[:, 0:128], start=True, stop=True)
                            mm(o[:, 128:256], VH[:, bb, hc], P[0:64, 128:256], start=True, stop=False)
                            m = mm(o[:, 128:256], V[:, 2 * bb + 1, hc], P[:, 256:384], start=False, stop=True)
                        m.then_inc(full, 1)

                    for n in range(0, NB * FH + 2, 2):
                        if n < NB * FH:
                            transposes(n)
                            transposes(n + 1)
                        if n >= 2:
                            pv_pair(n - 2)
                    pe.wait_ge(S["f_oT"], upto(g, "f_oT", (l + 1) * NB * FP))
                    pe.wait_ge(*bank_free(g, ("f_wo", l)))
                    t, full = bank_to_fill(("f_wo", l))
                    for p in range(FP):
                        m = mm(t[:, :], wt(f"fo{l}")[:, p * D:p * D + D], OT[:, p, :], start=(p == 0),
                               stop=(p == FP - 1))
                    m.then_inc(full, 1)
                    pe.wait_ge(S["shifted"], upto(g, "shifted", 2 * l + 2))
                    layer_norm(g, 1 + l, h2)
                    pe.wait_ge(S["f_affine"], upto(g, "f_affine", l + 1))
                    for c in range(HC):
                        for part in (1, 0):
                            pe.wait_ge(*bank_free(g, ("w1", l, c, part)))
                            t, full = bank_to_fill(("w1", l, c, part))
                            a = part * HID + c * HCW
                            mm(t[0:HCN[c], :], wt(f"w1{l}")[:, a:a + HCN[c]], hn[:, :], start=True,
                               stop=True).then_inc(full, 1)
                    pe.wait_ge(*bank_free(g, ("w2", l)))
                    t, full = bank_to_fill(("w2", l))
                    for c in range(HC):
                        pe.wait_ge(S["f_hidden"], upto(g, "f_hidden", l * HC + c + 1))
                        m = mm(t[:, :], wt(f"w2{l}", HCN[c])[:, c * D:c * D + D], hid[0:HCN[c], c, :],
                               start=(c == 0), stop=(c == HC - 1))
                    m.then_inc(full, 1)

                pe.wait_ge(S["x_new"], upto(g, "x_new", 1))
                layer_norm(g, 3, x1T[:, :])
                pe.wait_ge(S["ln_done"], upto(g, "ln_done", 4))
                inp = wt("inp")
                pe.wait_ge(*bank_free(g, "m_dt"))
                t, full = bank_to_fill("m_dt")
                for j in range(NT):
                    m = mm(t[:, j * MH:j * MH + MH], xn[:, j * 128:j * 128 + 128], inp[:, 2 * DI + 2 * NS:],
                           start=True, stop=True)
                m.then_inc(full, 1)
                for j in range(XBC):
                    pe.wait_ge(*bank_free(g, ("m_xbc", j)))
                    t, full = bank_to_fill(("m_xbc", j))
                    mm(t[:, :], inp[:, DI + j * 128:DI + j * 128 + 128], xn[:, :], start=True,
                       stop=True).then_inc(full, 1)
                for j in range(2):
                    pe.wait_ge(*bank_free(g, ("m_z", j)))
                    t, full = bank_to_fill(("m_z", j))
                    mm(t[:, :], inp[:, j * 128:j * 128 + 128], xn[:, :], start=True, stop=True).then_inc(full, 1)
                pe.wait_ge(S["pool_rows"], upto(g, "pool_rows", NB))
                pe.wait_ge(*bank_free(g, "logits"))
                t, full = bank_to_fill("logits")
                for bb in range(NB):
                    m = mm(t[:, bb * NE:bb * NE + NE], poolb[:, bb, :], wt("gw"), start=True, stop=True)
                m.then_inc(full, 1)
                pe.wait_ge(S["dA"], upto(g, "dA", 1))
                pe.wait_ge(*bank_free(g, "dAT"))
                t, full = bank_to_fill("dAT")
                pe.sem_inc(spacer, 1)
                for j in range(NT):
                    m = pe.transpose(t[0:MH, j * 128:j * 128 + 128], dt_dA[:, j, :], ident)
                m.then_inc(full, 1)
                pe.wait_ge(S["conv_silu"], upto(g, "conv_silu", 2))
                for j in range(NT):
                    pe.wait_ge(*bank_free(g, ("m_xt", j)))
                    t, full = bank_to_fill(("m_xt", j))
                    for c in range(2):
                        m = pe.transpose(t[:, c * 128:c * 128 + 128], cs[:, c, j * 128:j * 128 + 128], ident)
                    m.then_inc(full, 1)
                pe.wait_ge(S["conv_silu"], upto(g, "conv_silu", 4))
                for bb in range(NB):
                    t0 = bb * SEQ
                    pe.wait_ge(*bank_free(g, ("m_cb", bb)))
                    t, full = bank_to_fill(("m_cb", bb))
                    mm(t[:, 0:256], cs[:, 2, t0:t0 + 128], cs[:, 3, t0:t0 + 256], start=True, stop=True)
                    mm(t[:, 256:384], cs[:, 2, t0 + 128:t0 + 256], cs[:, 3, t0 + 128:t0 + 256], start=True,
                       stop=True).then_inc(full, 1)
                pe.wait_ge(S["dA_rows"], upto(g, "dA_rows", 1))
                pe.wait_ge(S["xdt"], upto(g, "xdt", NT))
                for bb in range(NB):
                    for h in range(MH):
                        pe.wait_ge(*bank_free(g, ("m_dA", bb, h)))
                        t, full = bank_to_fill(("m_dA", bb, h))
                        mm(t[:, 0:SEQ], wt("sel", MH)[:, h * 128:h * 128 + 128],
                           dA_rows[:, bb * SEQ:bb * SEQ + SEQ], start=True, stop=True).then_inc(full, 1)
                        if h == 0 and bb > 0:
                            pe.wait_ge(S["y_skip"], upto(g, "y_skip", bb))
                        n = bb * MH + h
                        pe.wait_ge(S["weights"], upto(g, "weights", n + 1))
                        lo, j = 64 * (h % 2), h // 2
                        o = PVB[lo:lo + 64, j * SEQ:j * SEQ + SEQ]
                        mm(o, xd[:, 2 * bb, h, :], wgt[:, n % 2, 0:256], start=True, stop=False)
                        m = mm(o[:, 128:256], xd[:, 2 * bb + 1, h, :], wgt[:, n % 2, 256:384], start=False,
                               stop=True)
                        m.then_inc(S["weights_used"], 1)
                pe.wait_ge(S["y_squared"], upto(g, "y_squared", 1))
                pe.wait_ge(*bank_free(g, "m_ss"))
                t, full = bank_to_fill("m_ss")
                for j in range(2):
                    m = mm(t[:, :], wt("mean"), ysq[:, j, :], start=(j == 0), stop=(j == 1))
                m.then_inc(full, 1)
                pe.wait_ge(*bank_free(g, "m_out"))
                t, full = bank_to_fill("m_out")
                for j in range(2):
                    m = mm(t[:, :], outp[:, j, :], ym[:, j, :, :].rearrange("p b t -> p (b t)"),
                           start=(j == 0), stop=(j == 1))
                m.then_inc(full, 1)
                for e in range(NE):
                    pe.wait_ge(*bank_free(g, ("expert", e)))
                    t, full = bank_to_fill(("expert", e))
                    mm(t[:, :], wt("ew")[:, e * D:e * D + D], xn[:, :], start=True, stop=True).then_inc(full, 1)
                pe.wait_ge(S["x_new"], upto(g, "x_new", 2))
                pe.wait_ge(*bank_free(g, "outT"))
                t, full = bank_to_fill("outT")
                for j in range(NT):
                    m = pe.transpose(t[:, j * 128:j * 128 + 128], xT[:, j * 128:j * 128 + 128], ident)
                m.then_inc(full, 1)
                pe.sem_inc(S["pe_trip"], 1)
            assert len(work_place) == WORK_TILES, len(work_place)

        @block.scalar
        def _(act):
            act.wait_ge(consts, CONSTS)
            act.wait_ge(weights_in[len(spans) - 1], 16)
            act.preload_act_table_set("natural_log_exp_and_others")
            A = act.activation
            A(neg_a, neg_a, ACT.Exp).then_inc(setup, 1)
            act.sem_inc(S["act_trip"], 1)

            def layer_norm(g, n):
                act.wait_ge(S["ln_centered"], upto(g, "ln_centered", n + 1))
                A(sqr[:, :], cen[:, :], ACT.Square).then_inc(S["ln_squared"], 1)
                act.wait_ge(*bank_filled(g, ("var", n)))
                t, free = bank_to_read(("var", n))
                A(rst[:, :], t[:, :], ACT.Ln, bias=EPS).then_inc(S["ln_log"], 1)
                act.wait_ge(S["ln_log"], upto(g, "ln_log", n + 1))
                A(rst[:, :], rst[:, :], ACT.Exp, scale=-0.5).then_inc(S["ln_rstd"], 1)
                act.sem_inc(free, 1)

            with act.Fori(0, NG) as g:
                act.preload_act_table_set("natural_log_exp_and_others")
                act.wait_ge(S["pe_trip"], g + 1)
                act.wait_ge(S["dve_trip"], g + 1)
                act.wait_ge(S["pool_trip"], g + 1)
                act.wait_ge(S["sp_trip"], g + 1)
                act.wait_ge(*bank_filled(g, "xT"))
                t, free = bank_to_read("xT")
                A(xT[:, :], t[:, :], ACT.Identity).then_inc(S["xT"], 1)
                act.wait_ge(S["xT"], upto(g, "xT", 1))
                act.sem_inc(free, 1)
                layer_norm(g, 0)
                act.wait_ge(*bank_filled(g, "a_lat"))
                t, free = bank_to_read("a_lat")
                A(lat[0:LATENT, :], t[0:LATENT, :], ACT.Identity, bias=col("bl", 0, LATENT)).then_inc(S["latent"], 1)
                act.wait_ge(S["latent"], upto(g, "latent", 1))
                act.sem_inc(free, 1)
                for i in range(2):
                    act.wait_ge(S["a_q32"], upto(g, "a_q32", i + 1))
                    A(parts[:, i, 0, :], f32op[:, i, :], ACT.Identity).then_inc(S["a_part0"], 1)
                    act.wait_ge(S["a_rest1"], upto(g, "a_rest1", i + 1))
                    A(parts[:, i, 1, :], rest[:, i, :], ACT.Identity).then_inc(S["a_part1"], 1)
                act.wait_ge(*bank_filled(g, "maxT"))
                t, free = bank_to_read("maxT")
                A(mx[:, :], t[0:AH, :], ACT.Identity).then_inc(S["m_rows"], 1)
                act.wait_ge(S["m_rows"], upto(g, "m_rows", 1))
                act.sem_inc(free, 1)
                A(mparts[:, 0, :], mx[:, :], ACT.Identity).then_inc(S["m_part0"], 1)
                act.wait_ge(S["m_rest1"], upto(g, "m_rest1", 1))
                A(mparts[:, 1, :], mrest[:, :], ACT.Identity).then_inc(S["m_part1"], 1)
                for n in range(2 * AH):
                    act.wait_ge(exp_filled, g * 2 * AH + n + 1)
                    if n >= NPT:
                        act.wait_ge(S["a_pv"], upto(g, "a_pv", n - NPT + 1))
                    A(PT[:, n % NPT, :, :].rearrange("p c q -> p (c q)"), EXPB[n % 2][:, :], ACT.Exp,
                      scale=ADH ** -0.5).then_inc(S["a_exp"], 1)
                act.wait_ge(*bank_filled(g, "a_oT"))
                t, free = bank_to_read("a_oT")
                A(aoT[:, :], t[:, :], ACT.Identity).then_inc(S["a_oT"], 1)
                act.wait_ge(S["a_oT"], upto(g, "a_oT", 1))
                act.sem_inc(free, 1)
                act.wait_ge(*bank_filled(g, "a_out"))
                t, free = bank_to_read("a_out")
                A(s_out[:, :], t[:, :], ACT.Identity, bias=col("bo")).then_inc(S["attn_out"], 1)
                act.wait_ge(S["attn_out"], upto(g, "attn_out", 1))
                act.sem_inc(free, 1)

                for l in range(DEPTH):
                    if l > 0:
                        act.preload_act_table_set("natural_log_exp_and_others")
                    for p in range(FP):
                        k = l * FP + p
                        act.wait_ge(*bank_filled(g, ("fq", l, p)))
                        t, free = bank_to_read(("fq", l, p))
                        act.wait_ge(S["q_cos"], upto(g, "q_cos", k + 1))
                        A(sqq[:, p, :], t[:, :], ACT.Square).then_inc(S["q_squared"], 1)
                        act.wait_ge(S["q_squared"], upto(g, "q_squared", k + 1))
                        act.sem_inc(free, 1)
                        act.wait_ge(*bank_filled(g, ("fk", l, p)))
                        t, free = bank_to_read(("fk", l, p))
                        act.wait_ge(S["k_cos"], upto(g, "k_cos", k + 1))
                        A(sqk[:, p % 2, :], t[:, :], ACT.Square).then_inc(S["k_squared"], 1)
                        act.wait_ge(S["k_squared"], upto(g, "k_squared", k + 1))
                        act.sem_inc(free, 1)
                        act.wait_ge(S["k_norm2"], upto(g, "k_norm2", k + 1))
                        A(kn[:, p % 2, :], kn[:, p % 2, :], ACT.Ln, scale=NORM_SHIFT).then_inc(S["k_nlog"], 1)
                        act.wait_ge(S["k_nlog"], upto(g, "k_nlog", k + 1))
                        A(kn[:, p % 2, :], kn[:, p % 2, :], ACT.Exp, scale=-0.5, bias=HALF_SHIFT)\
                            .then_inc(S["k_rnorm"], 1)
                    act.wait_ge(S["q_norm2"], upto(g, "q_norm2", l + 1))
                    q2 = qn[:, :, :].rearrange("p t h -> p (t h)")
                    A(q2, q2, ACT.Ln, scale=NORM_SHIFT).then_inc(S["q_nlog"], 1)
                    act.wait_ge(S["q_nlog"], upto(g, "q_nlog", l + 1))
                    A(q2, q2, ACT.Exp, scale=-0.5, bias=HALF_SHIFT8).then_inc(S["q_rnorm"], 1)
                    for j in range(NT):
                        act.wait_ge(*bank_filled(g, ("f_v", l, j)))
                        t, free = bank_to_read(("f_v", l, j))
                        A(V[:, j, :], t[:, :], ACT.Identity).then_inc(S["f_v"], 1)
                        act.wait_ge(S["f_v"], upto(g, "f_v", l * (NT + NB) + j + 1))
                        act.sem_inc(free, 1)
                    for bb in range(NB):
                        act.wait_ge(*bank_filled(g, ("f_vh", l, bb)))
                        t, free = bank_to_read(("f_vh", l, bb))
                        A(VH[:, bb, :], t[0:64, :], ACT.Identity).then_inc(S["f_v"], 1)
                        act.wait_ge(S["f_v"], upto(g, "f_v", l * (NT + NB) + NT + bb + 1))
                        act.sem_inc(free, 1)

                    def exps(n):
                        k = l * NB * FH + n
                        act.wait_ge(S["f_negmax"], upto(g, "f_negmax", k + 1))
                        A(MS[:, n, 0:128], MS[:, n, 0:128], ACT.Exp, bias=fnm[:, n, 0:1], accum_out=fsum[:, n, 0:1])
                        A(MS[:, n, 128:SW], MS[:, n, 128:SW], ACT.Exp, bias=fnm[:, n, 1:2],
                          accum_out=fsum[:, n, 1:2]).then_inc(S["f_exp"], 1)

                    def copy_pT(n):
                        k = l * NB * FH + n
                        act.wait_ge(*bank_filled(g, ("f_pT", l, n)))
                        t, free = bank_to_read(("f_pT", l, n))
                        P = PP[:, n % NPP, :]
                        A(P[:, 0:128], t[:, 0:128], ACT.Identity)
                        A(P[0:64, 128:256], t[0:64, 128:256], ACT.Identity)
                        A(P[:, 256:384], t[:, 256:384], ACT.Identity).then_inc(S["f_probsT"], 1)
                        act.wait_ge(S["f_probsT"], upto(g, "f_probsT", k + 1))
                        act.sem_inc(free, 1)

                    def copy_o(n):
                        bb, p = n // FP, n % FP
                        act.wait_ge(*bank_filled(g, ("f_o", l, n)))
                        t, free = bank_to_read(("f_o", l, n))
                        A(OT[:, p, bb * SEQ:bb * SEQ + SEQ], t[:, 0:SEQ], ACT.Identity).then_inc(S["f_oT"], 1)
                        act.wait_ge(S["f_oT"], upto(g, "f_oT", l * NB * FP + n + 1))
                        act.sem_inc(free, 1)

                    for n in range(NB * FH):
                        exps(n)
                        if n % 2 and n >= 5:
                            copy_o((n - 5) // 2)
                    for n in range(NB * FP - 2, NB * FP):
                        copy_o(n)
                    layer_norm(g, 1 + l)
                    act.preload_act_table(ACT.Gelu)
                    for c in range(HC):
                        r = HCN[c]
                        act.wait_ge(*bank_filled(g, ("w1", l, c, 1)))
                        t, free = bank_to_read(("w1", l, c, 1))
                        A(ge[0:r, c, :], t[0:r, :], ACT.Gelu, bias=col(f"b1{l}", HC + c, r)).then_inc(S["f_gelu"], 1)
                        act.wait_ge(S["f_gelu"], upto(g, "f_gelu", l * HC + c + 1))
                        act.sem_inc(free, 1)
                act.preload_act_table(ACT.Silu)
                act.wait_ge(S["f_res2"], upto(g, "f_res2", DEPTH))
                A(gate[:, :], yT[:, :], ACT.Silu).then_inc(S["silu"], 1)

                act.preload_act_table_set("natural_log_exp_and_others")
                layer_norm(g, 3)
                act.wait_ge(S["dt_raw"], upto(g, "dt_raw", 1))
                A(dt_e, dt_raw, ACT.Abs).then_inc(S["dt_abs"], 1)
                act.wait_ge(S["dt_abs"], upto(g, "dt_abs", 1))
                A(dt_e, dt_e, ACT.Exp, scale=-1.0).then_inc(S["dt_exp"], 1)
                act.wait_ge(S["dt_a"], upto(g, "dt_a", 1))
                A(dt_dA, dt_dA, ACT.Exp).then_inc(S["dA"], 1)
                for j in range(XBC):
                    act.wait_ge(*bank_filled(g, ("m_xbc", j)))
                    t, free = bank_to_read(("m_xbc", j))
                    A(cin[:, j, :, TAPS - 1:], t[:, :].rearrange("p (b t) -> p b t", b=NB), ACT.Identity)\
                        .then_inc(S["conv_in"], 1)
                    act.wait_ge(S["conv_in"], upto(g, "conv_in", j + 1))
                    act.sem_inc(free, 1)
                act.preload_act_table(ACT.Silu)
                for j in range(2):
                    act.wait_ge(*bank_filled(g, ("m_z", j)))
                    t, free = bank_to_read(("m_z", j))
                    A(zs[:, j, :], t[:, :], ACT.Silu).then_inc(S["z_silu"], 1)
                    act.wait_ge(S["z_silu"], upto(g, "z_silu", j + 1))
                    act.sem_inc(free, 1)
                for j in range(XBC):
                    act.wait_ge(S["conv"], upto(g, "conv", TAPS * (j + 1)))
                    A(cs[:, j, :], cv[:, j, :, :].rearrange("p b t -> p (b t)"), ACT.Silu).then_inc(S["conv_silu"], 1)
                act.preload_act_table_set("natural_log_exp_and_others")
                for bb in range(NB):
                    act.wait_ge(S["g_negmax"], upto(g, "g_negmax", bb + 1))
                    A(gex[:, bb, :], lg_[:, bb, :], ACT.Exp, bias=gsm[:, bb, 0:1]).then_inc(S["g_exp"], 1)
                act.wait_ge(*bank_filled(g, "dAT"))
                t, free = bank_to_read("dAT")
                A(dA_rows, t[0:MH, :], ACT.Identity).then_inc(S["dA_rows"], 1)
                act.wait_ge(S["dA_rows"], upto(g, "dA_rows", 1))
                act.sem_inc(free, 1)
                for bb in range(NB):
                    act.wait_ge(*bank_filled(g, ("m_cb", bb)))
                    t, free = bank_to_read(("m_cb", bb))
                    A(cbp[:, bb, :], t[:, 0:384], ACT.Identity).then_inc(S["cb_prod"], 1)
                    act.wait_ge(S["cb_prod"], upto(g, "cb_prod", bb + 1))
                    act.sem_inc(free, 1)
                act.wait_ge(S["y_gated"], upto(g, "y_gated", NB))
                A(ysq[:, :, :], ym[:, :, :, :].rearrange("p j b t -> p j (b t)"), ACT.Square).then_inc(S["y_squared"], 1)
                act.wait_ge(*bank_filled(g, "m_ss"))
                t, free = bank_to_read("m_ss")
                A(rst[:, :], t[:, :], ACT.Ln, bias=EPS, scale=0.5).then_inc(S["y_log"], 1)
                act.wait_ge(S["y_log"], upto(g, "y_log", 1))
                A(rst[:, :], rst[:, :], ACT.Exp, scale=-0.5).then_inc(S["y_rstd"], 1)
                act.sem_inc(free, 1)
                act.preload_act_table(ACT.Gelu)
                for e in range(NE):
                    if e >= 2:
                        act.wait_ge(S["mixed"], upto(g, "mixed", e - 1))
                    act.wait_ge(*bank_filled(g, ("expert", e)))
                    t, free = bank_to_read(("expert", e))
                    A(eg[:, e % 2, :], t[:, :], ACT.Gelu, bias=col("eb", e)).then_inc(S["expert"], 1)
                    act.wait_ge(S["expert"], upto(g, "expert", e + 1))
                    act.sem_inc(free, 1)
                act.preload_act_table(ACT.Silu)
                act.wait_ge(S["mixed"], upto(g, "mixed", NE))
                A(gate[:, :], mix[:, :, :].rearrange("p b t -> p (b t)"), ACT.Silu).then_inc(S["silu"], 1)
                act.wait_ge(*bank_filled(g, "outT"))
                t, free = bank_to_read("outT")
                A(out_rows[:, :, :].rearrange("p t d -> p (t d)"), t[:, :], ACT.Identity).then_inc(S["out_rows"], 1)
                act.wait_ge(S["out_rows"], upto(g, "out_rows", 1))
                act.sem_inc(free, 1)
                act.sem_inc(S["act_trip"], 1)

        @block.vector
        def _(dve):
            for i in range(len(spans)):
                dve.wait_ge(weights_in[i], 16)
            dve.wait_ge(tables_in, 16)
            for l in range(DEPTH):
                for k, scale in enumerate(("qs", "qsr", "ks", "ksr")):
                    dve.tensor_scalar(rope[:, l, k, :], rope0[:, k, :], col(scale, l), None, ALU.mult).then_inc(setup, 1)
            for j in range(2):
                dve.tensor_scalar(outp[:, j, :], outp[:, j, :], col("nw", j), None, ALU.mult)\
                    .then_inc(setup, 1)
            dve.wait_ge(setup, SETUP - 1)
            dve.tensor_scalar(neg_a, neg_a, -1.0, None, ALU.mult).then_inc(setup, 1)
            dve.wait_ge(setup, SETUP)
            dve.wait_ge(consts, CONSTS)
            dve.sem_inc(max_read, 2)
            for b in range(NBANK):
                dve.sem_inc(work_read[b], 1)
            dve.sem_inc(S["dve_trip"], 1)
            TS, TT, STT = dve.tensor_scalar, dve.tensor_tensor, dve.scalar_tensor_tensor

            def layer_norm(g, n, src, dst):
                dve.wait_ge(*bank_filled(g, ("mean", n)))
                t, free = bank_to_read(("mean", n))
                TT(cen[:, :], src, t[:, :], ALU.subtract).then_inc(S["ln_centered"], 1)
                dve.wait_ge(S["ln_centered"], upto(g, "ln_centered", n + 1))
                dve.sem_inc(free, 1)
                dve.wait_ge(S["ln_rstd"], upto(g, "ln_rstd", n + 1))
                TT(dst, cen[:, :], rst[:, :], ALU.mult).then_inc(S["ln_done"], 1)
                dve.wait_ge(S["ln_done"], upto(g, "ln_done", n + 1))

            def shift(g, k, src):
                s3 = src.rearrange("p (b t) -> p b t", b=NB)
                dve.tensor_copy(hT[0:64, :, :], s3[0:64, :, :])
                dve.tensor_copy(hT[64:128, :, 1:], s3[64:128, :, 0:SEQ - 1]).then_inc(S["shifted"], 1)
                dve.wait_ge(S["shifted"], upto(g, "shifted", k))

            def rows2(t):
                return t.rearrange("p (b t) -> p b t", b=NB)

            def table(l, k):
                return rope[:, l, k, :].unsqueeze(1).to_broadcast([128, NB, SEQ])

            with dve.Fori(0, NG) as g:
                dve.wait_ge(S["pe_trip"], g + 1)
                dve.wait_ge(S["act_trip"], g + 1)
                dve.wait_ge(S["pool_trip"], g + 1)
                dve.wait_ge(S["sp_trip"], g + 1)
                dve.wait_ge(S["xT"], upto(g, "xT", 1))
                layer_norm(g, 0, xT[:, :], xn[:, :])
                for i, b in enumerate(("bq", "bk")):
                    dve.wait_ge(*bank_filled(g, ("a_proj", i)))
                    t, free = bank_to_read(("a_proj", i))
                    TS(f32op[:, i, :], t[:, :], col(b), None, ALU.add).then_inc(S["a_q32"], 1)
                    dve.wait_ge(S["a_q32"], upto(g, "a_q32", i + 1))
                    dve.sem_inc(free, 1)
                    dve.wait_ge(S["a_part0"], upto(g, "a_part0", i + 1))
                    TT(rest[:, i, :], f32op[:, i, :], parts[:, i, 0, :], ALU.subtract).then_inc(S["a_rest1"], 1)
                    dve.wait_ge(S["a_part1"], upto(g, "a_part1", i + 1))
                    TT(parts[:, i, 2, :], rest[:, i, :], parts[:, i, 1, :], ALU.subtract).then_inc(S["a_part2"], 1)
                dve.wait_ge(*bank_filled(g, "a_v"))
                t, free = bank_to_read("a_v")
                dve.tensor_copy(VA[:, :, :, 0:ADH], t[:, :].rearrange("p (t h d) -> p t h d", t=NT, h=AH))\
                    .then_inc(S["a_v"], 1)
                dve.wait_ge(S["a_v"], upto(g, "a_v", 1))
                dve.sem_inc(free, 1)
                shift(g, 1, xn[:, :])
                for n, (bb, h) in enumerate(units()):
                    dve.wait_ge(max_filled, g * 2 * AH + n + 1)
                    dve.tensor_reduce(nmax[:, 2 * bb:2 * bb + 2, (h % 2) * AP + h // 2],
                                      MAXB[n % 2][:, :].rearrange("p (a k) -> p a k", a=2), AXX, ALU.max,
                                      negate=True).then_inc(S["neg_max"], 1)
                    dve.wait_ge(S["neg_max"], upto(g, "neg_max", n + 1))
                    dve.sem_inc(max_read, 1)
                dve.wait_ge(S["m_part0"], upto(g, "m_part0", 1))
                TT(mrest[:, :], mx[:, :], mparts[:, 0, :], ALU.subtract).then_inc(S["m_rest1"], 1)
                dve.wait_ge(S["m_part1"], upto(g, "m_part1", 1))
                TT(mparts[:, 2, :], mrest[:, :], mparts[:, 1, :], ALU.subtract).then_inc(S["m_part2"], 1)
                o = PVB[:, 0:2 * AH * (ADH + 1)].rearrange("p (a h d) -> p a h d", a=2, h=AH)
                for bb in range(NB):
                    dve.wait_ge(pv_filled, g * NB + bb + 1)
                    dve.wait_ge(S["a_pv"], upto(g, "a_pv", (bb + 1) * AH))
                    dve.reciprocal(arsum[:, bb, :, :], o[:, :, :, ADH]).then_inc(S["a_rsum"], 1)
                    dve.wait_ge(S["a_rsum"], upto(g, "a_rsum", bb + 1))
                    TT(AN[:, 2 * bb:2 * bb + 2, :, :], o[:, :, :, 0:ADH],
                       arsum[:, bb, :, :].unsqueeze(3).to_broadcast([128, 2, AH, ADH]), ALU.mult)\
                        .then_inc(S["a_norm"], 1)

                for l in range(DEPTH):
                    src = xn if l == 0 else yT
                    for p in range(FP):
                        k = l * FP + p
                        for name, c, ca, sa in (("fq", 0, "q_cos", "q_sin"), ("fk", 2, "k_cos", "k_sin")):
                            b = 0 if c == 0 else 1
                            dve.wait_ge(*bank_filled(g, (name, l, p)))
                            t, free = bank_to_read((name, l, p))
                            if k > 0:
                                dve.wait_ge(S["q_rot" if b == 0 else "k_rot"], upto(g, "q_rot" if b == 0 else "k_rot", k))
                            TT(rows2(cosp[:, b, :]), rows2(t[:, :]), table(l, c), ALU.mult).then_inc(S[ca], 1)
                            dve.wait_ge(*bank_filled(g, (name + "r", l, p)))
                            t, free = bank_to_read((name + "r", l, p))
                            TT(rows2(sinp[:, b, :]), rows2(t[:, :]), table(l, c + 1), ALU.mult).then_inc(S[sa], 1)
                            dve.wait_ge(S[sa], upto(g, sa, k + 1))
                            dve.sem_inc(free, 1)
                        dve.wait_ge(*bank_filled(g, ("k_norm", l, p)))
                        t, free = bank_to_read(("k_norm", l, p))
                        TS(kn[:, p % 2, :], t[:, :], 1e-24, None, ALU.max).then_inc(S["k_norm2"], 1)
                        dve.wait_ge(S["k_norm2"], upto(g, "k_norm2", k + 1))
                        dve.sem_inc(free, 1)
                        dve.wait_ge(S["k_rnorm"], upto(g, "k_rnorm", k + 1))
                        dve.wait_ge(S["k_rot"], upto(g, "k_rot", k + 1))
                        TT(KR[:, p, :], KR[:, p, :], kn[:, p % 2, :], ALU.mult).then_inc(S["k_final"], 1)
                        dve.wait_ge(S["k_final"], upto(g, "k_final", k + 1))
                    dve.wait_ge(*bank_filled(g, ("q_norm", l)))
                    t, free = bank_to_read(("q_norm", l))
                    TS(qn[:, :, :].rearrange("p t h -> p (t h)"), t[:, 0:NT * FH], 1e-24, None, ALU.max)\
                        .then_inc(S["q_norm2"], 1)
                    dve.wait_ge(S["q_norm2"], upto(g, "q_norm2", l + 1))
                    dve.sem_inc(free, 1)
                    dve.wait_ge(S["q_rnorm"], upto(g, "q_rnorm", l + 1))
                    for n, (bb, h) in enumerate(fills(l)):
                        k = l * NB * FH + n
                        dve.wait_ge(*bank_filled(g, ("f_s", l, n)))
                        t, free = bank_to_read(("f_s", l, n))
                        if n > 0:
                            TS(fnm[:, n - 1, :], fmx[:, n - 1, :], -1.0, None, ALU.mult).then_inc(S["f_negmax"], 1)
                        else:
                            dve.sem_inc(spacer, 1)
                        for u, a, e in ((0, 0, 128), (1, 128, SW)):
                            m = dve.tensor_tensor_reduce(MS[:, n, a:e], t[:, a:e], wt("band")[:, a:e],
                                                         qn[:, 2 * bb + u, h:h + 1], -3.0e38, ALU.add, ALU.max,
                                                         fmx[:, n, u:u + 1])
                        m.then_inc(S["f_masked"], 1)
                        dve.wait_ge(S["f_masked"], upto(g, "f_masked", k + 1))
                        dve.sem_inc(free, 1)
                    TS(fnm[:, n, :], fmx[:, n, :], -1.0, None, ALU.mult).then_inc(S["f_negmax"], 1)

                    def rsum(n):
                        k = l * NB * FH + n
                        dve.wait_ge(S["f_exp"], upto(g, "f_exp", k + 1))
                        dve.reciprocal(frs[:, n, :], fsum[:, n, :]).then_inc(S["f_rsum"], 1)

                    def copy_pT(n):
                        k = l * NB * FH + n
                        dve.wait_ge(*bank_filled(g, ("f_pT", l, n)))
                        t, free = bank_to_read(("f_pT", l, n))
                        if n >= NPP:
                            dve.wait_ge(*bank_filled(g, ("f_o", l, (n - NPP) // 2)))
                        P = PP[:, n % NPP, :]
                        dve.tensor_copy(P[:, 0:128], t[:, 0:128])
                        dve.tensor_copy(P[0:64, 128:256], t[0:64, 128:256])
                        dve.tensor_copy(P[:, 256:384], t[:, 256:384]).then_inc(S["f_probsT"], 1)
                        dve.wait_ge(S["f_probsT"], upto(g, "f_probsT", k + 1))
                        dve.sem_inc(free, 1)

                    for n in range(NB * FH + 2):
                        if n < NB * FH:
                            rsum(n)
                        if n >= 2:
                            copy_pT(n - 2)
                    dve.wait_ge(*bank_filled(g, ("f_wo", l)))
                    t, free = bank_to_read(("f_wo", l))
                    TT(yT[:, :], t[:, :], src[:, :], ALU.add).then_inc(S["f_res1"], 1)
                    dve.wait_ge(S["f_res1"], upto(g, "f_res1", l + 1))
                    dve.sem_inc(free, 1)
                    shift(g, 2 * l + 2, yT[:, :])
                    layer_norm(g, 1 + l, hT[:, :, :].rearrange("p b t -> p (b t)"), hn[:, :])
                    TS(hn[:, :], hn[:, :], col(f"lg{l}"), col(f"lb{l}"), ALU.mult, ALU.add).then_inc(S["f_affine"], 1)
                    for c in range(HC):
                        r = HCN[c]
                        dve.wait_ge(S["f_gelu"], upto(g, "f_gelu", l * HC + c + 1))
                        dve.wait_ge(*bank_filled(g, ("w1", l, c, 0)))
                        t, free = bank_to_read(("w1", l, c, 0))
                        STT(out=hid[0:r, c, :], in0=t[0:r, :], scalar=col(f"b1{l}", c, r), in1=ge[0:r, c, :],
                            op0=ALU.add, op1=ALU.mult).then_inc(S["f_hidden"], 1)
                        dve.wait_ge(S["f_hidden"], upto(g, "f_hidden", l * HC + c + 1))
                        dve.sem_inc(free, 1)
                    dve.wait_ge(*bank_filled(g, ("w2", l)))
                    t, free = bank_to_read(("w2", l))
                    STT(out=yT[:, :], in0=t[:, :], scalar=col(f"b2{l}"), in1=yT[:, :], op0=ALU.add,
                        op1=ALU.add).then_inc(S["f_res2"], 1)
                    dve.wait_ge(S["f_res2"], upto(g, "f_res2", l + 1))
                    dve.sem_inc(free, 1)
                    if l + 1 < DEPTH:
                        shift(g, 2 * l + 3, yT[:, :])

                dve.wait_ge(S["silu"], upto(g, "silu", 1))
                dve.wait_ge(S["attn_out"], upto(g, "attn_out", 1))
                TT(s_out[:, :], s_out[:, :], gate[:, :], ALU.mult).then_inc(S["gated"], 1)
                dve.wait_ge(S["gated"], upto(g, "gated", 1))
                TT(x1T[:, :], s_out[:, :], xT[:, :], ALU.add).then_inc(S["x_new"], 1)
                dve.wait_ge(S["x_new"], upto(g, "x_new", 1))
                layer_norm(g, 3, x1T[:, :], xn[:, :])
                dve.wait_ge(*bank_filled(g, "m_dt"))
                t, free = bank_to_read("m_dt")
                heads = [128, NT, MH]
                TT(dt_raw, t[:, 0:NT * MH].rearrange("p (t h) -> p t h", t=NT),
                   wt("dtb").unsqueeze(1).to_broadcast(heads), ALU.add).then_inc(S["dt_raw"], 1)
                dve.wait_ge(S["dt_raw"], upto(g, "dt_raw", 1))
                dve.sem_inc(free, 1)
                dve.tensor_reduce(pool[:, :], rows2(xn[:, :]), AXX, ALU.add).then_inc(S["pooled"], 1)
                dve.wait_ge(S["pooled"], upto(g, "pooled", 1))
                for bb in range(NB):
                    TS(poolb[:, bb, :], pool[:, bb:bb + 1].to_broadcast([128, 128]), 1.0 / SEQ, None, ALU.mult)\
                        .then_inc(S["pool_rows"], 1)
                TS(dt_pos, dt_raw, 0.0, None, ALU.max)
                dve.wait_ge(S["dt_exp"], upto(g, "dt_exp", 1))
                TS(dt_w, dt_e, 2.0, None, ALU.add).then_inc(S["dt_step"], 1)
                dve.wait_ge(S["dt_step"], upto(g, "dt_step", 1))
                dve.reciprocal(dt_w, dt_w).then_inc(S["dt_step"], 1)
                dve.wait_ge(S["dt_step"], upto(g, "dt_step", 2))
                TT(dt_w, dt_w, dt_e, ALU.mult).then_inc(S["dt_step"], 1)
                dve.wait_ge(S["dt_step"], upto(g, "dt_step", 3))
                TT(dt_w2, dt_w, dt_w, ALU.mult).then_inc(S["dt_step"], 1)
                for k, c in enumerate(SERIES):
                    dve.wait_ge(S["dt_step"], upto(g, "dt_step", 4 + k))
                    if k == 0:
                        TS(dt_p, dt_w2, c, None, ALU.mult).then_inc(S["dt_step"], 1)
                    else:
                        STT(out=dt_p, in0=dt_p, scalar=c, in1=dt_w2, op0=ALU.add, op1=ALU.mult)\
                            .then_inc(S["dt_step"], 1)
                dve.wait_ge(S["dt_step"], upto(g, "dt_step", 4 + len(SERIES)))
                STT(out=dt_p, in0=dt_p, scalar=1.0, in1=dt_w, op0=ALU.add, op1=ALU.mult).then_inc(S["dt_step"], 1)
                dve.wait_ge(S["dt_step"], upto(g, "dt_step", 5 + len(SERIES)))
                STT(out=dt_, in0=dt_p, scalar=2.0, in1=dt_pos, op0=ALU.mult, op1=ALU.add).then_inc(S["dt"], 1)
                dve.wait_ge(S["dt"], upto(g, "dt", 1))
                TT(dt_dA, dt_, neg_a.unsqueeze(1).to_broadcast(heads), ALU.mult).then_inc(S["dt_a"], 1)
                for j in range(XBC):
                    dve.wait_ge(S["conv_in"], upto(g, "conv_in", j + 1))
                    for k in range(TAPS):
                        a = cin[:, j, :, k:k + SEQ]
                        if k == 0:
                            TS(cv[:, j, :, :], a, col("cw", j * TAPS), col("cb", j), ALU.mult, ALU.add)\
                                .then_inc(S["conv"], 1)
                        else:
                            dve.wait_ge(S["conv"], upto(g, "conv", j * TAPS + k))
                            STT(out=cv[:, j, :, :], in0=a, scalar=col("cw", j * TAPS + k), in1=cv[:, j, :, :],
                                op0=ALU.mult, op1=ALU.add).then_inc(S["conv"], 1)
                dve.wait_ge(*bank_filled(g, "logits"))
                t, free = bank_to_read("logits")
                TT(lg_[:, :, :], t[:, 0:NB * NE].rearrange("p (b e) -> p b e", b=NB),
                   wt("gb").unsqueeze(1).to_broadcast([128, NB, NE]), ALU.add).then_inc(S["logits"], 1)
                dve.wait_ge(S["logits"], upto(g, "logits", 1))
                dve.sem_inc(free, 1)
                for bb in range(NB):
                    dve.max(top[:, bb, :], lg_[:, bb, :]).then_inc(S["top"], 1)
                for bb in range(NB):
                    dve.wait_ge(S["top"], upto(g, "top", bb + 1))
                    TS(gsm[:, bb, 0:1], top[:, bb, 0:1], -1.0, None, ALU.mult).then_inc(S["g_negmax"], 1)
                    TS(gkp[:, bb, :], lg_[:, bb, :], top[:, bb, 1:2], None, ALU.is_ge).then_inc(S["g_keep"], 1)
                for bb in range(NB):
                    dve.wait_ge(S["g_exp"], upto(g, "g_exp", bb + 1))
                    dve.wait_ge(S["g_keep"], upto(g, "g_keep", bb + 1))
                    dve.tensor_tensor_reduce(gkp[:, bb, :], gkp[:, bb, :], gex[:, bb, :], 1.0, 0.0, ALU.mult,
                                             ALU.add, gsm[:, bb, 1:2]).then_inc(S["g_sum"], 1)
                for bb in range(NB):
                    dve.wait_ge(S["g_sum"], upto(g, "g_sum", bb + 1))
                    dve.reciprocal(gsm[:, bb, 2:3], gsm[:, bb, 1:2]).then_inc(S["g_rsum"], 1)
                for bb in range(NB):
                    dve.wait_ge(S["g_rsum"], upto(g, "g_rsum", bb + 1))
                    TS(gt[:, bb, :], gkp[:, bb, :], gsm[:, bb, 2:3], None, ALU.mult).then_inc(S["gates"], 1)
                for j in range(NT):
                    dve.wait_ge(*bank_filled(g, ("m_xt", j)))
                    t, free = bank_to_read(("m_xt", j))
                    TT(xd[:, j, :, :], t[:, 0:DI].rearrange("p (h d) -> p h d", h=MH),
                       dt_[:, j, :].unsqueeze(2).to_broadcast([128, MH, MDH]), ALU.mult)\
                        .then_inc(S["xdt"], 1)
                    dve.wait_ge(S["xdt"], upto(g, "xdt", j + 1))
                    dve.sem_inc(free, 1)
                dve.wait_ge(S["z_silu"], upto(g, "z_silu", 2))
                for bb in range(NB):
                    dve.wait_ge(S["cb_prod"], upto(g, "cb_prod", bb + 1))
                    for h in range(MH):
                        n = bb * MH + h
                        dve.wait_ge(*bank_filled(g, ("m_dA", bb, h)))
                        t, free = bank_to_read(("m_dA", bb, h))
                        dve.tensor_tensor_scan(dec[:, n % 2, 0:256], t[:, 0:256], wt("step"), 0.0, ALU.mult, ALU.add)
                        dve.tensor_tensor_scan(dec[:, n % 2, 256:384], t[:, 128:256], wt("step")[:, 0:128], 0.0,
                                               ALU.mult, ALU.add).then_inc(S["decay"], 1)
                        dve.wait_ge(S["decay"], upto(g, "decay", n + 1))
                        dve.sem_inc(free, 1)
                        if n >= 2:
                            dve.wait_ge(S["weights_used"], upto(g, "weights_used", n - 1))
                        TT(wgt[:, n % 2, :], dec[:, n % 2, :], cbp[:, bb, :], ALU.mult).then_inc(S["weights"], 1)
                    dve.wait_ge(S["weights_used"], upto(g, "weights_used", (bb + 1) * MH))
                    t = PVB
                    for j in range(2):
                        m = STT(out=ym[:, j, bb, :], in0=rows2(cs[:, j, :])[:, bb, :], scalar=col("dsk", j),
                                in1=t[:, j * SEQ:j * SEQ + SEQ], op0=ALU.mult, op1=ALU.add)
                    m.then_inc(S["y_skip"], 1)
                    dve.wait_ge(S["y_skip"], upto(g, "y_skip", bb + 1))
                    TT(ym[:, :, bb, :], ym[:, :, bb, :],
                       zs[:, :, bb * SEQ:bb * SEQ + SEQ], ALU.mult).then_inc(S["y_gated"], 1)
                dve.wait_ge(S["y_rstd"], upto(g, "y_rstd", 1))
                dve.wait_ge(*bank_filled(g, "m_out"))
                t, free = bank_to_read("m_out")
                TT(s_out[:, :], t[:, :], rst[:, :], ALU.mult).then_inc(S["mamba_out"], 1)
                dve.wait_ge(S["mamba_out"], upto(g, "mamba_out", 1))
                dve.sem_inc(free, 1)
                TT(s_out[:, :], s_out[:, :], xn[:, :], ALU.add).then_inc(S["mamba_out"], 1)
                dve.wait_ge(S["gates"], upto(g, "gates", NB))
                for e in range(NE):
                    dve.wait_ge(S["expert"], upto(g, "expert", e + 1))
                    if e > 0:
                        dve.wait_ge(S["mixed"], upto(g, "mixed", e))
                    for bb in range(NB):
                        a = rows2(eg[:, e % 2, :])[:, bb, :]
                        if e == 0:
                            m = TS(mix[:, bb, :], a, gt[:, bb, e:e + 1], None, ALU.mult)
                        else:
                            m = STT(out=mix[:, bb, :], in0=a, scalar=gt[:, bb, e:e + 1], in1=mix[:, bb, :],
                                    op0=ALU.mult, op1=ALU.add)
                    m.then_inc(S["mixed"], 1)
                dve.wait_ge(S["silu"], upto(g, "silu", 2))
                dve.wait_ge(S["mamba_out"], upto(g, "mamba_out", 2))
                TT(s_out[:, :], s_out[:, :], gate[:, :], ALU.mult).then_inc(S["gated"], 1)
                dve.wait_ge(S["gated"], upto(g, "gated", 2))
                TT(xT[:, :], s_out[:, :], x1T[:, :], ALU.add).then_inc(S["x_new"], 1)
                dve.sem_inc(S["dve_trip"], 1)

        @block.gpsimd
        def _(pool_):
            n = 0
            for dst, value in ((KS[:, :, :], 1.0), (lat[:, :], 1.0), (VA[:, :, :, :], 1.0), (hT[:, :, :], 0.0),
                               (cin[:, :, :, :], 0.0), (EPS, 1e-5), (HALF_SHIFT, LN_SHIFT / 2),
                               (HALF_SHIFT8, LN_SHIFT / 2 + LN_8), (ONE, 1.0)):
                pool_.memset(dst, value).then_inc(consts, 1)
                n += 1
            assert n == CONSTS
            pool_.sem_inc(S["pool_trip"], 1)
            with pool_.Fori(0, NG) as g:
                pool_.wait_ge(S["pe_trip"], g + 1)
                pool_.wait_ge(S["act_trip"], g + 1)
                pool_.wait_ge(S["dve_trip"], g + 1)
                pool_.wait_ge(S["sp_trip"], g + 1)
                for l in range(DEPTH):
                    for p in range(FP):
                        k = l * FP + p
                        pool_.wait_ge(S["q_sin"], upto(g, "q_sin", k + 1))
                        pool_.wait_ge(S["q_cos"], upto(g, "q_cos", k + 1))
                        pool_.tensor_tensor(QR[:, p, :], cosp[:, 0, :], sinp[:, 0, :], ALU.add).then_inc(S["q_rot"], 1)
                        pool_.wait_ge(S["k_sin"], upto(g, "k_sin", k + 1))
                        pool_.wait_ge(S["k_cos"], upto(g, "k_cos", k + 1))
                        pool_.tensor_tensor(KR[:, p, :], cosp[:, 1, :], sinp[:, 1, :], ALU.add).then_inc(S["k_rot"], 1)
                    for n in range(NB * FH):
                        k = l * NB * FH + n
                        pool_.wait_ge(S["f_rsum"], upto(g, "f_rsum", k + 1))
                        pool_.sem_inc(spacer, 1)
                        pool_.tensor_scalar(MS[:, n, 0:128], MS[:, n, 0:128], frs[:, n, 0:1], None, ALU.mult)
                        pool_.tensor_scalar(MS[:, n, 128:SW], MS[:, n, 128:SW], frs[:, n, 1:2], None, ALU.mult)\
                            .then_inc(S["f_probs"], 1)
                pool_.sem_inc(S["pool_trip"], 1)

        @block.sync
        def _(sp):
            for i, (a, e) in enumerate(spans):
                sp.dma_start(W[:, a:e], w[:, a:e]).then_inc(weights_in[i], 16)
            sp.dma_start(rope0, tables).then_inc(tables_in, 16)
            sp.wait_ge(consts, CONSTS)
            sp.sem_inc(S["sp_trip"], 1)
            with sp.Fori(0, NG) as g:
                sp.wait_ge(S["pe_trip"], g + 1)
                sp.wait_ge(S["act_trip"], g + 1)
                sp.wait_ge(S["dve_trip"], g + 1)
                sp.wait_ge(S["pool_trip"], g + 1)
                sp.dma_start(x_rows[:, :, :], x[g]).then_inc(S["x_loaded"], 16)
                for i, (dst, which, name) in enumerate(((QS, Q_PART, "q_spread"), (KS, K_PART, "k_spread"))):
                    for part in range(NPART):
                        sp.wait_ge(S[("a_part0", "a_part1", "a_part2")[part]], upto(g, ("a_part0", "a_part1", "a_part2")[part], i + 1))
                        for r, part_r in enumerate(which):
                            if part_r == part:
                                for lo in (0, 64):
                                    sp.dma_start(dst[lo + r * ADH:lo + r * ADH + ADH, :, :],
                                                 parts[lo:lo + 64, i, part, :]).then_inc(S[name], 16)
                for part in range(NPART):
                    sp.wait_ge(S[("m_part0", "m_part1", "m_part2")[part]], upto(g, ("m_part0", "m_part1", "m_part2")[part], 1))
                    for i in range(2):
                        row = 64 * i + QROWS + part
                        sp.dma_start(QS[row:row + 1, :, :], mparts[i * AP:i * AP + AP, part, :])\
                            .then_inc(S["m_spread"], 16)
                sp.wait_ge(S["out_rows"], upto(g, "out_rows", 1))
                sp.dma_start(out[g], out_rows[:, :, :]).then_inc(S["out_stored"], 16)
                sp.wait_ge(S["out_stored"], upto(g, "out_stored", 16))
                sp.sem_inc(S["sp_trip"], 1)


CONSTS = 9
SETUP = DEPTH * 4 + 2 + 1 + 1


def rotary_tables():
    import numpy as np

    half = np.arange(0, FDH, 2, dtype=np.float32)
    freqs = np.arange(SEQ, dtype=np.float32)[:, None] * (np.float32(1.0) / np.float32(10000.0) ** (half / FDH))[None, :]
    base = (half + 0.4 * FDH) / (1.4 * FDH)
    power = (np.arange(SEQ, dtype=np.float32) - SEQ // 2) / float(WIN // 2)
    scale = (base[None, :].astype(np.float64) ** power[:, None]).T
    cos, sin = np.cos(freqs.astype(np.float64)).T, np.sin(freqs.astype(np.float64)).T
    return np.stack([np.tile(cos * scale, (4, 1)), np.concatenate([-sin * scale, sin * scale] * 2),
                     np.tile(cos / scale, (4, 1)), np.concatenate([-sin / scale, sin / scale] * 2)],
                    1).astype(np.float32)


def host_layout(v):
    import numpy as np

    place, _, width = layout()
    w = np.zeros((128, width), np.float32)

    def put(name, a):
        at, n = place[name]
        a = np.asarray(a)
        w[:a.shape[0], at:at + n] = a

    def colv(a):
        return np.asarray(a).reshape(-1, 1)

    put("ident", np.eye(128))
    put("mean", np.full((128, 128), 1.0 / D))
    r = np.arange(128)
    put("block", (r[:, None] // 64 == r[None, :] // 64) * 1.0)
    put("heads2", (r[:, None] // 64 == np.arange(2)[None, :]) * 1.0)
    gap0 = r[:, None] - r[None, :]
    gap1 = 128 + r[:, None] - (64 + np.arange(192)[None, :])
    gap = np.concatenate([gap0, gap1], 1)
    put("band", np.where((gap < 0) | (gap > WIN), -1e30, 0.0))
    put("step", (r[:, None] == np.arange(SEQ)[None, :]) * 1.0)
    put("sel", np.repeat(np.eye(MH), 128, axis=1))

    def by_pair(a):
        a = np.asarray(a)
        return a.reshape(a.shape[0], AP, 2, ADH).transpose(0, 2, 3, 1).reshape(a.shape[0], D)

    put("wq", by_pair(v["L0_attn_Wq"]))
    put("bq", by_pair(np.asarray(v["L0_attn_bq"]).reshape(1, D)).reshape(D, 1))
    put("wl", v["L0_attn_Wl"])
    put("bl", colv(v["L0_attn_bl"]))
    put("wk", by_pair(v["L0_attn_Wk"]))
    put("bk", by_pair(np.asarray(v["L0_attn_bk"]).reshape(1, D)).reshape(D, 1))
    put("wv", np.concatenate([np.asarray(v["L0_attn_Wv"]), np.asarray(v["L0_attn_bv"]).reshape(1, D)]))
    put("wo", v["L0_attn_Wo"])
    put("bo", colv(v["L0_attn_bo"]))

    def swap(a):
        a = np.asarray(a)
        return a.reshape(a.shape[0], -1, 2, FDH // 2)[:, :, ::-1].reshape(a.shape)

    def twice(a):
        return np.concatenate([a, a])

    for name, src in (("qs", "L0_ffn_q_scale"), ("ks", "L0_ffn_k_scale")):
        s = np.asarray(v[src])
        put(name, twice(s.T))
        put(name + "r", twice(swap(s).T))
    for l in range(DEPTH):
        qkv = np.asarray(v["L0_ffn_wqkv"])[l]
        q, k, vv = qkv[:, :INNER], qkv[:, INNER:2 * INNER], qkv[:, 2 * INNER:]
        put(f"fq{l}", q)
        put(f"fqr{l}", swap(q))
        put(f"fk{l}", k)
        put(f"fkr{l}", swap(k))
        put(f"fv{l}", vv)
        put(f"fo{l}", np.asarray(v["L0_ffn_wo"])[l].reshape(FP, 128, D).transpose(1, 0, 2).reshape(128, FP * D))
        put(f"w1{l}", np.asarray(v["L0_ffn_w1"])[l])
        w2 = np.zeros((128, HC, D), np.float32)
        b1 = np.zeros((128, 2 * HC), np.float32)
        for c in range(HC):
            w2[:HCN[c], c] = np.asarray(v["L0_ffn_w2"])[l][c * HCW:c * HCW + HCN[c]]
            for part in range(2):
                a = part * HID + c * HCW
                b1[:HCN[c], part * HC + c] = np.asarray(v["L0_ffn_b1"])[l][a:a + HCN[c]]
        put(f"w2{l}", w2.reshape(128, HC * D))
        put(f"b1{l}", b1)
        put(f"lg{l}", colv(np.asarray(v["L0_ffn_ln_g"])[l]))
        put(f"lb{l}", colv(np.asarray(v["L0_ffn_ln_b"])[l]))
        put(f"b2{l}", colv(np.asarray(v["L0_ffn_b2"])[l]))
    put("inp", np.asarray(v["L1_attn_in_proj_w"]).T)
    put("cw", np.asarray(v["L1_attn_conv_w"]).reshape(XBC, 128, TAPS).transpose(1, 0, 2).reshape(128, XBC * TAPS))
    put("cb", np.asarray(v["L1_attn_conv_b"]).reshape(XBC, 128).T)
    put("dtb", np.broadcast_to(np.asarray(v["L1_attn_dt_bias"]).reshape(1, MH), (128, MH)))
    put("alog", np.broadcast_to(np.asarray(v["L1_attn_A_log"]).reshape(1, MH), (128, MH)))
    put("dsk", np.repeat(np.asarray(v["L1_attn_D"]), MDH).reshape(2, 128).T)
    put("nw", np.asarray(v["L1_attn_norm_w"]).reshape(2, 128).T)
    put("outp", np.asarray(v["L1_attn_out_proj_w"]).T.reshape(2, 128, D).transpose(1, 0, 2).reshape(128, 2 * D))
    put("gw", np.asarray(v["L1_ffn_gate_w"]).T)
    put("gb", np.broadcast_to(np.asarray(v["L1_ffn_gate_b"]).reshape(1, NE), (128, NE)))
    put("ew", np.asarray(v["L1_ffn_expert_w"]).transpose(2, 0, 1).reshape(D, NE * D))
    put("eb", np.asarray(v["L1_ffn_expert_b"]).T)
    return w


def kernel(**inputs):
    import numpy as np
    import concourse.bacc as bacc
    from concourse.bass_utils import run_bass_kernel_spmd

    nc = bacc.Bacc("TRN2", target_bir_lowering=False, num_devices=1)
    w = host_layout(inputs)
    x = np.ascontiguousarray(np.asarray(inputs["L0_attn_x"]).reshape(NG, NT, 128, D).transpose(0, 2, 1, 3))
    xd = nc.dram_tensor("x", x.shape, F32, kind="ExternalInput").ap()
    wd = nc.dram_tensor("w", w.shape, F32, kind="ExternalInput").ap()
    od = nc.dram_tensor("out", x.shape, F32, kind="ExternalOutput").ap()
    tables = rotary_tables()
    td = nc.dram_tensor("tables", tables.shape, F32, kind="ExternalInput").ap()
    build(nc, xd, wd, td, od)
    r = run_bass_kernel_spmd(nc, [{"x": x, "w": w, "tables": tables}], core_ids=[0])
    got = np.asarray(r.results[0]["out"])
    return np.ascontiguousarray(got.transpose(0, 2, 1, 3)).reshape(BATCH, SEQ, D)
```

```python
import concourse.bass as bass
from concourse import mybir
from contextlib import ExitStack

F32 = mybir.dt.float32
BF16 = mybir.dt.bfloat16
ALU = mybir.AluOpType
ACT = mybir.ActivationFunctionType
AXX = mybir.AxisListType.X

D = 128
SEQ = 256
NB = 2
TOK = NB * SEQ
NT = TOK // 128
BATCH = 16
NG = BATCH // NB
AH, ADH, LATENT = 16, 8, 32
AP = AH // 2
NPART = 3
Q_PART = [0, 0, 0, 1, 1, 2]
K_PART = [0, 1, 2, 0, 1, 0]
QROWS = ADH * len(Q_PART)
MROWS = QROWS + NPART
DEPTH, FH, FDH, WIN = 2, 8, 64, 64
INNER = FH * FDH
FP = INNER // 128
HID = D * 4 * 2 // 3
HC = 3
HCW = -(-HID // HC)
HCN = [min(HCW, HID - c * HCW) for c in range(HC)]
SW = 128 + 192
DI, NS, MH, MDH, TAPS = 256, 128, 4, 64, 4
XBC = (DI + 2 * NS) // 128
NE = 8

NORM_SHIFT = 2.0 ** 20
LN_SHIFT = 20 * 0.6931471805599453
LN_8 = 3 * 0.6931471805599453


def layout():
    parts = [
        [("ident", 128), ("zeros", 128), ("mean", 128), ("wq", 128), ("wl", 32), ("wk", 128), ("wv", 128), ("wo", 128),
         ("bq", 1), ("bl", 1), ("bk", 1), ("bo", 1),
         ("block", 128), ("heads", FP * FH), ("band", SW),
         ("qs", 2), ("qsr", 2), ("ks", 2), ("ksr", 2)],
    ]
    for l in range(DEPTH):
        parts.append([(f"{n}{l}", w) for n, w in [
            ("fq", INNER), ("fqr", INNER), ("fk", INNER), ("fkr", INNER), ("fv", INNER), ("fo", FP * D),
            ("w1", 2 * HID), ("w2", HC * D), ("lg", 1), ("lb", 1), ("b1", 2 * HC), ("b2", 1)]])
    parts.append([("inp", 2 * DI + 2 * NS + MH), ("cw", XBC * TAPS), ("cb", XBC), ("dtb", MH), ("alog", MH),
                  ("dsk", 2), ("nw", 2), ("outp", 2 * D), ("gw", NE), ("gb", NE), ("ew", NE * D), ("eb", NE)])
    at, spans, place = 0, [], {}
    for part in parts:
        first = at
        for name, width in part:
            place[name] = (at, width)
            at += width
        spans.append((first, at))
    return place, spans, at


SERIES = [1.0 / n for n in (15, 13, 11, 9, 7, 5, 3)]

UNITS = NB * AH
GROUPS = UNITS // 4
FUNITS = NB * FH
PER = {
    "x_loaded": 16, "xT": 1,
    "ln_centered": 3, "ln_squared": 3, "ln_log": 3, "ln_rstd": 3, "ln_done": 3,
    "a_q32": 2, "a_part0": 2, "a_rest1": 2, "a_part1": 2, "a_part2": 2,
    "q_spread": 16 * 12, "k_spread": 16 * 12, "m_spread": 16 * 6,
    "latent": 1, "a_v": 1, "max_filled": UNITS, "neg_max": UNITS,
    "m_rows": 1, "m_part0": 1, "m_rest1": 1, "m_part1": 1, "m_part2": 1,
    "exp_filled": UNITS, "a_exp": UNITS, "a_pv": UNITS, "a_heads": GROUPS, "a_rsum": GROUPS, "a_norm": GROUPS,
    "a_oT": 1, "attn_out": 1,
    "shifted": 2 * DEPTH,
    "q_squared": DEPTH * FP, "k_squared": DEPTH * FP, "q_cos": DEPTH * FP, "q_sin": DEPTH * FP,
    "k_cos": DEPTH * FP, "k_sin": DEPTH * FP, "q_rot": DEPTH * FP, "k_rot": DEPTH * FP,
    "k_norm2": DEPTH * FP, "k_nlog": DEPTH * FP, "k_rnorm": DEPTH * FP, "k_final": DEPTH * FP,
    "q_norm2": DEPTH, "q_nlog": DEPTH, "q_rnorm": DEPTH, "f_v": DEPTH * (NT + NB),
    "f_masked": DEPTH * FUNITS, "f_negmax": DEPTH * FUNITS, "f_exp": DEPTH * FUNITS,
    "f_rsum": DEPTH * FUNITS, "f_probs": DEPTH * FUNITS, "f_probsT": DEPTH * FUNITS,
    "f_oT": DEPTH * FUNITS // 2, "f_res1": DEPTH, "f_affine": DEPTH,
    "f_gelu": DEPTH * HC, "f_hidden": DEPTH * HC, "f_res2": DEPTH,
    "f_silu": 1, "f_gated": 1, "x1": 1,
    "c_centered": 1, "c_squared": 1, "c_log": 1, "c_rstd": 1, "c_xn": 1,
    "conv_in": XBC, "conv": XBC * TAPS, "conv_silu": XBC, "z_silu": 2,
    "dt_raw": 1, "dt_abs": 1, "dt_exp": 1, "dt_step": 5 + len(SERIES), "dt": 1, "dt_a": 1, "dA": 1, "dA_rows": 1,
    "xdt": NT, "cb_prod": NB, "decay": NB * MH, "weights": NB * MH, "weights_used": NB * MH,
    "y_skip": NB, "y_gated": NB, "y_squared": 1, "y_log": 1, "y_rstd": 1, "mamba_out": 2,
    "pooled": 1, "pool_rows": NB, "logits": 1, "top": NB, "g_keep": NB, "g_negmax": NB, "g_exp": NB,
    "g_sum": NB, "g_rsum": NB, "gates": NB, "expert": NE, "mixed": NE,
    "c_silu": 1, "c_gated": 1, "x2": 1, "out_rows": 1, "out_stored": 16,
}
TRIPS = ["pe_trip", "act_trip", "dve_trip", "pool_trip", "sp_trip"]

F_STEPS = [("f_ln0", 9)]
for _l in range(DEPTH):
    F_STEPS += [("f_proj", 5, _l, p) for p in range(FP)] + [("f_norms", 6, _l)]
    F_STEPS += [("f_v", 3, _l, half) for half in range(2)]
    F_STEPS += [("f_att", 4, _l, s) for s in range(FUNITS // 2 + 3)]
    F_STEPS += [("f_wo", 5, _l), ("f_ln", 5, _l), ("f_mlp", 10, _l)]
A_STEPS = [("a_proj", 5), ("a_kv", 14)] + [("a_max", 2, s) for s in range(UNITS // 2)] + [("a_maxT", 10)]
A_STEPS += [("a_exp", 2, s) for s in range(UNITS // 2 + 2)] + [("a_out", 3)]
C_STEPS = [("c_ln", 6), ("c_dt", 6), ("c_conv", 5, 0), ("c_conv", 5, 1), ("c_z", 4), ("c_rows", 5)]
C_STEPS += [("c_head", 3, n) for n in range(NB * MH)]
C_STEPS += [("c_norm", 5), ("c_expert", 5, 0), ("c_expert", 5, 1), ("c_end", 5)]
F_END = [("f_end", 3)]


def side_by_side(a, b):
    def placed(steps):
        total, at = float(sum(s[1] for s in steps)), 0.0
        for s in steps:
            yield (at / total, s)
            at += s[1]

    both = sorted(list(placed(a)) + list(placed(b)), key=lambda e: e[0])
    return [(s[0],) + tuple(s[2:]) for _, s in both]


FIRST_ORDER = side_by_side(F_STEPS, A_STEPS) + [("f_end",)]
ORDER = side_by_side(F_STEPS, C_STEPS + A_STEPS) + [("f_end",)]
LAST_ORDER = [(s[0],) + tuple(s[2:]) for s in C_STEPS]

NBANK = 4
FA_TILES, C_TILES = 174, 36


def build(nc, x, w, tables, out):
    place, spans, width = layout()
    ctx = ExitStack()
    with ctx:
        def sb(name, shape, dt=F32):
            return ctx.enter_context(nc.sbuf_tensor(name, shape, dt))

        def sem(name):
            return ctx.enter_context(nc.semaphore(name))

        W = sb("W", [128, width])

        def wt(name, rows=128):
            a, n = place[name]
            return W[0:rows, a:a + n]

        def col(name, j=0, rows=128):
            a, _ = place[name]
            return W[0:rows, a + j:a + j + 1]

        ident = wt("ident")
        at_ident, _ = place["ident"]
        step = W[:, at_ident:at_ident + SEQ]
        cols = sb("cols", [128, 3])
        EPS, HALF_SHIFT, HALF_SHIFT8 = (cols[:, j:j + 1] for j in range(3))
        rope = sb("rope", [128, DEPTH, 4, SEQ])
        outp = wt("outp").rearrange("p (j d) -> p j d", j=2)
        neg_a = wt("alog")

        f32op = sb("f32op", [128, 2, TOK])
        rest = sb("rest", [128, 2, TOK])
        parts = sb("parts", [128, 2, NPART, TOK], BF16)
        QS = sb("QS", [128, AP, TOK], BF16)
        KS = sb("KS", [128, AP, TOK], BF16)
        lat = sb("lat", [LATENT + 1, TOK])
        VW = ADH + 1
        VA = sb("VA", [128, NT, AH * VW + 32 - VW])
        nmax = sb("nmax", [128, NT, AH])
        mxr = sb("mxr", [AH, 2, TOK])
        mx, mrest = mxr[:, 0, :], mxr[:, 1, :]
        mparts = sb("mparts", [AH, NPART, TOK], BF16)
        NPT = 3
        PT = sb("PT", [128, NPT, 2, SEQ])
        heads4 = sb("heads4", [128, 2, SEQ])
        arsum = sb("arsum", [128, 2, 2, 4])
        AO = sb("AO", [128, 2, TOK])
        AN = AO[:, 0, :].rearrange("p (t h d) -> p t h d", t=NT, h=AH)
        aoT = AO[:, 1, :]
        s_out = sb("s_out", [128, TOK])

        x_rows = sb("x_rows", [128, NT, D])
        xT = sb("xT_", [128, TOK])
        xn = sb("xn", [128, TOK])
        cen = sb("cen", [128, TOK])
        sqr = sb("sqr", [128, TOK])
        rst = sqr
        hT = sb("hT", [128, NB, SEQ])
        QR = sb("QR", [128, FP, TOK])
        KR = sb("KR", [128, FP, TOK])
        sqq = sb("sqq", [128, FP, TOK])
        sqk = sb("sqk", [128, 2, TOK])
        sinp = sb("sinp", [128, 2, TOK])
        kn = sb("kn", [128, 2, TOK])
        qn2 = sb("qn2", [FH, TOK])
        qn = sb("qn", [128, NT, FH])
        V = sb("V", [128, NT, INNER])
        VH = sb("VH", [64, NB, INNER])
        NMS = 8
        MS = sb("MS", [128, NMS, SW])
        fmx = sb("fmx", [128, FUNITS, 2])
        fnm = sb("fnm", [128, FUNITS, 2])
        fsum = sb("fsum", [128, FUNITS, 2])
        frs = sb("frs", [128, FUNITS, 2])
        NPP = 4
        PP = sb("PP", [128, NPP, 384])
        OT = sqq
        yT = sb("yT", [128, TOK])
        hn = cen
        ge = MS[:, :, :].rearrange("p n s -> p (n s)")[:, 0:HC * TOK].rearrange("p (c t) -> p c t", c=HC)
        hid = ge
        gate_f = sinp[:, 0, :]

        x1T = sb("x1T", [128, TOK])
        cxn = sb("cxn", [128, TOK])
        ccen = sb("ccen", [128, TOK])
        csqr = sb("csqr", [128, TOK])
        crst = csqr
        cin = sb("cin", [128, XBC, NB, SEQ + TAPS - 1])
        cs = QS[:, :, :].rearrange("p a t -> p (a t)").bitcast(F32).rearrange("p (j t) -> p j t", j=XBC)
        cv = cs.rearrange("p j (b t) -> p j b t", b=NB)
        zs = f32op
        dt7 = sb("dt7", [128, 8, NT, MH])
        dt_raw, dt_e, dt_w, dt_w2, dt_p, dt_pos, dt_, dt_dA = (dt7[:, k, :, :] for k in range(8))
        dA_rows = mxr[0:MH, 0, :]
        xd = rest[:, :, :].rearrange("p a (b h d) -> p (a b) h d", b=2, h=MH)
        pt = PT[:, :, :, :].rearrange("p n c q -> p (n c q)")
        cbp, dec = (pt[:, a * 768:a * 768 + 768].rearrange("p (b t) -> p b t", b=2) for a in range(2))
        pf = parts[:, :, :, :].rearrange("p i r t -> p (i r t)").bitcast(F32)
        wgt = pf[:, 0:768].rearrange("p (b t) -> p b t", b=2)
        out_rows = pf[:, 768:768 + NT * D].rearrange("p (t d) -> p t d", t=NT)
        poolb = pf[:, 1280:1280 + NB * 128].rearrange("p (b k) -> p b k", b=NB)
        ym = AO[:, :, :].rearrange("p j (b t) -> p j b t", b=NB)
        ysq = zs
        eg = pt[:, 0:2 * TOK].rearrange("p (a t) -> p a t", a=2)
        gate_c = heads4[:, :, :].rearrange("p b t -> p (b t)")
        mix = heads4
        x2T = ccen
        pool = sb("pool", [128, NB])
        lg_ = sb("lg_", [128, NB, NE])
        top = sb("top", [128, NB, 8])
        gsm = sb("gsm", [128, NB, 4])
        gex = sb("gex", [128, NB, NE])
        gkp = sb("gkp", [128, NB, NE])
        gt = sb("gt", [128, NB, NE])

        banks = [ctx.enter_context(nc.psum_tensor(f"bank{i}", [128, 512], F32)) for i in range(8)]
        MAXB, EXPB, WORK = banks[0:2], banks[2:4], banks[4:8]
        YB = MAXB[0]
        rope0 = MS[:, :, :].rearrange("p n s -> p (n s)")[:, 0:4 * SEQ].rearrange("p (k t) -> p k t", k=4)

        S = {name: sem(name) for name in list(PER) + TRIPS}
        weights_in = [sem(f"weights_in{i}") for i in range(len(spans))]
        tables_in = sem("tables_in")
        setup = sem("setup")
        consts = sem("consts")
        spacer = sem("spacer")
        work_filled = [sem(f"work_filled{b}") for b in range(NBANK)]
        work_read = [sem(f"work_read{b}") for b in range(NBANK)]

        def upto(g, name, k):
            return g * PER[name] + k

        def uses(tiles):
            return [len(range(b, tiles, NBANK)) for b in range(NBANK)]

        first_uses, loop_uses = uses(FA_TILES), uses(FA_TILES + C_TILES)
        FIRST, LOOP, LAST = range(3)
        work_place = [{}, {}, {}]
        before = [[0] * NBANK, first_uses, [a + (NG - 1) * b for a, b in zip(first_uses, loop_uses)]]
        trip = {"kind": FIRST, "i": 0}

        def turn(n):
            b = n % NBANK
            return before[trip["kind"]][b] + trip["i"] * loop_uses[b] + n // NBANK + 1

        def bank_free(name):
            n = len(work_place[trip["kind"]])
            work_place[trip["kind"]][name] = n
            return work_read[n % NBANK], turn(n)

        def bank_to_fill(name):
            n = work_place[trip["kind"]][name]
            return WORK[n % NBANK], work_filled[n % NBANK]

        def bank_filled(name):
            n = work_place[trip["kind"]][name]
            return work_filled[n % NBANK], turn(n)

        def bank_to_read(name):
            n = work_place[trip["kind"]][name]
            return WORK[n % NBANK], work_read[n % NBANK]

        def run_trips(eng, own, steps):
            def one(kind, i, g, gc, order):
                trip["kind"], trip["i"] = kind, i
                if kind != FIRST:
                    for name in TRIPS:
                        if name != own:
                            eng.wait_ge(S[name], i + 1 if kind == LOOP else NG)
                mine = steps(g, gc)
                for name, *args in order:
                    if name in mine:
                        mine[name](*args)
                eng.sem_inc(S[own], 1)

            one(FIRST, 0, 0, None, FIRST_ORDER)
            with eng.Fori(0, NG - 1) as i:
                one(LOOP, i, i + 1, i, ORDER)
            one(LAST, 0, None, NG - 1, LAST_ORDER)

        def unit(n):
            bb, h = n // AH, n % AH
            return bb, h, h // 2, 64 * (h % 2)

        def funit(n):
            bb, h = n // FH, n % FH
            return bb, h, h // 2, 64 * (h % 2)

        block = ctx.enter_context(nc.Block())

        @block.tensor
        def _(pe):
            for i in range(len(spans)):
                pe.wait_ge(weights_in[i], 16)
            pe.wait_ge(consts, CONSTS)
            pe.wait_ge(setup, SETUP)
            mm = pe.matmul

            def steps(g, gc):
                h2 = hT[:, :, :].rearrange("p b t -> p (b t)")

                def ln_sums(n, src):
                    pe.wait_ge(*bank_free(("mean", n)))
                    t, full = bank_to_fill(("mean", n))
                    mm(t[:, :], wt("mean"), src, start=True, stop=True).then_inc(full, 1)
                    pe.wait_ge(S["ln_squared"], upto(g, "ln_squared", n + 1))
                    pe.wait_ge(*bank_free(("var", n)))
                    t, full = bank_to_fill(("var", n))
                    mm(t[:, :], wt("mean"), sqr[:, :], start=True, stop=True).then_inc(full, 1)

                def f_ln0():
                    pe.wait_ge(S["x_loaded"], upto(g, "x_loaded", 16))
                    pe.wait_ge(*bank_free("xT"))
                    t, full = bank_to_fill("xT")
                    for j in range(NT):
                        m = pe.transpose(t[:, j * 128:j * 128 + 128], x_rows[:, j, :], ident)
                    m.then_inc(full, 1)
                    pe.wait_ge(S["xT"], upto(g, "xT", 1))
                    ln_sums(0, xT[:, :])

                def f_proj(l, p):
                    if p == 0:
                        pe.wait_ge(S["shifted"], upto(g, "shifted", 2 * l + 1))
                    for name in ("fq", "fqr", "fk", "fkr"):
                        pe.wait_ge(*bank_free((name, l, p)))
                        t, full = bank_to_fill((name, l, p))
                        mm(t[:, :], wt(f"{name}{l}")[:, p * 128:p * 128 + 128], h2,
                           start=True, stop=True).then_inc(full, 1)
                    if p > 0:
                        k_norm(l, p - 1)

                def k_norm(l, p):
                    pe.wait_ge(S["k_squared"], upto(g, "k_squared", l * FP + p + 1))
                    pe.wait_ge(*bank_free(("k_norm", l, p)))
                    t, full = bank_to_fill(("k_norm", l, p))
                    mm(t[:, :], wt("block"), sqk[:, p % 2, :], start=True, stop=True).then_inc(full, 1)

                def f_norms(l):
                    k_norm(l, FP - 1)
                    pe.wait_ge(S["q_squared"], upto(g, "q_squared", (l + 1) * FP))
                    pe.wait_ge(*bank_free(("q_norm", l)))
                    t, full = bank_to_fill(("q_norm", l))
                    for p in range(FP):
                        m = mm(t[0:FH, :], wt("heads")[:, p * FH:p * FH + FH], sqq[:, p, :], start=(p == 0),
                               stop=(p == FP - 1))
                    m.then_inc(full, 1)
                    pe.wait_ge(S["q_norm2"], upto(g, "q_norm2", l + 1))
                    pe.wait_ge(*bank_free(("q_normT", l)))
                    t, full = bank_to_fill(("q_normT", l))
                    pe.sem_inc(spacer, 1)
                    for j in range(NT):
                        m = pe.transpose(t[:, j * FH:j * FH + FH], qn2[:, j * 128:j * 128 + 128], ident[0:FH, 0:FH])
                    m.then_inc(full, 1)

                def f_v(l, half):
                    for j in range(2 * half, 2 * half + 2):
                        pe.wait_ge(*bank_free(("f_v", l, j)))
                        t, full = bank_to_fill(("f_v", l, j))
                        mm(t[:, :], h2[:, j * 128:j * 128 + 128], wt(f"fv{l}"), start=True,
                           stop=True).then_inc(full, 1)
                    k0 = half * SEQ + WIN
                    pe.wait_ge(*bank_free(("f_vh", l, half)))
                    t, full = bank_to_fill(("f_vh", l, half))
                    mm(t[0:64, :], h2[:, k0:k0 + WIN], wt(f"fv{l}"), start=True, stop=True).then_inc(full, 1)

                def f_scores(l, n):
                    bb, h, p, lo = funit(n)
                    q0 = bb * SEQ
                    if n < FH:
                        pe.wait_ge(S["q_rot"], upto(g, "q_rot", l * FP + p + 1))
                        pe.wait_ge(S["k_final"], upto(g, "k_final", l * FP + p + 1))
                    pe.wait_ge(*bank_free(("f_s", l, n)))
                    t, full = bank_to_fill(("f_s", l, n))
                    mm(t[:, 0:128], QR[lo:lo + 64, p, q0:q0 + 128], KR[lo:lo + 64, p, q0:q0 + 128],
                       start=True, stop=True)
                    mm(t[:, 128:SW], QR[lo:lo + 64, p, q0 + 128:q0 + 256],
                       KR[lo:lo + 64, p, q0 + 64:q0 + 256], start=True, stop=True).then_inc(full, 1)

                def f_transposes(l, n):
                    pe.wait_ge(S["f_probs"], upto(g, "f_probs", l * FUNITS + n + 1))
                    pe.wait_ge(*bank_free(("f_pT", l, n)))
                    t, full = bank_to_fill(("f_pT", l, n))
                    P = MS[:, n % NMS, :]
                    pe.transpose(t[:, 0:128], P[:, 0:128], ident)
                    pe.transpose(t[:, 128:256], P[:, 128:256], ident)
                    pe.transpose(t[:, 256:384], P[:, 192:320], ident).then_inc(full, 1)

                def f_pv(l, n):
                    bb, _, p, _ = funit(n)
                    pe.wait_ge(*bank_free(("f_o", l, n // 2)))
                    t, full = bank_to_fill(("f_o", l, n // 2))
                    for i in range(2):
                        pe.wait_ge(S["f_probsT"], upto(g, "f_probsT", l * FUNITS + n + i + 1))
                        P, h = PP[:, (n + i) % NPP, :], 2 * p + i
                        hc = slice(h * FDH, h * FDH + FDH)
                        o = t[64 * i:64 * i + 64, :]
                        mm(o[:, 0:128], V[:, 2 * bb, hc], P[:, 0:128], start=True, stop=True)
                        mm(o[:, 128:256], VH[:, bb, hc], P[0:64, 128:256], start=True, stop=False)
                        m = mm(o[:, 128:256], V[:, 2 * bb + 1, hc], P[:, 256:384], start=False, stop=True)
                    m.then_inc(full, 1)

                def f_att(l, s):
                    if s < FUNITS // 2:
                        f_scores(l, 2 * s)
                        f_scores(l, 2 * s + 1)
                    if 2 <= s < FUNITS // 2 + 2:
                        f_transposes(l, 2 * s - 4)
                        f_transposes(l, 2 * s - 3)
                    if s == 3:
                        pe.wait_ge(S["f_v"], upto(g, "f_v", (l + 1) * (NT + NB)))
                    if 3 <= s:
                        f_pv(l, 2 * s - 6)

                def f_wo(l):
                    pe.wait_ge(S["f_oT"], upto(g, "f_oT", (l + 1) * FUNITS // 2))
                    pe.wait_ge(*bank_free(("f_wo", l)))
                    t, full = bank_to_fill(("f_wo", l))
                    for p in range(FP):
                        m = mm(t[:, :], wt(f"fo{l}")[:, p * D:p * D + D], OT[:, p, :], start=(p == 0),
                               stop=(p == FP - 1))
                    m.then_inc(full, 1)

                def f_ln(l):
                    pe.wait_ge(S["shifted"], upto(g, "shifted", 2 * l + 2))
                    ln_sums(1 + l, h2)

                def f_mlp(l):
                    pe.wait_ge(S["f_affine"], upto(g, "f_affine", l + 1))
                    for c in range(HC):
                        for part in (1, 0):
                            pe.wait_ge(*bank_free(("w1", l, c, part)))
                            t, full = bank_to_fill(("w1", l, c, part))
                            a = part * HID + c * HCW
                            mm(t[0:HCN[c], :], wt(f"w1{l}")[:, a:a + HCN[c]], hn[:, :], start=True,
                               stop=True).then_inc(full, 1)
                    pe.wait_ge(*bank_free(("w2", l)))
                    t, full = bank_to_fill(("w2", l))
                    for c in range(HC):
                        pe.wait_ge(S["f_hidden"], upto(g, "f_hidden", l * HC + c + 1))
                        m = mm(t[:, :], wt(f"w2{l}", HCN[c])[:, c * D:c * D + D], hid[0:HCN[c], c, :],
                               start=(c == 0), stop=(c == HC - 1))
                    m.then_inc(full, 1)

                def a_proj():
                    pe.wait_ge(S["ln_done"], upto(g, "ln_done", 1))
                    pe.wait_ge(*bank_free("a_lat"))
                    t, full = bank_to_fill("a_lat")
                    mm(t[0:LATENT, :], wt("wl"), xn[:, :], start=True, stop=True).then_inc(full, 1)
                    pe.wait_ge(*bank_free(("a_proj", 0)))
                    t, full = bank_to_fill(("a_proj", 0))
                    mm(t[:, :], wt("wq"), xn[:, :], start=True, stop=True).then_inc(full, 1)

                def a_kv():
                    pe.wait_ge(S["latent"], upto(g, "latent", 1))
                    pe.wait_ge(*bank_free(("a_proj", 1)))
                    t, full = bank_to_fill(("a_proj", 1))
                    mm(t[:, :], wt("wk", LATENT), lat[0:LATENT, :], start=True, stop=True).then_inc(full, 1)
                    pe.wait_ge(*bank_free("a_v"))
                    t, full = bank_to_fill("a_v")
                    for j in range(NT):
                        m = mm(t[:, j * 128:j * 128 + 128], lat[:, j * 128:j * 128 + 128], wt("wv", LATENT + 1),
                               start=True, stop=True)
                    m.then_inc(full, 1)

                def a_max(s):
                    if s == 0:
                        pe.wait_ge(S["q_spread"], upto(g, "q_spread", PER["q_spread"]))
                        pe.wait_ge(S["k_spread"], upto(g, "k_spread", PER["k_spread"]))
                    for n in (2 * s, 2 * s + 1):
                        bb, h, p, lo = unit(n)
                        if n >= 2:
                            pe.wait_ge(S["neg_max"], upto(g, "neg_max", n - 1))
                        for qt in range(2):
                            q0 = bb * SEQ + qt * 128
                            m = mm(MAXB[n % 2][:, qt * SEQ:qt * SEQ + SEQ], QS[lo:lo + QROWS, p, q0:q0 + 128],
                                   KS[lo:lo + QROWS, p, bb * SEQ:bb * SEQ + SEQ], start=True, stop=True)
                        m.then_inc(S["max_filled"], 1)

                def a_maxT():
                    pe.wait_ge(S["neg_max"], upto(g, "neg_max", UNITS))
                    pe.wait_ge(*bank_free("maxT"))
                    t, full = bank_to_fill("maxT")
                    for j in range(NT):
                        m = pe.transpose(t[0:AH, j * 128:j * 128 + 128], nmax[:, j, :], ident)
                    m.then_inc(full, 1)

                def shifted_scores(n):
                    bb, h, p, lo = unit(n)
                    if n >= 2:
                        pe.wait_ge(S["a_exp"], upto(g, "a_exp", n - 1))
                    for c in range(2):
                        k0 = bb * SEQ + c * 128
                        m = mm(EXPB[n % 2][:, c * SEQ:c * SEQ + SEQ], KS[lo:lo + MROWS, p, k0:k0 + 128],
                               QS[lo:lo + MROWS, p, bb * SEQ:bb * SEQ + SEQ], start=True, stop=True)
                    m.then_inc(S["exp_filled"], 1)

                def probs_v(n):
                    bb, h, _, _ = unit(n)
                    r = n // 4
                    if n % 4 == 0 and r >= 2:
                        pe.wait_ge(S["a_heads"], upto(g, "a_heads", r - 1))
                    pe.wait_ge(S["a_exp"], upto(g, "a_exp", n + 1))
                    lo = 32 * (n % 4)
                    for c in range(2):
                        m = mm(MAXB[r % 2][lo:lo + 32, 0:SEQ], VA[:, 2 * bb + c, h * VW:h * VW + 32],
                               PT[:, n % NPT, c, :], start=(c == 0), stop=(c == 1))
                    m.then_inc(S["a_pv"], 1)

                def a_exp(s):
                    if s == 0:
                        pe.wait_ge(S["m_spread"], upto(g, "m_spread", PER["m_spread"]))
                        pe.wait_ge(S["a_v"], upto(g, "a_v", 1))
                    for n in (2 * s, 2 * s + 1):
                        if n < UNITS:
                            shifted_scores(n)
                        if 1 <= n <= UNITS:
                            probs_v(n - 1)
                    if s % 2 == 1 and s >= 3:
                        r = (s - 3) // 2
                        pe.wait_ge(S["a_heads"], upto(g, "a_heads", r + 1))
                        pe.wait_ge(*bank_free(("a_heads", r)))
                        t, full = bank_to_fill(("a_heads", r))
                        for qt in range(2):
                            m = pe.transpose(t[:, qt * 128:qt * 128 + 128], heads4[:, r % 2, qt * 128:qt * 128 + 128],
                                             ident)
                        m.then_inc(full, 1)

                def a_out():
                    pe.wait_ge(S["a_norm"], upto(g, "a_norm", GROUPS))
                    pe.wait_ge(*bank_free("a_oT"))
                    t, full = bank_to_fill("a_oT")
                    for j in range(NT):
                        m = pe.transpose(t[:, j * 128:j * 128 + 128],
                                         AN[:, j, :, :].rearrange("p h d -> p (h d)"), ident)
                    m.then_inc(full, 1)
                    pe.wait_ge(S["a_oT"], upto(g, "a_oT", 1))
                    pe.wait_ge(*bank_free("a_out"))
                    t, full = bank_to_fill("a_out")
                    mm(t[:, :], wt("wo"), aoT, start=True, stop=True).then_inc(full, 1)

                inp = wt("inp")

                def c_ln():
                    pe.wait_ge(S["x1"], upto(gc, "x1", 1))
                    pe.wait_ge(*bank_free("c_mean"))
                    t, full = bank_to_fill("c_mean")
                    mm(t[:, :], wt("mean"), x1T[:, :], start=True, stop=True).then_inc(full, 1)
                    pe.wait_ge(S["c_squared"], upto(gc, "c_squared", 1))
                    pe.wait_ge(*bank_free("c_var"))
                    t, full = bank_to_fill("c_var")
                    mm(t[:, :], wt("mean"), csqr[:, :], start=True, stop=True).then_inc(full, 1)

                def c_dt():
                    pe.wait_ge(S["c_xn"], upto(gc, "c_xn", 1))
                    pe.wait_ge(*bank_free("m_dt"))
                    t, full = bank_to_fill("m_dt")
                    for j in range(NT):
                        m = mm(t[:, j * MH:j * MH + MH], cxn[:, j * 128:j * 128 + 128], inp[:, 2 * DI + 2 * NS:],
                               start=True, stop=True)
                    m.then_inc(full, 1)
                    pe.wait_ge(S["pool_rows"], upto(gc, "pool_rows", NB))
                    pe.wait_ge(*bank_free("logits"))
                    t, full = bank_to_fill("logits")
                    for bb in range(NB):
                        m = mm(t[:, bb * NE:bb * NE + NE], poolb[:, bb, :], wt("gw"), start=True, stop=True)
                    m.then_inc(full, 1)

                def c_conv(half):
                    for j in range(2 * half, 2 * half + 2):
                        pe.wait_ge(*bank_free(("m_xbc", j)))
                        t, full = bank_to_fill(("m_xbc", j))
                        mm(t[:, :], inp[:, DI + j * 128:DI + j * 128 + 128], cxn[:, :], start=True,
                           stop=True).then_inc(full, 1)

                def c_z():
                    for j in range(2):
                        pe.wait_ge(*bank_free(("m_z", j)))
                        t, full = bank_to_fill(("m_z", j))
                        mm(t[:, :], inp[:, j * 128:j * 128 + 128], cxn[:, :], start=True, stop=True).then_inc(full, 1)

                def c_rows():
                    pe.wait_ge(S["dA"], upto(gc, "dA", 1))
                    pe.wait_ge(*bank_free("dAT"))
                    t, full = bank_to_fill("dAT")
                    pe.sem_inc(spacer, 1)
                    for j in range(NT):
                        m = pe.transpose(t[0:MH, j * 128:j * 128 + 128], dt_dA[:, j, :], ident)
                    m.then_inc(full, 1)
                    pe.wait_ge(S["conv_silu"], upto(gc, "conv_silu", XBC))
                    for j in range(NT):
                        pe.wait_ge(*bank_free(("m_xt", j)))
                        t, full = bank_to_fill(("m_xt", j))
                        for c in range(2):
                            m = pe.transpose(t[:, c * 128:c * 128 + 128], cs[:, c, j * 128:j * 128 + 128], ident)
                        m.then_inc(full, 1)
                    for bb in range(NB):
                        t0 = bb * SEQ
                        pe.wait_ge(*bank_free(("m_cb", bb)))
                        t, full = bank_to_fill(("m_cb", bb))
                        mm(t[:, 0:256], cs[:, 2, t0:t0 + 128], cs[:, 3, t0:t0 + 256], start=True, stop=True)
                        mm(t[:, 256:384], cs[:, 2, t0 + 128:t0 + 256], cs[:, 3, t0 + 128:t0 + 256], start=True,
                           stop=True).then_inc(full, 1)

                def c_head(n):
                    bb, h = n // MH, n % MH
                    if n == 0:
                        pe.wait_ge(S["dA_rows"], upto(gc, "dA_rows", 1))
                        pe.wait_ge(S["xdt"], upto(gc, "xdt", NT))
                    pe.wait_ge(*bank_free(("m_dA", n)))
                    t, full = bank_to_fill(("m_dA", n))
                    mm(t[:, 0:SEQ], ident[0:MH, h:h + 1].to_broadcast([MH, 128]),
                       dA_rows[:, bb * SEQ:bb * SEQ + SEQ], start=True, stop=True).then_inc(full, 1)
                    if h == 0 and bb > 0:
                        pe.wait_ge(S["y_skip"], upto(gc, "y_skip", bb))
                    pe.wait_ge(S["weights"], upto(gc, "weights", n + 1))
                    lo, j = 64 * (h % 2), h // 2
                    o = YB[lo:lo + 64, j * SEQ:j * SEQ + SEQ]
                    mm(o, xd[:, 2 * bb, h, :], wgt[:, n % 2, 0:256], start=True, stop=False)
                    mm(o[:, 128:256], xd[:, 2 * bb + 1, h, :], wgt[:, n % 2, 256:384], start=False,
                       stop=True).then_inc(S["weights_used"], 1)

                def c_norm():
                    pe.wait_ge(S["y_squared"], upto(gc, "y_squared", 1))
                    pe.wait_ge(*bank_free("m_ss"))
                    t, full = bank_to_fill("m_ss")
                    for j in range(2):
                        m = mm(t[:, :], wt("mean"), ysq[:, j, :], start=(j == 0), stop=(j == 1))
                    m.then_inc(full, 1)
                    pe.wait_ge(*bank_free("m_out"))
                    t, full = bank_to_fill("m_out")
                    for j in range(2):
                        m = mm(t[:, :], outp[:, j, :], ym[:, j, :, :].rearrange("p b t -> p (b t)"),
                               start=(j == 0), stop=(j == 1))
                    m.then_inc(full, 1)

                def c_expert(half):
                    for e in range(half * NE // 2, (half + 1) * NE // 2):
                        pe.wait_ge(*bank_free(("expert", e)))
                        t, full = bank_to_fill(("expert", e))
                        mm(t[:, :], wt("ew")[:, e * D:e * D + D], cxn[:, :], start=True, stop=True).then_inc(full, 1)

                def c_end():
                    pe.wait_ge(S["x2"], upto(gc, "x2", 1))
                    pe.wait_ge(*bank_free("outT"))
                    t, full = bank_to_fill("outT")
                    for j in range(NT):
                        m = pe.transpose(t[:, j * 128:j * 128 + 128], x2T[:, j * 128:j * 128 + 128], ident)
                    m.then_inc(full, 1)

                return {"f_ln0": f_ln0, "f_proj": f_proj, "f_norms": f_norms, "f_v": f_v, "f_att": f_att, "f_wo": f_wo,
                        "f_ln": f_ln, "f_mlp": f_mlp, "a_proj": a_proj, "a_kv": a_kv, "a_max": a_max,
                        "a_maxT": a_maxT, "a_exp": a_exp, "a_out": a_out, "c_ln": c_ln, "c_dt": c_dt,
                        "c_conv": c_conv, "c_z": c_z, "c_rows": c_rows, "c_head": c_head, "c_norm": c_norm,
                        "c_expert": c_expert, "c_end": c_end}

            run_trips(pe, "pe_trip", steps)
            assert [len(p) for p in work_place] == [FA_TILES, FA_TILES + C_TILES, C_TILES], \
                [len(p) for p in work_place]

        @block.scalar
        def _(act):
            act.wait_ge(consts, CONSTS)
            act.wait_ge(weights_in[len(spans) - 1], 16)
            act.preload_act_table_set("natural_log_exp_and_others")
            A = act.activation
            A(neg_a, neg_a, ACT.Exp).then_inc(setup, 1)
            loaded = [None]

            def steps(g, gc):
                loaded[0] = None

                def log_exp():
                    if loaded[0] != "log_exp":
                        act.sem_inc(spacer, 1)
                        act.preload_act_table_set("natural_log_exp_and_others")
                        loaded[0] = "log_exp"

                def table_of(f):
                    if loaded[0] != f:
                        act.sem_inc(spacer, 1)
                        act.preload_act_table(f)
                        loaded[0] = f

                def ln_rest(n):
                    act.wait_ge(S["ln_centered"], upto(g, "ln_centered", n + 1))
                    A(sqr[:, :], cen[:, :], ACT.Square).then_inc(S["ln_squared"], 1)
                    act.wait_ge(*bank_filled(("var", n)))
                    t, free = bank_to_read(("var", n))
                    A(rst[:, :], t[:, :], ACT.Ln, bias=EPS).then_inc(S["ln_log"], 1)
                    act.wait_ge(S["ln_log"], upto(g, "ln_log", n + 1))
                    act.sem_inc(free, 1)
                    A(rst[:, :], rst[:, :], ACT.Exp, scale=-0.5).then_inc(S["ln_rstd"], 1)

                def f_ln0():
                    log_exp()
                    act.wait_ge(*bank_filled("xT"))
                    t, free = bank_to_read("xT")
                    A(xT[:, :], t[:, :], ACT.Identity).then_inc(S["xT"], 1)
                    act.wait_ge(S["xT"], upto(g, "xT", 1))
                    act.sem_inc(free, 1)
                    ln_rest(0)

                def k_rnorm(l, p):
                    k = l * FP + p
                    act.wait_ge(S["k_norm2"], upto(g, "k_norm2", k + 1))
                    A(kn[:, p % 2, :], kn[:, p % 2, :], ACT.Ln, scale=NORM_SHIFT).then_inc(S["k_nlog"], 1)
                    act.wait_ge(S["k_nlog"], upto(g, "k_nlog", k + 1))
                    A(kn[:, p % 2, :], kn[:, p % 2, :], ACT.Exp, scale=-0.5, bias=HALF_SHIFT)\
                        .then_inc(S["k_rnorm"], 1)

                def f_proj(l, p):
                    log_exp()
                    k = l * FP + p
                    act.wait_ge(*bank_filled(("fq", l, p)))
                    t, free = bank_to_read(("fq", l, p))
                    act.wait_ge(S["q_cos"], upto(g, "q_cos", k + 1))
                    A(sqq[:, p, :], t[:, :], ACT.Square).then_inc(S["q_squared"], 1)
                    act.wait_ge(S["q_squared"], upto(g, "q_squared", k + 1))
                    act.sem_inc(free, 1)
                    act.wait_ge(*bank_filled(("fk", l, p)))
                    t, free = bank_to_read(("fk", l, p))
                    act.wait_ge(S["k_cos"], upto(g, "k_cos", k + 1))
                    A(sqk[:, p % 2, :], t[:, :], ACT.Square).then_inc(S["k_squared"], 1)
                    act.wait_ge(S["k_squared"], upto(g, "k_squared", k + 1))
                    act.sem_inc(free, 1)
                    if p > 0:
                        k_rnorm(l, p - 1)

                def f_norms(l):
                    log_exp()
                    k_rnorm(l, FP - 1)
                    act.wait_ge(*bank_filled(("q_normT", l)))
                    t, free = bank_to_read(("q_normT", l))
                    q2 = qn[:, :, :].rearrange("p t h -> p (t h)")
                    A(q2, t[:, 0:NT * FH], ACT.Ln, scale=NORM_SHIFT).then_inc(S["q_nlog"], 1)
                    act.wait_ge(S["q_nlog"], upto(g, "q_nlog", l + 1))
                    act.sem_inc(free, 1)
                    A(q2, q2, ACT.Exp, scale=-0.5, bias=HALF_SHIFT8).then_inc(S["q_rnorm"], 1)

                def f_v(l, half):
                    k = l * (NT + NB) + 3 * half
                    for j in range(2):
                        act.wait_ge(*bank_filled(("f_v", l, 2 * half + j)))
                        t, free = bank_to_read(("f_v", l, 2 * half + j))
                        A(V[:, 2 * half + j, :], t[:, :], ACT.Identity).then_inc(S["f_v"], 1)
                        act.wait_ge(S["f_v"], upto(g, "f_v", k + j + 1))
                        act.sem_inc(free, 1)
                    act.wait_ge(*bank_filled(("f_vh", l, half)))
                    t, free = bank_to_read(("f_vh", l, half))
                    A(VH[:, half, :], t[0:64, :], ACT.Identity).then_inc(S["f_v"], 1)
                    act.wait_ge(S["f_v"], upto(g, "f_v", k + 3))
                    act.sem_inc(free, 1)

                def f_exps(l, n):
                    log_exp()
                    act.wait_ge(S["f_negmax"], upto(g, "f_negmax", l * FUNITS + n + 1))
                    P = MS[:, n % NMS, :]
                    A(P[:, 0:128], P[:, 0:128], ACT.Exp, bias=fnm[:, n, 0:1], accum_out=fsum[:, n, 0:1])
                    A(P[:, 128:SW], P[:, 128:SW], ACT.Exp, bias=fnm[:, n, 1:2],
                      accum_out=fsum[:, n, 1:2]).then_inc(S["f_exp"], 1)

                def f_copy_pT(l, n):
                    act.wait_ge(*bank_filled(("f_pT", l, n)))
                    t, free = bank_to_read(("f_pT", l, n))
                    A(PP[:, n % NPP, :], t[:, 0:384], ACT.Identity).then_inc(S["f_probsT"], 1)
                    act.wait_ge(S["f_probsT"], upto(g, "f_probsT", l * FUNITS + n + 1))
                    act.sem_inc(free, 1)

                def f_att(l, s):
                    if 3 <= s:
                        n = s - 3
                        bb, p = n // FP, n % FP
                        if 2 <= s < FUNITS // 2 + 2:
                            f_copy_pT(l, 2 * s - 4)
                            f_copy_pT(l, 2 * s - 3)
                        act.wait_ge(*bank_filled(("f_o", l, n)))
                        t, free = bank_to_read(("f_o", l, n))
                        A(OT[:, p, bb * SEQ:bb * SEQ + SEQ], t[:, 0:SEQ], ACT.Identity).then_inc(S["f_oT"], 1)
                        act.wait_ge(S["f_oT"], upto(g, "f_oT", l * FUNITS // 2 + n + 1))
                        act.sem_inc(free, 1)
                    elif s == 2:
                        f_copy_pT(l, 0)
                        f_copy_pT(l, 1)
                    if s < FUNITS // 2:
                        f_exps(l, 2 * s)
                        f_exps(l, 2 * s + 1)

                def f_ln(l):
                    log_exp()
                    ln_rest(1 + l)

                def f_mlp(l):
                    table_of(ACT.Gelu)
                    for c in range(HC):
                        r = HCN[c]
                        act.wait_ge(*bank_filled(("w1", l, c, 1)))
                        t, free = bank_to_read(("w1", l, c, 1))
                        A(ge[0:r, c, :], t[0:r, :], ACT.Gelu, bias=col(f"b1{l}", HC + c, r)).then_inc(S["f_gelu"], 1)
                        act.wait_ge(S["f_gelu"], upto(g, "f_gelu", l * HC + c + 1))
                        act.sem_inc(free, 1)

                def f_end():
                    table_of(ACT.Silu)
                    act.wait_ge(S["f_res2"], upto(g, "f_res2", DEPTH))
                    A(gate_f, yT[:, :], ACT.Silu).then_inc(S["f_silu"], 1)

                def a_proj():
                    act.wait_ge(*bank_filled("a_lat"))
                    t, free = bank_to_read("a_lat")
                    A(lat[0:LATENT, :], t[0:LATENT, :], ACT.Identity, bias=col("bl", 0, LATENT))\
                        .then_inc(S["latent"], 1)
                    act.wait_ge(S["latent"], upto(g, "latent", 1))
                    act.sem_inc(free, 1)

                def a_kv():
                    if gc is not None:
                        act.wait_ge(S["out_stored"], upto(gc, "out_stored", 16))
                    for i in range(2):
                        act.wait_ge(S["a_q32"], upto(g, "a_q32", i + 1))
                        A(parts[:, i, 0, :], f32op[:, i, :], ACT.Identity).then_inc(S["a_part0"], 1)
                        act.wait_ge(S["a_rest1"], upto(g, "a_rest1", i + 1))
                        A(parts[:, i, 1, :], rest[:, i, :], ACT.Identity).then_inc(S["a_part1"], 1)

                def a_maxT():
                    act.wait_ge(*bank_filled("maxT"))
                    t, free = bank_to_read("maxT")
                    A(mx, t[0:AH, :], ACT.Identity).then_inc(S["m_rows"], 1)
                    act.wait_ge(S["m_rows"], upto(g, "m_rows", 1))
                    act.sem_inc(free, 1)
                    A(mparts[:, 0, :], mx, ACT.Identity).then_inc(S["m_part0"], 1)
                    act.wait_ge(S["m_rest1"], upto(g, "m_rest1", 1))
                    A(mparts[:, 1, :], mrest, ACT.Identity).then_inc(S["m_part1"], 1)

                def a_exp(s):
                    for n in (2 * s, 2 * s + 1):
                        if n < UNITS:
                            log_exp()
                            act.wait_ge(S["exp_filled"], upto(g, "exp_filled", n + 1))
                            if n >= NPT:
                                act.wait_ge(S["a_pv"], upto(g, "a_pv", n - NPT + 1))
                            A(PT[:, n % NPT, :, :].rearrange("p c q -> p (c q)"), EXPB[n % 2][:, :], ACT.Exp,
                              scale=ADH ** -0.5).then_inc(S["a_exp"], 1)

                def a_out():
                    act.wait_ge(*bank_filled("a_oT"))
                    t, free = bank_to_read("a_oT")
                    A(aoT, t[:, :], ACT.Identity).then_inc(S["a_oT"], 1)
                    act.wait_ge(S["a_oT"], upto(g, "a_oT", 1))
                    act.sem_inc(free, 1)
                    act.wait_ge(*bank_filled("a_out"))
                    t, free = bank_to_read("a_out")
                    A(s_out[:, :], t[:, :], ACT.Identity, bias=col("bo")).then_inc(S["attn_out"], 1)
                    act.wait_ge(S["attn_out"], upto(g, "attn_out", 1))
                    act.sem_inc(free, 1)

                def c_ln():
                    log_exp()
                    act.wait_ge(S["c_centered"], upto(gc, "c_centered", 1))
                    A(csqr[:, :], ccen[:, :], ACT.Square).then_inc(S["c_squared"], 1)
                    act.wait_ge(*bank_filled("c_var"))
                    t, free = bank_to_read("c_var")
                    A(crst[:, :], t[:, :], ACT.Ln, bias=EPS).then_inc(S["c_log"], 1)
                    act.wait_ge(S["c_log"], upto(gc, "c_log", 1))
                    act.sem_inc(free, 1)
                    A(crst[:, :], crst[:, :], ACT.Exp, scale=-0.5).then_inc(S["c_rstd"], 1)

                def c_dt():
                    log_exp()
                    act.wait_ge(S["dt_raw"], upto(gc, "dt_raw", 1))
                    A(dt_e, dt_raw, ACT.Abs).then_inc(S["dt_abs"], 1)
                    act.wait_ge(S["dt_abs"], upto(gc, "dt_abs", 1))
                    A(dt_e, dt_e, ACT.Exp, scale=-1.0).then_inc(S["dt_exp"], 1)
                    for bb in range(NB):
                        act.wait_ge(S["g_negmax"], upto(gc, "g_negmax", bb + 1))
                        A(gex[:, bb, :], lg_[:, bb, :], ACT.Exp, bias=gsm[:, bb, 0:1]).then_inc(S["g_exp"], 1)

                def c_conv(half):
                    for j in range(2 * half, 2 * half + 2):
                        act.wait_ge(*bank_filled(("m_xbc", j)))
                        t, free = bank_to_read(("m_xbc", j))
                        A(cin[:, j, :, TAPS - 1:], t[:, :].rearrange("p (b t) -> p b t", b=NB), ACT.Identity)\
                            .then_inc(S["conv_in"], 1)
                        act.wait_ge(S["conv_in"], upto(gc, "conv_in", j + 1))
                        act.sem_inc(free, 1)
                    if half == 0:
                        log_exp()
                        act.wait_ge(S["dt_a"], upto(gc, "dt_a", 1))
                        A(dt_dA, dt_dA, ACT.Exp).then_inc(S["dA"], 1)

                def c_z():
                    table_of(ACT.Silu)
                    for j in range(2):
                        act.wait_ge(*bank_filled(("m_z", j)))
                        t, free = bank_to_read(("m_z", j))
                        A(zs[:, j, :], t[:, :], ACT.Silu).then_inc(S["z_silu"], 1)
                        act.wait_ge(S["z_silu"], upto(gc, "z_silu", j + 1))
                        act.sem_inc(free, 1)
                    for j in range(XBC):
                        act.wait_ge(S["conv"], upto(gc, "conv", TAPS * (j + 1)))
                        A(cs[:, j, :], cs[:, j, :], ACT.Silu).then_inc(S["conv_silu"], 1)

                def c_rows():
                    act.wait_ge(*bank_filled("dAT"))
                    t, free = bank_to_read("dAT")
                    A(dA_rows, t[0:MH, :], ACT.Identity).then_inc(S["dA_rows"], 1)
                    act.wait_ge(S["dA_rows"], upto(gc, "dA_rows", 1))
                    act.sem_inc(free, 1)
                    for bb in range(NB):
                        act.wait_ge(*bank_filled(("m_cb", bb)))
                        t, free = bank_to_read(("m_cb", bb))
                        A(cbp[:, bb, :], t[:, 0:384], ACT.Identity).then_inc(S["cb_prod"], 1)
                        act.wait_ge(S["cb_prod"], upto(gc, "cb_prod", bb + 1))
                        act.sem_inc(free, 1)

                def c_norm():
                    log_exp()
                    act.wait_ge(S["y_gated"], upto(gc, "y_gated", NB))
                    A(ysq[:, :, :], AO[:, :, :], ACT.Square).then_inc(S["y_squared"], 1)
                    act.wait_ge(*bank_filled("m_ss"))
                    t, free = bank_to_read("m_ss")
                    A(crst[:, :], t[:, :], ACT.Ln, bias=EPS, scale=0.5).then_inc(S["y_log"], 1)
                    act.wait_ge(S["y_log"], upto(gc, "y_log", 1))
                    act.sem_inc(free, 1)
                    A(crst[:, :], crst[:, :], ACT.Exp, scale=-0.5).then_inc(S["y_rstd"], 1)

                def c_expert(half):
                    table_of(ACT.Gelu)
                    for e in range(half * NE // 2, (half + 1) * NE // 2):
                        if e >= 2:
                            act.wait_ge(S["mixed"], upto(gc, "mixed", e - 1))
                        act.wait_ge(*bank_filled(("expert", e)))
                        t, free = bank_to_read(("expert", e))
                        A(eg[:, e % 2, :], t[:, :], ACT.Gelu, bias=col("eb", e)).then_inc(S["expert"], 1)
                        act.wait_ge(S["expert"], upto(gc, "expert", e + 1))
                        act.sem_inc(free, 1)

                def c_end():
                    table_of(ACT.Silu)
                    act.wait_ge(S["mixed"], upto(gc, "mixed", NE))
                    A(gate_c, gate_c, ACT.Silu).then_inc(S["c_silu"], 1)
                    act.wait_ge(*bank_filled("outT"))
                    t, free = bank_to_read("outT")
                    A(out_rows[:, :, :].rearrange("p t d -> p (t d)"), t[:, :], ACT.Identity)\
                        .then_inc(S["out_rows"], 1)
                    act.wait_ge(S["out_rows"], upto(gc, "out_rows", 1))
                    act.sem_inc(free, 1)

                return {"f_ln0": f_ln0, "f_proj": f_proj, "f_norms": f_norms, "f_v": f_v, "f_att": f_att,
                        "f_ln": f_ln, "f_mlp": f_mlp, "f_end": f_end, "a_proj": a_proj, "a_kv": a_kv,
                        "a_maxT": a_maxT, "a_exp": a_exp, "a_out": a_out, "c_ln": c_ln, "c_dt": c_dt,
                        "c_conv": c_conv, "c_z": c_z, "c_rows": c_rows, "c_norm": c_norm,
                        "c_expert": c_expert, "c_end": c_end}

            run_trips(act, "act_trip", steps)

        @block.vector
        def _(dve):
            for i in range(len(spans)):
                dve.wait_ge(weights_in[i], 16)
            dve.wait_ge(tables_in, 16)
            for l in range(DEPTH):
                for k, scale in enumerate(("qs", "qsr", "ks", "ksr")):
                    dve.tensor_scalar(rope[:, l, k, :], rope0[:, k, :], col(scale, l), None, ALU.mult).then_inc(setup, 1)
            for j in range(2):
                dve.tensor_scalar(outp[:, j, :], outp[:, j, :], col("nw", j), None, ALU.mult)\
                    .then_inc(setup, 1)
            dve.wait_ge(setup, SETUP - 1)
            dve.tensor_scalar(neg_a, neg_a, -1.0, None, ALU.mult).then_inc(setup, 1)
            dve.wait_ge(setup, SETUP)
            dve.wait_ge(consts, CONSTS)
            for b in range(NBANK):
                dve.sem_inc(work_read[b], 1)
            TS, TT, STT = dve.tensor_scalar, dve.tensor_tensor, dve.scalar_tensor_tensor

            def rows2(t):
                return t.rearrange("p (b t) -> p b t", b=NB)

            def table(l, k):
                return rope[:, l, k, :].unsqueeze(1).to_broadcast([128, NB, SEQ])

            def steps(g, gc):
                def layer_norm(n, src, dst):
                    dve.wait_ge(*bank_filled(("mean", n)))
                    t, free = bank_to_read(("mean", n))
                    TT(cen[:, :], src, t[:, :], ALU.subtract).then_inc(S["ln_centered"], 1)
                    dve.wait_ge(S["ln_centered"], upto(g, "ln_centered", n + 1))
                    dve.sem_inc(free, 1)
                    dve.wait_ge(S["ln_rstd"], upto(g, "ln_rstd", n + 1))
                    TT(dst, cen[:, :], rst[:, :], ALU.mult).then_inc(S["ln_done"], 1)
                    dve.wait_ge(S["ln_done"], upto(g, "ln_done", n + 1))

                def shift(k, src):
                    s3 = rows2(src)
                    dve.tensor_copy(hT[0:64, :, :], s3[0:64, :, :])
                    dve.tensor_copy(hT[64:128, :, 1:], s3[64:128, :, 0:SEQ - 1]).then_inc(S["shifted"], 1)
                    dve.wait_ge(S["shifted"], upto(g, "shifted", k))

                def f_ln0():
                    dve.wait_ge(S["xT"], upto(g, "xT", 1))
                    layer_norm(0, xT[:, :], xn[:, :])
                    shift(1, xn[:, :])

                def k_squares(l, p):
                    k = l * FP + p
                    if k >= 2:
                        dve.wait_ge(S["k_final"], upto(g, "k_final", k - 1))
                    dve.wait_ge(*bank_filled(("k_norm", l, p)))
                    t, free = bank_to_read(("k_norm", l, p))
                    TS(kn[:, p % 2, :], t[:, :], 1e-24, None, ALU.max).then_inc(S["k_norm2"], 1)
                    dve.wait_ge(S["k_norm2"], upto(g, "k_norm2", l * FP + p + 1))
                    dve.sem_inc(free, 1)

                def k_final(l, p):
                    k = l * FP + p
                    dve.wait_ge(S["k_rnorm"], upto(g, "k_rnorm", k + 1))
                    dve.wait_ge(S["k_rot"], upto(g, "k_rot", k + 1))
                    TT(KR[:, p, :], KR[:, p, :], kn[:, p % 2, :], ALU.mult).then_inc(S["k_final"], 1)

                def f_proj(l, p):
                    k = l * FP + p
                    for name, c, ca, sa, rot, R in (("fq", 0, "q_cos", "q_sin", "q_rot", QR),
                                                    ("fk", 2, "k_cos", "k_sin", "k_rot", KR)):
                        b = 0 if c == 0 else 1
                        dve.wait_ge(*bank_filled((name, l, p)))
                        t, free = bank_to_read((name, l, p))
                        TT(rows2(R[:, p, :]), rows2(t[:, :]), table(l, c), ALU.mult).then_inc(S[ca], 1)
                        dve.wait_ge(*bank_filled((name + "r", l, p)))
                        t, free = bank_to_read((name + "r", l, p))
                        if k > 0:
                            dve.wait_ge(S[rot], upto(g, rot, k))
                        TT(rows2(sinp[:, b, :]), rows2(t[:, :]), table(l, c + 1), ALU.mult).then_inc(S[sa], 1)
                        dve.wait_ge(S[sa], upto(g, sa, k + 1))
                        dve.sem_inc(free, 1)
                    if p > 0:
                        k_squares(l, p - 1)
                    if p > 1:
                        k_final(l, p - 2)

                def f_norms(l):
                    k_squares(l, FP - 1)
                    dve.wait_ge(*bank_filled(("q_norm", l)))
                    t, free = bank_to_read(("q_norm", l))
                    TS(qn2[:, :], t[0:FH, :], 1e-24, None, ALU.max).then_inc(S["q_norm2"], 1)
                    dve.wait_ge(S["q_norm2"], upto(g, "q_norm2", l + 1))
                    dve.sem_inc(free, 1)
                    k_final(l, FP - 2)

                def f_v(l, half):
                    if half == 0:
                        k_final(l, FP - 1)

                def masked(l, n):
                    bb, h, _, _ = funit(n)
                    t, free = bank_to_read(("f_s", l, n))
                    for u, a, e in ((0, 0, 128), (1, 128, SW)):
                        m = dve.tensor_tensor_reduce(MS[:, n % NMS, a:e], t[:, a:e], wt("band")[:, a:e],
                                                     qn[:, 2 * bb + u, h:h + 1], -3.0e38, ALU.add, ALU.max,
                                                     fmx[:, n, u:u + 1])
                    m.then_inc(S["f_masked"], 1)

                def f_att(l, s):
                    if s == 0:
                        dve.wait_ge(S["q_rnorm"], upto(g, "q_rnorm", l + 1))
                    if s < FUNITS // 2:
                        n = 2 * s
                        k = l * FUNITS + n
                        if n >= NMS:
                            dve.wait_ge(S["f_probsT"], upto(g, "f_probsT", k + 2 - NMS))
                        dve.wait_ge(*bank_filled(("f_s", l, n)))
                        dve.sem_inc(spacer, 1)
                        masked(l, n)
                        for j in (n, n + 1):
                            t, free = bank_to_read(("f_s", l, j))
                            dve.wait_ge(S["f_masked"], upto(g, "f_masked", l * FUNITS + j + 1))
                            dve.sem_inc(free, 1)
                            if j == n:
                                dve.wait_ge(*bank_filled(("f_s", l, n + 1)))
                            TS(fnm[:, j, :], fmx[:, j, :], -1.0, None, ALU.mult).then_inc(S["f_negmax"], 1)
                            if j == n:
                                masked(l, n + 1)
                    if 1 <= s < FUNITS // 2 + 1:
                        for j in (2 * s - 2, 2 * s - 1):
                            dve.wait_ge(S["f_exp"], upto(g, "f_exp", l * FUNITS + j + 1))
                            dve.reciprocal(frs[:, j, :], fsum[:, j, :]).then_inc(S["f_rsum"], 1)
                        for j in (2 * s - 2, 2 * s - 1):
                            dve.wait_ge(S["f_rsum"], upto(g, "f_rsum", l * FUNITS + j + 1))
                            P = MS[:, j % NMS, :]
                            TS(P[:, 0:128], P[:, 0:128], frs[:, j, 0:1], None, ALU.mult)
                            TS(P[:, 128:SW], P[:, 128:SW], frs[:, j, 1:2], None, ALU.mult).then_inc(S["f_probs"], 1)

                def f_wo(l):
                    src = xn if l == 0 else yT
                    dve.wait_ge(*bank_filled(("f_wo", l)))
                    t, free = bank_to_read(("f_wo", l))
                    TT(yT[:, :], t[:, :], src[:, :], ALU.add).then_inc(S["f_res1"], 1)
                    dve.wait_ge(S["f_res1"], upto(g, "f_res1", l + 1))
                    dve.sem_inc(free, 1)
                    shift(2 * l + 2, yT[:, :])

                def f_ln(l):
                    layer_norm(1 + l, hT[:, :, :].rearrange("p b t -> p (b t)"), hn[:, :])
                    TS(hn[:, :], hn[:, :], col(f"lg{l}"), col(f"lb{l}"), ALU.mult, ALU.add).then_inc(S["f_affine"], 1)

                def f_mlp(l):
                    for c in range(HC):
                        r = HCN[c]
                        dve.wait_ge(S["f_gelu"], upto(g, "f_gelu", l * HC + c + 1))
                        dve.wait_ge(*bank_filled(("w1", l, c, 0)))
                        t, free = bank_to_read(("w1", l, c, 0))
                        STT(out=hid[0:r, c, :], in0=t[0:r, :], scalar=col(f"b1{l}", c, r), in1=ge[0:r, c, :],
                            op0=ALU.add, op1=ALU.mult).then_inc(S["f_hidden"], 1)
                        dve.wait_ge(S["f_hidden"], upto(g, "f_hidden", l * HC + c + 1))
                        dve.sem_inc(free, 1)
                    dve.wait_ge(*bank_filled(("w2", l)))
                    t, free = bank_to_read(("w2", l))
                    STT(out=yT[:, :], in0=t[:, :], scalar=col(f"b2{l}"), in1=yT[:, :], op0=ALU.add,
                        op1=ALU.add).then_inc(S["f_res2"], 1)
                    dve.wait_ge(S["f_res2"], upto(g, "f_res2", l + 1))
                    dve.sem_inc(free, 1)
                    if l + 1 < DEPTH:
                        shift(2 * l + 3, yT[:, :])

                def f_end():
                    dve.wait_ge(S["f_silu"], upto(g, "f_silu", 1))
                    dve.wait_ge(S["attn_out"], upto(g, "attn_out", 1))
                    TT(s_out[:, :], s_out[:, :], gate_f, ALU.mult).then_inc(S["f_gated"], 1)
                    dve.wait_ge(S["f_gated"], upto(g, "f_gated", 1))
                    TT(x1T[:, :], s_out[:, :], xT[:, :], ALU.add).then_inc(S["x1"], 1)
                    dve.wait_ge(S["x1"], upto(g, "x1", 1))

                def split(i):
                    dve.wait_ge(*bank_filled(("a_proj", i)))
                    t, free = bank_to_read(("a_proj", i))
                    TS(f32op[:, i, :], t[:, :], col(("bq", "bk")[i]), None, ALU.add).then_inc(S["a_q32"], 1)
                    dve.wait_ge(S["a_q32"], upto(g, "a_q32", i + 1))
                    dve.sem_inc(free, 1)

                def split_rest(i):
                    dve.wait_ge(S["a_part0"], upto(g, "a_part0", i + 1))
                    TT(rest[:, i, :], f32op[:, i, :], parts[:, i, 0, :], ALU.subtract).then_inc(S["a_rest1"], 1)
                    dve.wait_ge(S["a_part1"], upto(g, "a_part1", i + 1))
                    TT(parts[:, i, 2, :], rest[:, i, :], parts[:, i, 1, :], ALU.subtract).then_inc(S["a_part2"], 1)

                def a_proj():
                    split(0)

                def a_kv():
                    split(1)
                    dve.wait_ge(*bank_filled("a_v"))
                    t, free = bank_to_read("a_v")
                    dve.tensor_copy(VA[:, :, 0:AH * VW].rearrange("p t (h w) -> p t h w", h=AH)[:, :, :, 0:ADH],
                                    t[:, :].rearrange("p (t h d) -> p t h d", t=NT, h=AH)).then_inc(S["a_v"], 1)
                    split_rest(0)
                    split_rest(1)
                    dve.wait_ge(S["a_v"], upto(g, "a_v", 1))
                    dve.sem_inc(free, 1)

                def a_max(s):
                    for n in (2 * s, 2 * s + 1):
                        bb, h, _, _ = unit(n)
                        dve.wait_ge(S["max_filled"], upto(g, "max_filled", n + 1))
                        dve.tensor_reduce(nmax[:, 2 * bb:2 * bb + 2, (h % 2) * AP + h // 2],
                                          MAXB[n % 2][:, :].rearrange("p (a k) -> p a k", a=2), AXX, ALU.max,
                                          negate=True).then_inc(S["neg_max"], 1)

                def a_maxT():
                    dve.wait_ge(S["m_part0"], upto(g, "m_part0", 1))
                    TT(mrest, mx, mparts[:, 0, :], ALU.subtract).then_inc(S["m_rest1"], 1)
                    dve.wait_ge(S["m_part1"], upto(g, "m_part1", 1))
                    TT(mparts[:, 2, :], mrest, mparts[:, 1, :], ALU.subtract).then_inc(S["m_part2"], 1)

                def a_exp(s):
                    if s % 2 == 0 and 2 <= s <= 2 * GROUPS:
                        r = (s - 2) // 2
                        dve.wait_ge(S["a_pv"], upto(g, "a_pv", 4 * r + 4))
                        dve.tensor_copy(heads4[:, r % 2, :], MAXB[r % 2][:, 0:SEQ]).then_inc(S["a_heads"], 1)
                    if s % 2 == 1 and s >= 3:
                        r = (s - 3) // 2
                        bb, h0 = 4 * r // AH, 4 * r % AH
                        dve.wait_ge(*bank_filled(("a_heads", r)))
                        t, free = bank_to_read(("a_heads", r))
                        o = t[:, 0:256].rearrange("p (a h d) -> p a h d", a=2, h=4)
                        dve.reciprocal(arsum[:, r % 2, :, :], o[:, :, :, ADH]).then_inc(S["a_rsum"], 1)
                        dve.wait_ge(S["a_rsum"], upto(g, "a_rsum", r + 1))
                        TT(AN[:, 2 * bb:2 * bb + 2, h0:h0 + 4, :], o[:, :, :, 0:ADH],
                           arsum[:, r % 2, :, :].unsqueeze(3).to_broadcast([128, 2, 4, ADH]), ALU.mult)\
                            .then_inc(S["a_norm"], 1)
                        dve.wait_ge(S["a_norm"], upto(g, "a_norm", r + 1))
                        dve.sem_inc(free, 1)

                def c_ln():
                    dve.wait_ge(*bank_filled("c_mean"))
                    t, free = bank_to_read("c_mean")
                    TT(ccen[:, :], x1T[:, :], t[:, :], ALU.subtract).then_inc(S["c_centered"], 1)
                    dve.wait_ge(S["c_centered"], upto(gc, "c_centered", 1))
                    dve.sem_inc(free, 1)
                    dve.wait_ge(S["c_rstd"], upto(gc, "c_rstd", 1))
                    TT(cxn[:, :], ccen[:, :], crst[:, :], ALU.mult).then_inc(S["c_xn"], 1)

                def c_dt():
                    dve.wait_ge(*bank_filled("m_dt"))
                    t, free = bank_to_read("m_dt")
                    heads = [128, NT, MH]
                    TT(dt_raw, t[:, 0:NT * MH].rearrange("p (t h) -> p t h", t=NT),
                       wt("dtb").unsqueeze(1).to_broadcast(heads), ALU.add).then_inc(S["dt_raw"], 1)
                    dve.wait_ge(S["dt_raw"], upto(gc, "dt_raw", 1))
                    dve.sem_inc(free, 1)
                    dve.wait_ge(S["c_xn"], upto(gc, "c_xn", 1))
                    dve.tensor_reduce(pool[:, :], rows2(cxn[:, :]), AXX, ALU.add).then_inc(S["pooled"], 1)
                    dve.wait_ge(S["pooled"], upto(gc, "pooled", 1))
                    for bb in range(NB):
                        TS(poolb[:, bb, :], pool[:, bb:bb + 1].to_broadcast([128, 128]), 1.0 / SEQ, None, ALU.mult)\
                            .then_inc(S["pool_rows"], 1)
                    dve.wait_ge(*bank_filled("logits"))
                    t, free = bank_to_read("logits")
                    TT(lg_[:, :, :], t[:, 0:NB * NE].rearrange("p (b e) -> p b e", b=NB),
                       wt("gb").unsqueeze(1).to_broadcast([128, NB, NE]), ALU.add).then_inc(S["logits"], 1)
                    dve.wait_ge(S["logits"], upto(gc, "logits", 1))
                    dve.sem_inc(free, 1)
                    for bb in range(NB):
                        dve.max(top[:, bb, :], lg_[:, bb, :]).then_inc(S["top"], 1)
                    for bb in range(NB):
                        dve.wait_ge(S["top"], upto(gc, "top", bb + 1))
                        TS(gsm[:, bb, 0:1], top[:, bb, 0:1], -1.0, None, ALU.mult).then_inc(S["g_negmax"], 1)
                        TS(gkp[:, bb, :], lg_[:, bb, :], top[:, bb, 1:2], None, ALU.is_ge).then_inc(S["g_keep"], 1)

                def softplus():
                    TS(dt_pos, dt_raw, 0.0, None, ALU.max)
                    dve.wait_ge(S["dt_exp"], upto(gc, "dt_exp", 1))
                    TS(dt_w, dt_e, 2.0, None, ALU.add).then_inc(S["dt_step"], 1)
                    dve.wait_ge(S["dt_step"], upto(gc, "dt_step", 1))
                    dve.reciprocal(dt_w, dt_w).then_inc(S["dt_step"], 1)
                    dve.wait_ge(S["dt_step"], upto(gc, "dt_step", 2))
                    TT(dt_w, dt_w, dt_e, ALU.mult).then_inc(S["dt_step"], 1)
                    dve.wait_ge(S["dt_step"], upto(gc, "dt_step", 3))
                    TT(dt_w2, dt_w, dt_w, ALU.mult).then_inc(S["dt_step"], 1)
                    for k, c in enumerate(SERIES):
                        dve.wait_ge(S["dt_step"], upto(gc, "dt_step", 4 + k))
                        if k == 0:
                            TS(dt_p, dt_w2, c, None, ALU.mult).then_inc(S["dt_step"], 1)
                        else:
                            STT(out=dt_p, in0=dt_p, scalar=c, in1=dt_w2, op0=ALU.add, op1=ALU.mult)\
                                .then_inc(S["dt_step"], 1)
                    dve.wait_ge(S["dt_step"], upto(gc, "dt_step", 4 + len(SERIES)))
                    STT(out=dt_p, in0=dt_p, scalar=1.0, in1=dt_w, op0=ALU.add, op1=ALU.mult).then_inc(S["dt_step"], 1)
                    dve.wait_ge(S["dt_step"], upto(gc, "dt_step", 5 + len(SERIES)))
                    STT(out=dt_, in0=dt_p, scalar=2.0, in1=dt_pos, op0=ALU.mult, op1=ALU.add).then_inc(S["dt"], 1)
                    dve.wait_ge(S["dt"], upto(gc, "dt", 1))
                    TT(dt_dA, dt_, neg_a.unsqueeze(1).to_broadcast([128, NT, MH]), ALU.mult).then_inc(S["dt_a"], 1)

                def gates():
                    for bb in range(NB):
                        dve.wait_ge(S["g_exp"], upto(gc, "g_exp", bb + 1))
                        dve.wait_ge(S["g_keep"], upto(gc, "g_keep", bb + 1))
                        dve.tensor_tensor_reduce(gkp[:, bb, :], gkp[:, bb, :], gex[:, bb, :], 1.0, 0.0, ALU.mult,
                                                 ALU.add, gsm[:, bb, 1:2]).then_inc(S["g_sum"], 1)
                    for bb in range(NB):
                        dve.wait_ge(S["g_sum"], upto(gc, "g_sum", bb + 1))
                        dve.reciprocal(gsm[:, bb, 2:3], gsm[:, bb, 1:2]).then_inc(S["g_rsum"], 1)
                    for bb in range(NB):
                        dve.wait_ge(S["g_rsum"], upto(gc, "g_rsum", bb + 1))
                        TS(gt[:, bb, :], gkp[:, bb, :], gsm[:, bb, 2:3], None, ALU.mult).then_inc(S["gates"], 1)

                def c_conv(half):
                    if half == 0:
                        softplus()
                        gates()
                    for j in range(2 * half, 2 * half + 2):
                        dve.wait_ge(S["conv_in"], upto(gc, "conv_in", j + 1))
                        for k in range(TAPS):
                            a = cin[:, j, :, k:k + SEQ]
                            if k == 0:
                                TS(cv[:, j, :, :], a, col("cw", j * TAPS), col("cb", j), ALU.mult, ALU.add)\
                                    .then_inc(S["conv"], 1)
                            else:
                                dve.wait_ge(S["conv"], upto(gc, "conv", j * TAPS + k))
                                STT(out=cv[:, j, :, :], in0=a, scalar=col("cw", j * TAPS + k), in1=cv[:, j, :, :],
                                    op0=ALU.mult, op1=ALU.add).then_inc(S["conv"], 1)

                def c_rows():
                    for j in range(NT):
                        dve.wait_ge(*bank_filled(("m_xt", j)))
                        t, free = bank_to_read(("m_xt", j))
                        TT(xd[:, j, :, :], t[:, 0:DI].rearrange("p (h d) -> p h d", h=MH),
                           dt_[:, j, :].unsqueeze(2).to_broadcast([128, MH, MDH]), ALU.mult).then_inc(S["xdt"], 1)
                        dve.wait_ge(S["xdt"], upto(gc, "xdt", j + 1))
                        dve.sem_inc(free, 1)

                def c_head(n):
                    bb, h = n // MH, n % MH
                    dve.wait_ge(S["cb_prod"], upto(gc, "cb_prod", bb + 1))
                    dve.wait_ge(*bank_filled(("m_dA", n)))
                    t, free = bank_to_read(("m_dA", n))
                    dve.tensor_tensor_scan(dec[:, n % 2, 0:256], t[:, 0:256], step, 0.0, ALU.mult, ALU.add)
                    dve.tensor_tensor_scan(dec[:, n % 2, 256:384], t[:, 128:256], ident, 0.0,
                                           ALU.mult, ALU.add).then_inc(S["decay"], 1)
                    dve.wait_ge(S["decay"], upto(gc, "decay", n + 1))
                    dve.sem_inc(free, 1)
                    if n >= 2:
                        dve.wait_ge(S["weights_used"], upto(gc, "weights_used", n - 1))
                    TT(wgt[:, n % 2, :], dec[:, n % 2, :], cbp[:, bb, :], ALU.mult).then_inc(S["weights"], 1)
                    if h < MH - 1:
                        return
                    dve.wait_ge(S["z_silu"], upto(gc, "z_silu", 2))
                    dve.wait_ge(S["weights_used"], upto(gc, "weights_used", n + 1))
                    for j in range(2):
                        m = STT(out=ym[:, j, bb, :], in0=rows2(cs[:, j, :])[:, bb, :], scalar=col("dsk", j),
                                in1=YB[:, j * SEQ:j * SEQ + SEQ], op0=ALU.mult, op1=ALU.add)
                    m.then_inc(S["y_skip"], 1)
                    dve.wait_ge(S["y_skip"], upto(gc, "y_skip", bb + 1))
                    TT(ym[:, :, bb, :], ym[:, :, bb, :],
                       zs[:, :, bb * SEQ:bb * SEQ + SEQ], ALU.mult).then_inc(S["y_gated"], 1)

                def c_norm():
                    dve.wait_ge(S["y_rstd"], upto(gc, "y_rstd", 1))
                    dve.wait_ge(*bank_filled("m_out"))
                    t, free = bank_to_read("m_out")
                    TT(s_out[:, :], t[:, :], crst[:, :], ALU.mult).then_inc(S["mamba_out"], 1)
                    dve.wait_ge(S["mamba_out"], upto(gc, "mamba_out", 1))
                    dve.sem_inc(free, 1)
                    TT(s_out[:, :], s_out[:, :], cxn[:, :], ALU.add).then_inc(S["mamba_out"], 1)

                def c_expert(half):
                    for e in range(half * NE // 2, (half + 1) * NE // 2):
                        if e == 0:
                            dve.wait_ge(S["gates"], upto(gc, "gates", NB))
                        dve.wait_ge(S["expert"], upto(gc, "expert", e + 1))
                        if e > 0:
                            dve.wait_ge(S["mixed"], upto(gc, "mixed", e))
                        for bb in range(NB):
                            a = rows2(eg[:, e % 2, :])[:, bb, :]
                            if e == 0:
                                m = TS(mix[:, bb, :], a, gt[:, bb, e:e + 1], None, ALU.mult)
                            else:
                                m = STT(out=mix[:, bb, :], in0=a, scalar=gt[:, bb, e:e + 1], in1=mix[:, bb, :],
                                        op0=ALU.mult, op1=ALU.add)
                        m.then_inc(S["mixed"], 1)

                def c_end():
                    dve.wait_ge(S["c_silu"], upto(gc, "c_silu", 1))
                    dve.wait_ge(S["mamba_out"], upto(gc, "mamba_out", 2))
                    TT(s_out[:, :], s_out[:, :], gate_c, ALU.mult).then_inc(S["c_gated"], 1)
                    dve.wait_ge(S["c_gated"], upto(gc, "c_gated", 1))
                    TT(x2T[:, :], s_out[:, :], x1T[:, :], ALU.add).then_inc(S["x2"], 1)

                return {"f_ln0": f_ln0, "f_proj": f_proj, "f_norms": f_norms, "f_v": f_v, "f_att": f_att,
                        "f_wo": f_wo, "f_ln": f_ln, "f_mlp": f_mlp, "f_end": f_end, "a_proj": a_proj,
                        "a_kv": a_kv, "a_max": a_max, "a_maxT": a_maxT, "a_exp": a_exp, "c_ln": c_ln,
                        "c_dt": c_dt, "c_conv": c_conv, "c_rows": c_rows, "c_head": c_head, "c_norm": c_norm,
                        "c_expert": c_expert, "c_end": c_end}

            run_trips(dve, "dve_trip", steps)

        @block.gpsimd
        def _(gp):
            for n, (dst, value) in enumerate((
                    (KS[:, :, :], 1.0), (lat[:, :], 1.0), (VA[:, :, :], 1.0), (hT[:, :, :], 0.0),
                    (cin[:, :, :, :], 0.0), (EPS, 1e-5), (HALF_SHIFT, LN_SHIFT / 2),
                    (HALF_SHIFT8, LN_SHIFT / 2 + LN_8))):
                gp.memset(dst, value).then_inc(consts, 1)
            assert n + 1 == CONSTS

            def steps(g, gc):
                def f_proj(l, p):
                    k = l * FP + p
                    gp.wait_ge(S["q_sin"], upto(g, "q_sin", k + 1))
                    gp.wait_ge(S["q_cos"], upto(g, "q_cos", k + 1))
                    gp.tensor_tensor(QR[:, p, :], QR[:, p, :], sinp[:, 0, :], ALU.add).then_inc(S["q_rot"], 1)
                    gp.wait_ge(S["k_sin"], upto(g, "k_sin", k + 1))
                    gp.wait_ge(S["k_cos"], upto(g, "k_cos", k + 1))
                    gp.tensor_tensor(KR[:, p, :], KR[:, p, :], sinp[:, 1, :], ALU.add).then_inc(S["k_rot"], 1)

                return {"f_proj": f_proj}

            run_trips(gp, "pool_trip", steps)

        @block.sync
        def _(sp):
            for i, (a, e) in enumerate(spans):
                sp.dma_start(W[:, a:e], w[:, a:e]).then_inc(weights_in[i], 16)
            sp.dma_start(rope0, tables).then_inc(tables_in, 16)
            sp.wait_ge(consts, CONSTS)

            def steps(g, gc):
                def f_ln0():
                    sp.dma_start(x_rows[:, :, :], x[g]).then_inc(S["x_loaded"], 16)

                def a_kv():
                    for i, (dst, which, name) in enumerate(((QS, Q_PART, "q_spread"), (KS, K_PART, "k_spread"))):
                        for part in range(NPART):
                            ready = ("a_part0", "a_part1", "a_part2")[part]
                            sp.wait_ge(S[ready], upto(g, ready, i + 1))
                            for r, part_r in enumerate(which):
                                if part_r == part:
                                    for lo in (0, 64):
                                        sp.dma_start(dst[lo + r * ADH:lo + r * ADH + ADH, :, :],
                                                     parts[lo:lo + 64, i, part, :]).then_inc(S[name], 16)

                def a_maxT():
                    for part in range(NPART):
                        ready = ("m_part0", "m_part1", "m_part2")[part]
                        sp.wait_ge(S[ready], upto(g, ready, 1))
                        for i in range(2):
                            row = 64 * i + QROWS + part
                            sp.dma_start(QS[row:row + 1, :, :], mparts[i * AP:i * AP + AP, part, :])\
                                .then_inc(S["m_spread"], 16)

                def c_end():
                    sp.wait_ge(S["out_rows"], upto(gc, "out_rows", 1))
                    sp.dma_start(out[gc], out_rows[:, :, :]).then_inc(S["out_stored"], 16)

                def stored():
                    sp.wait_ge(S["out_stored"], upto(gc, "out_stored", 16))

                return {"f_ln0": f_ln0, "a_kv": a_kv, "a_maxT": a_maxT, "c_end": c_end,
                        "f_end": stored if gc is not None else (lambda: None)}

            run_trips(sp, "sp_trip", steps)
            sp.wait_ge(S["out_stored"], NG * PER["out_stored"])


CONSTS = 8
SETUP = DEPTH * 4 + 2 + 1 + 1


def rotary_tables():
    import numpy as np

    half = np.arange(0, FDH, 2, dtype=np.float32)
    freqs = np.arange(SEQ, dtype=np.float32)[:, None] * (np.float32(1.0) / np.float32(10000.0) ** (half / FDH))[None, :]
    base = (half + 0.4 * FDH) / (1.4 * FDH)
    power = (np.arange(SEQ, dtype=np.float32) - SEQ // 2) / float(WIN // 2)
    scale = (base[None, :].astype(np.float64) ** power[:, None]).T
    cos, sin = np.cos(freqs.astype(np.float64)).T, np.sin(freqs.astype(np.float64)).T
    return np.stack([np.tile(cos * scale, (4, 1)), np.concatenate([-sin * scale, sin * scale] * 2),
                     np.tile(cos / scale, (4, 1)), np.concatenate([-sin / scale, sin / scale] * 2)],
                    1).astype(np.float32)


def host_layout(v):
    import numpy as np

    place, _, width = layout()
    w = np.zeros((128, width), np.float32)

    def put(name, a):
        at, n = place[name]
        a = np.asarray(a)
        w[:a.shape[0], at:at + n] = a

    def colv(a):
        return np.asarray(a).reshape(-1, 1)

    put("ident", np.eye(128))
    put("mean", np.full((128, 128), 1.0 / D))
    r = np.arange(128)
    put("block", (r[:, None] // 64 == r[None, :] // 64) * 1.0)
    put("heads", (r[:, None, None] // 64 + 2 * np.arange(FP)[None, :, None] == np.arange(FH)[None, None, :])
        .reshape(128, FP * FH) * 1.0)
    gap0 = r[:, None] - r[None, :]
    gap1 = 128 + r[:, None] - (64 + np.arange(192)[None, :])
    gap = np.concatenate([gap0, gap1], 1)
    put("band", np.where((gap < 0) | (gap > WIN), -1e30, 0.0))

    def by_pair(a):
        a = np.asarray(a)
        return a.reshape(a.shape[0], AP, 2, ADH).transpose(0, 2, 3, 1).reshape(a.shape[0], D)

    put("wq", by_pair(v["L0_attn_Wq"]))
    put("bq", by_pair(np.asarray(v["L0_attn_bq"]).reshape(1, D)).reshape(D, 1))
    put("wl", v["L0_attn_Wl"])
    put("bl", colv(v["L0_attn_bl"]))
    put("wk", by_pair(v["L0_attn_Wk"]))
    put("bk", by_pair(np.asarray(v["L0_attn_bk"]).reshape(1, D)).reshape(D, 1))
    put("wv", np.concatenate([np.asarray(v["L0_attn_Wv"]), np.asarray(v["L0_attn_bv"]).reshape(1, D)]))
    put("wo", v["L0_attn_Wo"])
    put("bo", colv(v["L0_attn_bo"]))

    def swap(a):
        a = np.asarray(a)
        return a.reshape(a.shape[0], -1, 2, FDH // 2)[:, :, ::-1].reshape(a.shape)

    def twice(a):
        return np.concatenate([a, a])

    for name, src in (("qs", "L0_ffn_q_scale"), ("ks", "L0_ffn_k_scale")):
        s = np.asarray(v[src])
        put(name, twice(s.T))
        put(name + "r", twice(swap(s).T))
    for l in range(DEPTH):
        qkv = np.asarray(v["L0_ffn_wqkv"])[l]
        q, k, vv = qkv[:, :INNER], qkv[:, INNER:2 * INNER], qkv[:, 2 * INNER:]
        put(f"fq{l}", q)
        put(f"fqr{l}", swap(q))
        put(f"fk{l}", k)
        put(f"fkr{l}", swap(k))
        put(f"fv{l}", vv)
        put(f"fo{l}", np.asarray(v["L0_ffn_wo"])[l].reshape(FP, 128, D).transpose(1, 0, 2).reshape(128, FP * D))
        put(f"w1{l}", np.asarray(v["L0_ffn_w1"])[l])
        w2 = np.zeros((128, HC, D), np.float32)
        b1 = np.zeros((128, 2 * HC), np.float32)
        for c in range(HC):
            w2[:HCN[c], c] = np.asarray(v["L0_ffn_w2"])[l][c * HCW:c * HCW + HCN[c]]
            for part in range(2):
                a = part * HID + c * HCW
                b1[:HCN[c], part * HC + c] = np.asarray(v["L0_ffn_b1"])[l][a:a + HCN[c]]
        put(f"w2{l}", w2.reshape(128, HC * D))
        put(f"b1{l}", b1)
        put(f"lg{l}", colv(np.asarray(v["L0_ffn_ln_g"])[l]))
        put(f"lb{l}", colv(np.asarray(v["L0_ffn_ln_b"])[l]))
        put(f"b2{l}", colv(np.asarray(v["L0_ffn_b2"])[l]))
    put("inp", np.asarray(v["L1_attn_in_proj_w"]).T)
    put("cw", np.asarray(v["L1_attn_conv_w"]).reshape(XBC, 128, TAPS).transpose(1, 0, 2).reshape(128, XBC * TAPS))
    put("cb", np.asarray(v["L1_attn_conv_b"]).reshape(XBC, 128).T)
    put("dtb", np.broadcast_to(np.asarray(v["L1_attn_dt_bias"]).reshape(1, MH), (128, MH)))
    put("alog", np.broadcast_to(np.asarray(v["L1_attn_A_log"]).reshape(1, MH), (128, MH)))
    put("dsk", np.repeat(np.asarray(v["L1_attn_D"]), MDH).reshape(2, 128).T)
    put("nw", np.asarray(v["L1_attn_norm_w"]).reshape(2, 128).T)
    put("outp", np.asarray(v["L1_attn_out_proj_w"]).T.reshape(2, 128, D).transpose(1, 0, 2).reshape(128, 2 * D))
    put("gw", np.asarray(v["L1_ffn_gate_w"]).T)
    put("gb", np.broadcast_to(np.asarray(v["L1_ffn_gate_b"]).reshape(1, NE), (128, NE)))
    put("ew", np.asarray(v["L1_ffn_expert_w"]).transpose(2, 0, 1).reshape(D, NE * D))
    put("eb", np.asarray(v["L1_ffn_expert_b"]).T)
    return w


def kernel(**inputs):
    import numpy as np
    import concourse.bacc as bacc
    from concourse.bass_utils import run_bass_kernel_spmd

    nc = bacc.Bacc("TRN2", target_bir_lowering=False, num_devices=1)
    w = host_layout(inputs)
    x = np.ascontiguousarray(np.asarray(inputs["L0_attn_x"]).reshape(NG, NT, 128, D).transpose(0, 2, 1, 3))
    xd = nc.dram_tensor("x", x.shape, F32, kind="ExternalInput").ap()
    wd = nc.dram_tensor("w", w.shape, F32, kind="ExternalInput").ap()
    od = nc.dram_tensor("out", x.shape, F32, kind="ExternalOutput").ap()
    tables = rotary_tables()
    td = nc.dram_tensor("tables", tables.shape, F32, kind="ExternalInput").ap()
    build(nc, xd, wd, td, od)
    r = run_bass_kernel_spmd(nc, [{"x": x, "w": w, "tables": tables}], core_ids=[0])
    got = np.asarray(r.results[0]["out"])
    return np.ascontiguousarray(got.transpose(0, 2, 1, 3)).reshape(BATCH, SEQ, D)
```

```python
import concourse.bass as bass
from concourse import mybir
from contextlib import ExitStack

F32 = mybir.dt.float32
BF16 = mybir.dt.bfloat16
ALU = mybir.AluOpType
ACT = mybir.ActivationFunctionType
AXX = mybir.AxisListType.X

D = 128
SEQ = 256
NB = 2
TOK = NB * SEQ
NT = TOK // 128
BATCH = 16
NG = BATCH // NB
AH, ADH, LATENT = 16, 8, 32
AP = AH // 2
NPART = 3
Q_PART = [0, 0, 0, 1, 1, 2]
K_PART = [0, 1, 2, 0, 1, 0]
QROWS = ADH * len(Q_PART)
MROWS = QROWS + NPART
DEPTH, FH, FDH, WIN = 2, 8, 64, 64
INNER = FH * FDH
FP = INNER // 128
HID = D * 4 * 2 // 3
HC = 3
HCW = -(-HID // HC)
HCN = [min(HCW, HID - c * HCW) for c in range(HC)]
SW = 128 + 192
DI, NS, MH, MDH, TAPS = 256, 128, 4, 64, 4
XBC = (DI + 2 * NS) // 128
NE = 8

NORM_SHIFT = 2.0 ** 20
LN_SHIFT = 20 * 0.6931471805599453
LN_8 = 3 * 0.6931471805599453


def layout():
    parts = [
        [("ident", 128), ("zeros", 128), ("mean", 128), ("wq", 128), ("wl", 32), ("wk", 128), ("wv", 128), ("wo", 128),
         ("bq", 1), ("bl", 1), ("bk", 1), ("bo", 1),
         ("block", 128), ("heads", FP * FH), ("band", SW),
         ("qs", 2), ("qsr", 2), ("ks", 2), ("ksr", 2)],
    ]
    for l in range(DEPTH):
        parts.append([(f"{n}{l}", w) for n, w in [
            ("fq", INNER), ("fqr", INNER), ("fk", INNER), ("fkr", INNER), ("fv", INNER), ("fo", FP * D),
            ("w1", 2 * HID), ("w2", HC * D), ("lg", 1), ("lb", 1), ("b1", 2 * HC), ("b2", 1)]])
    parts.append([("inp", 2 * DI + 2 * NS + MH), ("cw", XBC * TAPS), ("cb", XBC), ("dtb", MH), ("alog", MH),
                  ("dsk", 2), ("nw", 2), ("outp", 2 * D), ("gw", NE), ("gb", NE), ("ew", NE * D), ("eb", NE)])
    at, spans, place = 0, [], {}
    for part in parts:
        first = at
        for name, width in part:
            place[name] = (at, width)
            at += width
        spans.append((first, at))
    return place, spans, at


SERIES = [1.0 / n for n in (15, 13, 11, 9, 7, 5, 3)]

UNITS = NB * AH
GROUPS = UNITS // 4
FUNITS = NB * FH
PER = {
    "x_loaded": 16, "xT": 1, "x_centered": 1, "x_squared": 1, "x_log": 1, "x_rstd": 1, "xn": 1, "x_kept": 1,
    "ln_centered": DEPTH, "ln_squared": DEPTH, "ln_log": DEPTH, "ln_rstd": DEPTH, "ln_done": DEPTH,
    "a_q32": 2, "a_part0": 2, "a_rest1": 2, "a_part1": 2, "a_part2": 2,
    "q_spread": 16 * 12, "k_spread": 16 * 12, "m_spread": 16 * 6,
    "latent": 1, "a_v": 1, "max_filled": UNITS, "neg_max": UNITS,
    "m_rows": 1, "m_part0": 1, "m_rest1": 1, "m_part1": 1, "m_part2": 1,
    "exp_filled": UNITS, "a_exp": UNITS, "a_pv": UNITS, "a_heads": GROUPS, "a_rsum": GROUPS, "a_norm": GROUPS,
    "a_oT": 1,
    "shifted": 2 * DEPTH,
    "q_squared": DEPTH * FP, "k_squared": DEPTH * FP, "q_cos": DEPTH * FP, "q_sin": DEPTH * FP,
    "k_cos": DEPTH * FP, "k_sin": DEPTH * FP, "q_rot": DEPTH * FP, "k_rot": DEPTH * FP,
    "k_norm2": DEPTH * FP, "k_nlog": DEPTH * FP, "k_rnorm": DEPTH * FP, "k_final": DEPTH * FP,
    "q_norm2": DEPTH, "q_nlog": DEPTH, "q_rnorm": DEPTH, "f_v": DEPTH * NT,
    "f_masked": DEPTH * FUNITS, "f_negmax": DEPTH * FUNITS, "f_exp": DEPTH * FUNITS,
    "f_rsum": DEPTH * FUNITS, "f_probs": DEPTH * FUNITS, "f_probsT": DEPTH * FUNITS,
    "f_oT": DEPTH * FUNITS // 2, "f_res1": DEPTH, "f_affine": DEPTH,
    "f_gelu": DEPTH * HC, "f_hidden": DEPTH * HC, "f_res2": DEPTH,
    "f_silu": 1, "f_gated": 1, "x1": 1,
    "c_centered": 1, "c_squared": 1, "c_log": 1, "c_rstd": 1, "c_xn": 1,
    "conv_in": XBC, "conv": XBC * TAPS, "conv_silu": XBC, "z_silu": 2,
    "dt_raw": 1, "dt_abs": 1, "dt_exp": 1, "dt_step": 5 + len(SERIES), "dt": 1, "dt_a": 1, "dA": 1,
    "xdt": NT, "cb_prod": NB, "decay": NB * MH, "weights": NB * MH, "weights_used": NB * MH,
    "y_skip": NB, "y_gated": NB, "y_squared": 1, "y_log": 1, "y_rstd": 1, "mamba_out": 2,
    "pooled": 1, "pool_rows": NB, "logits": 1, "top": NB, "g_keep": NB, "g_negmax": NB, "g_exp": NB,
    "g_sum": NB, "g_rsum": NB, "gates": NB, "expert": NE, "mixed": NE,
    "c_silu": 1, "c_gated": 1, "x2": 1, "out_rows": 1, "out_stored": 16,
}
TRIPS = ["pe_trip", "act_trip", "dve_trip", "pool_trip", "sp_trip"]

SHARE = {
    "f_proj": (2.7, 4.5), "f_norms": (2.0, 2.5), "f_v": (2.5, 2.0), "f_att": (3.2, 3.52), "f_wo": (3.84, 3.2),
    "f_ln": (4.0, 4.0), "f_mlp": (4.0, 2.5), "next_x": (1.0,), "keep_x": (1.1,), "a_proj": (2.0,), "a_kv": (21.6,),
    "a_max": (2.11, 1.6, 0.58), "a_maxT": (4.8,), "a_exp": (1.4, 1.4, 1.4), "a_out": (2.4,), "c_ln": (3.5,),
    "c_dt": (2.0,), "c_conv": (2.0,), "c_z": (9.0,), "c_rows": (3.0,), "c_head": (2.82,), "c_norm": (5.0,),
    "c_expert": (4.0,), "c_end": (2.0,),
}
F_STEPS = []
for _l in range(DEPTH):
    F_STEPS += [("f_proj", _l, p) for p in range(FP)] + [("f_norms", _l, 0)]
    F_STEPS += [("f_v", _l, 0), ("f_norms", _l, 1), ("f_v", _l, 1)]
    F_STEPS += [("f_att", _l, s) for s in range(FUNITS // 2 + 3)]
    _last = _l == DEPTH - 1
    F_STEPS += [("f_wo", _l)] + [("next_x", 0)] * _last + [("f_ln", _l, 0)] + [("next_x", 1)] * _last
    F_STEPS += [("f_ln", _l, 1)] + [("next_x", 2)] * _last
    F_STEPS += [("f_mlp", _l, c) for c in range(HC + 1)]
A_STEPS = [("keep_x",), ("a_proj",), ("a_kv",)] + [("a_max", s) for s in range(UNITS // 2)] + [("a_maxT",)]
A_STEPS += [("a_exp", s) for s in range(UNITS // 2 + 2)] + [("a_out", 0), ("a_out", 1)]
C_STEPS = [("c_ln", 0), ("c_ln", 1), ("c_dt", 0), ("c_dt", 1), ("c_conv", 0), ("c_conv", 1), ("c_z",), ("c_rows",)]
C_STEPS += [("c_head", n) for n in range(NB * MH + 1)]
C_STEPS += [("c_norm",), ("c_expert", 0), ("c_expert", 1), ("c_end",)]


def side_by_side(a, b):
    def placed(steps):
        shares = [SHARE[s[0]][s[1] if s[0][0] == "f" else s[1] * len(SHARE[s[0]]) // (UNITS // 2 + 2) if s[0] in
                              ("a_max", "a_exp") else 0] for s in steps]
        return [(sum(shares[:i]) / sum(shares), s) for i, s in enumerate(steps)]

    return [s for _, s in sorted(placed(a) + placed(b), key=lambda e: e[0])]


FIRST_ORDER = [("first_x", part) for part in range(3)] + side_by_side(F_STEPS, A_STEPS)
FIRST_ORDER += [("f_end",), ("c_weights",)]
ORDER = side_by_side(F_STEPS, C_STEPS + A_STEPS) + [("f_end",)]
LAST_ORDER = C_STEPS

NBANK = 4
X_TILES, FA_TILES, C_TILES = 3, 165, 35


def build(nc, x, w, tables, out):
    place, spans, width = layout()
    ctx = ExitStack()
    with ctx:
        def sb(name, shape, dt=F32):
            return ctx.enter_context(nc.sbuf_tensor(name, shape, dt))

        def sem(name):
            return ctx.enter_context(nc.semaphore(name))

        W = sb("W", [128, width])

        def wt(name, rows=128):
            a, n = place[name]
            return W[0:rows, a:a + n]

        def col(name, j=0, rows=128):
            a, _ = place[name]
            return W[0:rows, a + j:a + j + 1]

        ident = wt("ident")
        at_ident, _ = place["ident"]
        step = W[:, at_ident:at_ident + SEQ]
        cols = sb("cols", [128, 3])
        EPS, HALF_SHIFT, HALF_SHIFT8 = (cols[:, j:j + 1] for j in range(3))
        rope = sb("rope", [128, DEPTH, 4, SEQ])
        outp = wt("outp").rearrange("p (j d) -> p j d", j=2)
        neg_a = wt("alog")

        f32op = sb("f32op", [128, 2, TOK])
        rest = sb("rest", [128, 2, TOK])
        parts = sb("parts", [128, 2, NPART, TOK], BF16)
        QS = sb("QS", [128, AP, TOK], BF16)
        KS = sb("KS", [128, AP, TOK], BF16)
        lat = sb("lat", [LATENT + 1, TOK])
        VW = ADH + 1
        VA = sb("VA", [128, NT, AH * VW + 32 - VW])
        nmax = sb("nmax", [128, NT, AH])
        mxr = sb("mxr", [AH, 2, TOK])
        mx, mrest = mxr[:, 0, :], mxr[:, 1, :]
        mparts = sb("mparts", [AH, NPART, TOK], BF16)
        NPT = 3
        PT = sb("PT", [128, NPT, 2, SEQ])
        heads4 = sb("heads4", [128, 2, SEQ])
        arsum = sb("arsum", [128, 2, 2, 4])
        AO = sb("AO", [128, 2, TOK])
        AN = AO[:, 0, :].rearrange("p (t h d) -> p t h d", t=NT, h=AH)
        aoT = AO[:, 1, :]
        s_out = sb("s_out", [128, TOK])

        x_rows = sb("x_rows", [128, NT, D])
        xT = sb("xT_", [128, TOK])
        xn = sb("xn", [128, TOK])
        cen = sb("cen", [128, TOK])
        sqr = sb("sqr", [128, TOK])
        rst = sqr
        hT = sb("hT", [128, NB, SEQ])
        QR = sb("QR", [128, FP, TOK])
        KR = sb("KR", [128, FP, TOK])
        sqq = sb("sqq", [128, FP, TOK])
        sqk = sb("sqk", [128, 2, TOK])
        sinp = sb("sinp", [128, 2, TOK])
        kn = sb("kn", [128, 2, TOK])
        qn = sb("qn", [128, NT, FH])
        V = sb("V", [128, NT, INNER])
        NMS = 8
        MS = sb("MS", [128, NMS, SW])
        fmx = sb("fmx", [128, FUNITS, 2])
        fnm = sb("fnm", [128, FUNITS, 2])
        fsum = sb("fsum", [128, FUNITS, 2])
        frs = sb("frs", [128, FUNITS, 2])
        NPP = 4
        PP = sb("PP", [128, NPP, 384])
        OT = sqq
        yT = sb("yT", [128, TOK])
        hn = cen
        ge = MS[:, :, :].rearrange("p n s -> p (n s)")[:, 0:HC * TOK].rearrange("p (c t) -> p c t", c=HC)
        hid = ge
        gate_f = sinp[:, 0, :]

        x1T = sb("x1T", [128, TOK])
        cxn = sb("cxn", [128, TOK])
        ccen = sb("ccen", [128, TOK])
        csqr = sb("csqr", [128, TOK])
        crst = csqr
        cin = sb("cin", [128, XBC, NB, SEQ + TAPS - 1])
        cs = QS[:, :, :].rearrange("p a t -> p (a t)").bitcast(F32).rearrange("p (j t) -> p j t", j=XBC)
        cv = cs.rearrange("p j (b t) -> p j b t", b=NB)
        zs = f32op
        dt7 = sb("dt7", [128, 8, NT, MH])
        dt_raw, dt_e, dt_w, dt_w2, dt_p, dt_pos, dt_, dt_dA = (dt7[:, k, :, :] for k in range(8))
        xd = rest[:, :, :].rearrange("p a (b h d) -> p (a b) h d", b=2, h=MH)
        pt = PT[:, :, :, :].rearrange("p n c q -> p (n c q)")
        cbp, dec = (pt[:, a * 768:a * 768 + 768].rearrange("p (b t) -> p b t", b=2) for a in range(2))
        pf = parts[:, :, :, :].rearrange("p i r t -> p (i r t)").bitcast(F32)
        wgt = pf[:, 0:768].rearrange("p (b t) -> p b t", b=2)
        out_rows = pf[:, 768:768 + NT * D].rearrange("p (t d) -> p t d", t=NT)
        poolb = pf[:, 1280:1280 + NB * 128].rearrange("p (b k) -> p b k", b=NB)
        ym = AO[:, :, :].rearrange("p j (b t) -> p j b t", b=NB)
        ysq = zs
        eg = pt[:, 0:2 * TOK].rearrange("p (a t) -> p a t", a=2)
        gate_c = heads4[:, :, :].rearrange("p b t -> p (b t)")
        mix = heads4
        x2T = ccen
        pool = sb("pool", [128, NB])
        lg_ = sb("lg_", [128, NB, NE])
        top = sb("top", [128, NB, 8])
        gsm = sb("gsm", [128, NB, 4])
        gex = sb("gex", [128, NB, NE])
        gkp = sb("gkp", [128, NB, NE])
        gt = sb("gt", [128, NB, NE])

        banks = [ctx.enter_context(nc.psum_tensor(f"bank{i}", [128, 512], F32)) for i in range(8)]
        MAXB, EXPB, WORK = banks[0:2], banks[2:4], banks[4:8]
        YB = MAXB[0]
        rope0 = MS[:, :, :].rearrange("p n s -> p (n s)")[:, 0:4 * SEQ].rearrange("p (k t) -> p k t", k=4)

        S = {name: sem(name) for name in list(PER) + TRIPS}
        weights_in = [sem(f"weights_in{i}") for i in range(len(spans))]
        tables_in = sem("tables_in")
        setup, c_setup = sem("setup"), sem("c_setup")
        consts = sem("consts")
        spacer = sem("spacer")
        work_filled = [sem(f"work_filled{b}") for b in range(NBANK)]
        work_read = [sem(f"work_read{b}") for b in range(NBANK)]

        def upto(g, name, k):
            return g * PER[name] + k

        def uses(tiles):
            return [len(range(b, tiles, NBANK)) for b in range(NBANK)]

        first_uses, loop_uses = uses(2 * X_TILES + FA_TILES), uses(FA_TILES + C_TILES + X_TILES)
        late_uses = uses(FA_TILES + C_TILES)
        FIRST, LOOP, LATE, LAST = range(4)
        work_place = [{}, {}, {}, {}]
        before = [[0] * NBANK, first_uses, [a + (NG - 2) * b for a, b in zip(first_uses, loop_uses)]]
        before.append([a + b for a, b in zip(before[LATE], late_uses)])
        trip = {"kind": FIRST, "i": 0}

        def turn(n):
            b = n % NBANK
            return before[trip["kind"]][b] + trip["i"] * loop_uses[b] + n // NBANK + 1

        def bank_free(name):
            n = len(work_place[trip["kind"]])
            work_place[trip["kind"]][name] = n
            return work_read[n % NBANK], turn(n)

        def bank_to_fill(name):
            n = work_place[trip["kind"]][name]
            return WORK[n % NBANK], work_filled[n % NBANK]

        def bank_filled(name):
            n = work_place[trip["kind"]][name]
            return work_filled[n % NBANK], turn(n)

        def bank_to_read(name):
            n = work_place[trip["kind"]][name]
            return WORK[n % NBANK], work_read[n % NBANK]

        def run_trips(eng, own, steps):
            def one(kind, i, g, gc, gn, order, trips_before):
                trip["kind"], trip["i"] = kind, i
                if kind != FIRST:
                    for name in TRIPS:
                        if name != own:
                            eng.wait_ge(S[name], trips_before)
                mine = steps(g, gc, gn)
                for name, *args in order:
                    if name in mine:
                        mine[name](*args)
                eng.sem_inc(S[own], 1)

            one(FIRST, 0, 0, None, 1, FIRST_ORDER, 0)
            with eng.Fori(0, NG - 2) as i:
                one(LOOP, i, i + 1, i, i + 2, ORDER, i + 1)
            one(LATE, 0, NG - 1, NG - 2, None, ORDER, NG - 1)
            one(LAST, 0, None, NG - 1, None, LAST_ORDER, NG)

        def unit(n):
            bb, h = n // AH, n % AH
            return bb, h, h // 2, 64 * (h % 2)

        def funit(n):
            bb, h = n // FH, n % FH
            return bb, h, h // 2, 64 * (h % 2)

        block = ctx.enter_context(nc.Block())

        @block.tensor
        def _(pe):
            pe.wait_ge(weights_in[0], 16)
            pe.wait_ge(consts, CONSTS)
            mm = pe.matmul

            def steps(g, gc, gn):
                h2 = hT[:, :, :].rearrange("p b t -> p (b t)")

                def x_norm(gx, part):
                    if part == 0:
                        pe.wait_ge(S["x_loaded"], upto(gx, "x_loaded", 16))
                        pe.wait_ge(*bank_free(("xT", gx is g)))
                        t, full = bank_to_fill(("xT", gx is g))
                        for j in range(NT):
                            m = pe.transpose(t[:, j * 128:j * 128 + 128], x_rows[:, j, :], ident)
                        m.then_inc(full, 1)
                    elif part == 1:
                        pe.wait_ge(S["xT"], upto(gx, "xT", 1))
                        pe.wait_ge(*bank_free(("x_mean", gx is g)))
                        t, full = bank_to_fill(("x_mean", gx is g))
                        mm(t[:, :], wt("mean"), xT[:, :], start=True, stop=True).then_inc(full, 1)
                    else:
                        pe.wait_ge(S["x_squared"], upto(gx, "x_squared", 1))
                        pe.wait_ge(*bank_free(("x_var", gx is g)))
                        t, full = bank_to_fill(("x_var", gx is g))
                        mm(t[:, :], wt("mean"), csqr[:, :], start=True, stop=True).then_inc(full, 1)

                def first_x(part):
                    x_norm(g, part)

                def next_x(part):
                    if gn is not None:
                        x_norm(gn, part)

                def f_proj(l, p):
                    if p == 0 and gc is None:
                        pe.wait_ge(weights_in[1 + l], 16)
                    if p == 0:
                        pe.wait_ge(S["shifted"], upto(g, "shifted", 2 * l + 1))
                    for name in ("fq", "fqr", "fk", "fkr"):
                        pe.wait_ge(*bank_free((name, l, p)))
                        t, full = bank_to_fill((name, l, p))
                        mm(t[:, :], wt(f"{name}{l}")[:, p * 128:p * 128 + 128], h2,
                           start=True, stop=True).then_inc(full, 1)
                    if p > 0:
                        k_norm(l, p - 1)

                def k_norm(l, p):
                    pe.wait_ge(S["k_squared"], upto(g, "k_squared", l * FP + p + 1))
                    pe.wait_ge(*bank_free(("k_norm", l, p)))
                    t, full = bank_to_fill(("k_norm", l, p))
                    mm(t[:, :], wt("block"), sqk[:, p % 2, :], start=True, stop=True).then_inc(full, 1)

                def f_norms(l, part):
                    if part == 1:
                        return
                    k_norm(l, FP - 1)
                    pe.wait_ge(S["q_squared"], upto(g, "q_squared", (l + 1) * FP))
                    pe.wait_ge(*bank_free(("q_norm", l)))
                    t, full = bank_to_fill(("q_norm", l))
                    for j in range(NT):
                        for p in range(FP):
                            m = mm(t[:, j * FH:j * FH + FH], sqq[:, p, j * 128:j * 128 + 128],
                                   wt("heads")[:, p * FH:p * FH + FH], start=(p == 0), stop=(p == FP - 1))
                    m.then_inc(full, 1)

                def f_v(l, half):
                    for j in range(2 * half, 2 * half + 2):
                        pe.wait_ge(*bank_free(("f_v", l, j)))
                        t, full = bank_to_fill(("f_v", l, j))
                        mm(t[:, :], h2[:, j * 128:j * 128 + 128], wt(f"fv{l}"), start=True,
                           stop=True).then_inc(full, 1)

                def f_scores(l, n):
                    bb, h, p, lo = funit(n)
                    q0 = bb * SEQ
                    if n < FH:
                        pe.wait_ge(S["q_rot"], upto(g, "q_rot", l * FP + p + 1))
                        pe.wait_ge(S["k_final"], upto(g, "k_final", l * FP + p + 1))
                    pe.wait_ge(*bank_free(("f_s", l, n)))
                    t, full = bank_to_fill(("f_s", l, n))
                    mm(t[:, 0:128], QR[lo:lo + 64, p, q0:q0 + 128], KR[lo:lo + 64, p, q0:q0 + 128],
                       start=True, stop=True)
                    mm(t[:, 128:SW], QR[lo:lo + 64, p, q0 + 128:q0 + 256],
                       KR[lo:lo + 64, p, q0 + 64:q0 + 256], start=True, stop=True).then_inc(full, 1)

                def f_transposes(l, n):
                    pe.wait_ge(S["f_probs"], upto(g, "f_probs", l * FUNITS + n + 1))
                    pe.wait_ge(*bank_free(("f_pT", l, n)))
                    t, full = bank_to_fill(("f_pT", l, n))
                    P = MS[:, n % NMS, :]
                    pe.transpose(t[:, 0:128], P[:, 0:128], ident)
                    pe.transpose(t[:, 128:256], P[:, 64:192], ident)
                    pe.transpose(t[:, 256:384], P[:, 192:320], ident).then_inc(full, 1)

                def f_pv(l, n):
                    bb, _, p, _ = funit(n)
                    pe.wait_ge(*bank_free(("f_o", l, n // 2)))
                    t, full = bank_to_fill(("f_o", l, n // 2))
                    pe.wait_ge(S["f_probsT"], upto(g, "f_probsT", l * FUNITS + n + 2))
                    heads = []
                    for i in range(2):
                        h = 2 * p + i
                        heads.append((t[64 * i:64 * i + 64, :], PP[:, (n + i) % NPP, :],
                                      slice(h * FDH, h * FDH + FDH)))
                    for o, P, hc in heads:
                        mm(o[:, 0:128], V[:, 2 * bb, hc], P[:, 0:128], start=True, stop=True)
                    for o, P, hc in heads:
                        mm(o[:, 128:256], V[64:128, 2 * bb, hc], P[64:128, 128:256], start=True, stop=False)
                    for o, P, hc in heads:
                        m = mm(o[:, 128:256], V[:, 2 * bb + 1, hc], P[:, 256:384], start=False, stop=True)
                    m.then_inc(full, 1)

                def f_att(l, s):
                    if s < FUNITS // 2:
                        f_scores(l, 2 * s)
                        f_scores(l, 2 * s + 1)
                    if 2 <= s < FUNITS // 2 + 2:
                        f_transposes(l, 2 * s - 4)
                        f_transposes(l, 2 * s - 3)
                    if s == 3:
                        pe.wait_ge(S["f_v"], upto(g, "f_v", (l + 1) * NT))
                    if 3 <= s:
                        f_pv(l, 2 * s - 6)

                def f_wo(l):
                    pe.wait_ge(S["f_oT"], upto(g, "f_oT", (l + 1) * FUNITS // 2))
                    pe.wait_ge(*bank_free(("f_wo", l)))
                    t, full = bank_to_fill(("f_wo", l))
                    for p in range(FP):
                        m = mm(t[:, :], wt(f"fo{l}")[:, p * D:p * D + D], OT[:, p, :], start=(p == 0),
                               stop=(p == FP - 1))
                    m.then_inc(full, 1)

                def f_ln(l, part):
                    if part == 0:
                        pe.wait_ge(S["shifted"], upto(g, "shifted", 2 * l + 2))
                        pe.wait_ge(*bank_free(("mean", l)))
                        t, full = bank_to_fill(("mean", l))
                        mm(t[:, :], wt("mean"), h2, start=True, stop=True).then_inc(full, 1)
                    else:
                        pe.wait_ge(S["ln_squared"], upto(g, "ln_squared", l + 1))
                        pe.wait_ge(*bank_free(("var", l)))
                        t, full = bank_to_fill(("var", l))
                        mm(t[:, :], wt("mean"), sqr[:, :], start=True, stop=True).then_inc(full, 1)

                def f_mlp(l, c):
                    if c == 0:
                        pe.wait_ge(S["f_affine"], upto(g, "f_affine", l + 1))
                    if c < HC:
                        for part in (1, 0):
                            pe.wait_ge(*bank_free(("w1", l, c, part)))
                            t, full = bank_to_fill(("w1", l, c, part))
                            a = part * HID + c * HCW
                            mm(t[0:HCN[c], :], wt(f"w1{l}")[:, a:a + HCN[c]], hn[:, :], start=True,
                               stop=True).then_inc(full, 1)
                        return
                    pe.wait_ge(*bank_free(("w2", l)))
                    t, full = bank_to_fill(("w2", l))
                    for c in range(HC):
                        pe.wait_ge(S["f_hidden"], upto(g, "f_hidden", l * HC + c + 1))
                        m = mm(t[:, :], wt(f"w2{l}", HCN[c])[:, c * D:c * D + D], hid[0:HCN[c], c, :],
                               start=(c == 0), stop=(c == HC - 1))
                    m.then_inc(full, 1)

                def a_proj():
                    pe.wait_ge(S["xn"], upto(g, "xn", 1))
                    pe.wait_ge(*bank_free("a_lat"))
                    t, full = bank_to_fill("a_lat")
                    mm(t[0:LATENT, :], wt("wl"), xn[:, :], start=True, stop=True).then_inc(full, 1)
                    pe.wait_ge(*bank_free(("a_proj", 0)))
                    t, full = bank_to_fill(("a_proj", 0))
                    mm(t[:, :], wt("wq"), xn[:, :], start=True, stop=True).then_inc(full, 1)

                def a_kv():
                    pe.wait_ge(S["latent"], upto(g, "latent", 1))
                    pe.wait_ge(*bank_free(("a_proj", 1)))
                    t, full = bank_to_fill(("a_proj", 1))
                    mm(t[:, :], wt("wk", LATENT), lat[0:LATENT, :], start=True, stop=True).then_inc(full, 1)
                    pe.wait_ge(*bank_free("a_v"))
                    t, full = bank_to_fill("a_v")
                    for j in range(NT):
                        m = mm(t[:, j * 128:j * 128 + 128], lat[:, j * 128:j * 128 + 128], wt("wv", LATENT + 1),
                               start=True, stop=True)
                    m.then_inc(full, 1)

                def a_max(s):
                    if s == 0:
                        pe.wait_ge(S["q_spread"], upto(g, "q_spread", PER["q_spread"]))
                        pe.wait_ge(S["k_spread"], upto(g, "k_spread", PER["k_spread"]))
                    for n in (2 * s, 2 * s + 1):
                        bb, h, p, lo = unit(n)
                        if n >= 2:
                            pe.wait_ge(S["neg_max"], upto(g, "neg_max", n - 1))
                        for qt in range(2):
                            q0 = bb * SEQ + qt * 128
                            m = mm(MAXB[n % 2][:, qt * SEQ:qt * SEQ + SEQ], QS[lo:lo + QROWS, p, q0:q0 + 128],
                                   KS[lo:lo + QROWS, p, bb * SEQ:bb * SEQ + SEQ], start=True, stop=True)
                        m.then_inc(S["max_filled"], 1)

                def a_maxT():
                    pe.wait_ge(S["neg_max"], upto(g, "neg_max", UNITS))
                    pe.wait_ge(*bank_free("maxT"))
                    t, full = bank_to_fill("maxT")
                    for j in range(NT):
                        m = pe.transpose(t[0:AH, j * 128:j * 128 + 128], nmax[:, j, :], ident)
                    m.then_inc(full, 1)

                def shifted_scores(n):
                    bb, h, p, lo = unit(n)
                    if n >= 2:
                        pe.wait_ge(S["a_exp"], upto(g, "a_exp", n - 1))
                    for c in range(2):
                        k0 = bb * SEQ + c * 128
                        m = mm(EXPB[n % 2][:, c * SEQ:c * SEQ + SEQ], KS[lo:lo + MROWS, p, k0:k0 + 128],
                               QS[lo:lo + MROWS, p, bb * SEQ:bb * SEQ + SEQ], start=True, stop=True)
                    m.then_inc(S["exp_filled"], 1)

                def probs_v(n):
                    bb, h, _, _ = unit(n)
                    r = n // 4
                    if n % 4 == 0 and r >= 2:
                        pe.wait_ge(S["a_heads"], upto(g, "a_heads", r - 1))
                    pe.wait_ge(S["a_exp"], upto(g, "a_exp", n + 1))
                    lo = 32 * (n % 4)
                    for c in range(2):
                        m = mm(MAXB[r % 2][lo:lo + 32, 0:SEQ], VA[:, 2 * bb + c, h * VW:h * VW + 32],
                               PT[:, n % NPT, c, :], start=(c == 0), stop=(c == 1))
                    m.then_inc(S["a_pv"], 1)

                def a_exp(s):
                    if s == 0:
                        pe.wait_ge(S["m_spread"], upto(g, "m_spread", PER["m_spread"]))
                        pe.wait_ge(S["a_v"], upto(g, "a_v", 1))
                    for n in (2 * s, 2 * s + 1):
                        if n < UNITS:
                            shifted_scores(n)
                        if 2 <= n < UNITS + 2:
                            probs_v(n - 2)
                    if s % 2 == 1 and s >= 3:
                        r = (s - 3) // 2
                        pe.wait_ge(S["a_heads"], upto(g, "a_heads", r + 1))
                        pe.wait_ge(*bank_free(("a_heads", r)))
                        t, full = bank_to_fill(("a_heads", r))
                        for qt in range(2):
                            m = pe.transpose(t[:, qt * 128:qt * 128 + 128], heads4[:, r % 2, qt * 128:qt * 128 + 128],
                                             ident)
                        m.then_inc(full, 1)

                def a_out(part):
                    if part == 0:
                        pe.wait_ge(S["a_norm"], upto(g, "a_norm", GROUPS))
                        pe.wait_ge(*bank_free("a_oT"))
                        t, full = bank_to_fill("a_oT")
                        for j in range(NT):
                            m = pe.transpose(t[:, j * 128:j * 128 + 128],
                                             AN[:, j, :, :].rearrange("p h d -> p (h d)"), ident)
                        m.then_inc(full, 1)
                        return
                    pe.wait_ge(S["a_oT"], upto(g, "a_oT", 1))
                    pe.wait_ge(*bank_free("a_out"))
                    t, full = bank_to_fill("a_out")
                    mm(t[:, :], wt("wo"), aoT, start=True, stop=True).then_inc(full, 1)

                def c_weights():
                    pe.wait_ge(weights_in[1 + DEPTH], 16)
                    pe.wait_ge(c_setup, C_SETUP)

                inp = wt("inp")

                def c_ln(part):
                    if part == 0:
                        pe.wait_ge(S["x1"], upto(gc, "x1", 1))
                        pe.wait_ge(*bank_free("c_mean"))
                        t, full = bank_to_fill("c_mean")
                        mm(t[:, :], wt("mean"), x1T[:, :], start=True, stop=True).then_inc(full, 1)
                        return
                    pe.wait_ge(S["c_squared"], upto(gc, "c_squared", 1))
                    pe.wait_ge(*bank_free("c_var"))
                    t, full = bank_to_fill("c_var")
                    mm(t[:, :], wt("mean"), csqr[:, :], start=True, stop=True).then_inc(full, 1)

                def c_dt(part):
                    if part == 0:
                        pe.wait_ge(S["c_xn"], upto(gc, "c_xn", 1))
                        pe.wait_ge(*bank_free("m_dt"))
                        t, full = bank_to_fill("m_dt")
                        for j in range(NT):
                            m = mm(t[:, j * MH:j * MH + MH], cxn[:, j * 128:j * 128 + 128],
                                   inp[:, 2 * DI + 2 * NS:], start=True, stop=True)
                        m.then_inc(full, 1)
                        return
                    pe.wait_ge(S["pool_rows"], upto(gc, "pool_rows", NB))
                    pe.wait_ge(*bank_free("logits"))
                    t, full = bank_to_fill("logits")
                    for bb in range(NB):
                        m = mm(t[:, bb * NE:bb * NE + NE], poolb[:, bb, :], wt("gw"), start=True, stop=True)
                    m.then_inc(full, 1)

                def c_conv(half):
                    for j in range(2 * half, 2 * half + 2):
                        pe.wait_ge(*bank_free(("m_xbc", j)))
                        t, full = bank_to_fill(("m_xbc", j))
                        mm(t[:, :], inp[:, DI + j * 128:DI + j * 128 + 128], cxn[:, :], start=True,
                           stop=True).then_inc(full, 1)

                def c_z():
                    for j in range(2):
                        pe.wait_ge(*bank_free(("m_z", j)))
                        t, full = bank_to_fill(("m_z", j))
                        mm(t[:, :], inp[:, j * 128:j * 128 + 128], cxn[:, :], start=True, stop=True).then_inc(full, 1)

                def c_rows():
                    pe.wait_ge(S["conv_silu"], upto(gc, "conv_silu", XBC))
                    for j in range(NT):
                        pe.wait_ge(*bank_free(("m_xt", j)))
                        t, full = bank_to_fill(("m_xt", j))
                        for c in range(2):
                            m = pe.transpose(t[:, c * 128:c * 128 + 128], cs[:, c, j * 128:j * 128 + 128], ident)
                        m.then_inc(full, 1)
                    for bb in range(NB):
                        t0 = bb * SEQ
                        pe.wait_ge(*bank_free(("m_cb", bb)))
                        t, full = bank_to_fill(("m_cb", bb))
                        mm(t[:, 0:256], cs[:, 2, t0:t0 + 128], cs[:, 3, t0:t0 + 256], start=True, stop=True)
                        mm(t[:, 256:384], cs[:, 2, t0 + 128:t0 + 256], cs[:, 3, t0 + 128:t0 + 256], start=True,
                           stop=True).then_inc(full, 1)

                def c_head(n):
                    bb, h = n // MH, n % MH
                    if n == 0:
                        pe.wait_ge(S["dA"], upto(gc, "dA", 1))
                        pe.wait_ge(S["xdt"], upto(gc, "xdt", NT))
                    if n < NB * MH:
                        pe.wait_ge(*bank_free(("m_dA", n)))
                        t, full = bank_to_fill(("m_dA", n))
                        for i in range(2):
                            m = mm(t[:, i * 128:i * 128 + 128],
                                   dt_dA[:, 2 * bb + i, h:h + 1].to_broadcast([128, 128]), ident,
                                   start=True, stop=True)
                        m.then_inc(full, 1)
                    if n == 0:
                        return
                    n -= 1
                    bb, h = n // MH, n % MH
                    if h == 0 and bb > 0:
                        pe.wait_ge(S["y_skip"], upto(gc, "y_skip", bb))
                    pe.wait_ge(S["weights"], upto(gc, "weights", n + 1))
                    lo, j = 64 * (h % 2), h // 2
                    o = YB[lo:lo + 64, j * SEQ:j * SEQ + SEQ]
                    mm(o, xd[:, 2 * bb, h, :], wgt[:, n % 2, 0:256], start=True, stop=False)
                    mm(o[:, 128:256], xd[:, 2 * bb + 1, h, :], wgt[:, n % 2, 256:384], start=False,
                       stop=True).then_inc(S["weights_used"], 1)

                def c_norm():
                    pe.wait_ge(S["y_gated"], upto(gc, "y_gated", NB))
                    pe.wait_ge(*bank_free("m_out"))
                    t, full = bank_to_fill("m_out")
                    for j in range(2):
                        m = mm(t[:, :], outp[:, j, :], ym[:, j, :, :].rearrange("p b t -> p (b t)"),
                               start=(j == 0), stop=(j == 1))
                    m.then_inc(full, 1)
                    pe.wait_ge(S["y_squared"], upto(gc, "y_squared", 1))
                    pe.wait_ge(*bank_free("m_ss"))
                    t, full = bank_to_fill("m_ss")
                    for j in range(2):
                        m = mm(t[:, :], wt("mean"), ysq[:, j, :], start=(j == 0), stop=(j == 1))
                    m.then_inc(full, 1)

                def c_expert(half):
                    for e in range(half * NE // 2, (half + 1) * NE // 2):
                        pe.wait_ge(*bank_free(("expert", e)))
                        t, full = bank_to_fill(("expert", e))
                        mm(t[:, :], wt("ew")[:, e * D:e * D + D], cxn[:, :], start=True, stop=True).then_inc(full, 1)

                def c_end():
                    pe.wait_ge(S["x2"], upto(gc, "x2", 1))
                    pe.wait_ge(*bank_free("outT"))
                    t, full = bank_to_fill("outT")
                    for j in range(NT):
                        m = pe.transpose(t[:, j * 128:j * 128 + 128], x2T[:, j * 128:j * 128 + 128], ident)
                    m.then_inc(full, 1)

                return {"first_x": first_x, "c_weights": c_weights, "next_x": next_x, "f_proj": f_proj,
                        "f_norms": f_norms, "f_v": f_v, "f_att": f_att, "f_wo": f_wo,
                        "f_ln": f_ln, "f_mlp": f_mlp, "a_proj": a_proj, "a_kv": a_kv, "a_max": a_max,
                        "a_maxT": a_maxT, "a_exp": a_exp, "a_out": a_out, "c_ln": c_ln, "c_dt": c_dt,
                        "c_conv": c_conv, "c_z": c_z, "c_rows": c_rows, "c_head": c_head, "c_norm": c_norm,
                        "c_expert": c_expert, "c_end": c_end}

            run_trips(pe, "pe_trip", steps)
            assert [len(p) for p in work_place] == [
                2 * X_TILES + FA_TILES, FA_TILES + C_TILES + X_TILES, FA_TILES + C_TILES, C_TILES]

        @block.scalar
        def _(act):
            act.wait_ge(consts, CONSTS)
            act.wait_ge(weights_in[0], 16)
            A = act.activation
            loaded = [None]

            def steps(g, gc, gn):
                loaded[0] = None

                def log_exp():
                    if loaded[0] != "log_exp":
                        act.sem_inc(spacer, 1)
                        act.preload_act_table_set("natural_log_exp_and_others")
                        loaded[0] = "log_exp"

                def table_of(f):
                    if loaded[0] != f:
                        act.sem_inc(spacer, 1)
                        act.preload_act_table(f)
                        loaded[0] = f

                def f_ln(n, part):
                    if part == 0:
                        act.wait_ge(S["ln_centered"], upto(g, "ln_centered", n + 1))
                        A(sqr[:, :], cen[:, :], ACT.Square).then_inc(S["ln_squared"], 1)
                        return
                    log_exp()
                    act.wait_ge(*bank_filled(("var", n)))
                    t, free = bank_to_read(("var", n))
                    A(rst[:, :], t[:, :], ACT.Ln, bias=EPS).then_inc(S["ln_log"], 1)
                    act.wait_ge(S["ln_log"], upto(g, "ln_log", n + 1))
                    act.sem_inc(free, 1)
                    A(rst[:, :], rst[:, :], ACT.Exp, scale=-0.5).then_inc(S["ln_rstd"], 1)

                def x_norm(gx, part):
                    if part == 0:
                        act.wait_ge(*bank_filled(("xT", gx is g)))
                        t, free = bank_to_read(("xT", gx is g))
                        A(xT[:, :], t[:, :], ACT.Identity).then_inc(S["xT"], 1)
                        act.wait_ge(S["xT"], upto(gx, "xT", 1))
                        act.sem_inc(free, 1)
                        return
                    if part == 1:
                        act.wait_ge(S["x_centered"], upto(gx, "x_centered", 1))
                        A(csqr[:, :], ccen[:, :], ACT.Square).then_inc(S["x_squared"], 1)
                        return
                    log_exp()
                    act.wait_ge(*bank_filled(("x_var", gx is g)))
                    t, free = bank_to_read(("x_var", gx is g))
                    A(crst[:, :], t[:, :], ACT.Ln, bias=EPS).then_inc(S["x_log"], 1)
                    act.wait_ge(S["x_log"], upto(gx, "x_log", 1))
                    act.sem_inc(free, 1)
                    A(crst[:, :], crst[:, :], ACT.Exp, scale=-0.5).then_inc(S["x_rstd"], 1)

                def first_x(part):
                    x_norm(g, part)

                def next_x(part):
                    if gn is not None:
                        if part == 0:
                            act.wait_ge(S["x_kept"], upto(g, "x_kept", 1))
                        x_norm(gn, part)

                def k_rnorm(l, p):
                    k = l * FP + p
                    act.wait_ge(S["k_norm2"], upto(g, "k_norm2", k + 1))
                    A(kn[:, p % 2, :], kn[:, p % 2, :], ACT.Ln, scale=NORM_SHIFT).then_inc(S["k_nlog"], 1)
                    act.wait_ge(S["k_nlog"], upto(g, "k_nlog", k + 1))
                    A(kn[:, p % 2, :], kn[:, p % 2, :], ACT.Exp, scale=-0.5, bias=HALF_SHIFT)\
                        .then_inc(S["k_rnorm"], 1)

                def c_weights():
                    log_exp()
                    act.wait_ge(weights_in[1 + DEPTH], 16)
                    A(neg_a, neg_a, ACT.Exp).then_inc(c_setup, 1)

                def f_proj(l, p):
                    log_exp()
                    if p == 0 and gc is None:
                        act.wait_ge(weights_in[1 + l], 16)
                    k = l * FP + p
                    act.wait_ge(*bank_filled(("fq", l, p)))
                    t, free = bank_to_read(("fq", l, p))
                    act.wait_ge(S["q_cos"], upto(g, "q_cos", k + 1))
                    A(sqq[:, p, :], t[:, :], ACT.Square).then_inc(S["q_squared"], 1)
                    act.wait_ge(S["q_squared"], upto(g, "q_squared", k + 1))
                    act.sem_inc(free, 1)
                    act.wait_ge(*bank_filled(("fk", l, p)))
                    t, free = bank_to_read(("fk", l, p))
                    act.wait_ge(S["k_cos"], upto(g, "k_cos", k + 1))
                    A(sqk[:, p % 2, :], t[:, :], ACT.Square).then_inc(S["k_squared"], 1)
                    act.wait_ge(S["k_squared"], upto(g, "k_squared", k + 1))
                    act.sem_inc(free, 1)
                    if p > 0:
                        k_rnorm(l, p - 1)

                def f_norms(l, part):
                    log_exp()
                    if part == 0:
                        k_rnorm(l, FP - 1)
                        return
                    q2 = qn[:, :, :].rearrange("p t h -> p (t h)")
                    act.wait_ge(S["q_norm2"], upto(g, "q_norm2", l + 1))
                    A(q2, q2, ACT.Ln, scale=NORM_SHIFT).then_inc(S["q_nlog"], 1)
                    act.wait_ge(S["q_nlog"], upto(g, "q_nlog", l + 1))
                    A(q2, q2, ACT.Exp, scale=-0.5, bias=HALF_SHIFT8).then_inc(S["q_rnorm"], 1)

                def f_v(l, half):
                    k = l * NT + 2 * half
                    for j in range(2):
                        act.wait_ge(*bank_filled(("f_v", l, 2 * half + j)))
                        t, free = bank_to_read(("f_v", l, 2 * half + j))
                        A(V[:, 2 * half + j, :], t[:, :], ACT.Identity).then_inc(S["f_v"], 1)
                        act.wait_ge(S["f_v"], upto(g, "f_v", k + j + 1))
                        act.sem_inc(free, 1)

                def f_exps(l, n):
                    log_exp()
                    act.wait_ge(S["f_negmax"], upto(g, "f_negmax", l * FUNITS + n + 1))
                    P = MS[:, n % NMS, :]
                    A(P[:, 0:128], P[:, 0:128], ACT.Exp, bias=fnm[:, n, 0:1], accum_out=fsum[:, n, 0:1])
                    A(P[:, 128:SW], P[:, 128:SW], ACT.Exp, bias=fnm[:, n, 1:2],
                      accum_out=fsum[:, n, 1:2]).then_inc(S["f_exp"], 1)

                def f_copy_pT(l, n):
                    act.wait_ge(*bank_filled(("f_pT", l, n)))
                    t, free = bank_to_read(("f_pT", l, n))
                    A(PP[:, n % NPP, :], t[:, 0:384], ACT.Identity).then_inc(S["f_probsT"], 1)
                    act.wait_ge(S["f_probsT"], upto(g, "f_probsT", l * FUNITS + n + 1))
                    act.sem_inc(free, 1)

                def f_att(l, s):
                    if 3 <= s:
                        n = s - 3
                        bb, p = n // FP, n % FP
                        if 2 <= s < FUNITS // 2 + 2:
                            f_copy_pT(l, 2 * s - 4)
                            f_copy_pT(l, 2 * s - 3)
                        act.wait_ge(*bank_filled(("f_o", l, n)))
                        t, free = bank_to_read(("f_o", l, n))
                        A(OT[:, p, bb * SEQ:bb * SEQ + SEQ], t[:, 0:SEQ], ACT.Identity).then_inc(S["f_oT"], 1)
                        act.wait_ge(S["f_oT"], upto(g, "f_oT", l * FUNITS // 2 + n + 1))
                        act.sem_inc(free, 1)
                    elif s == 2:
                        f_copy_pT(l, 0)
                        f_copy_pT(l, 1)
                    if s < FUNITS // 2:
                        f_exps(l, 2 * s)
                        f_exps(l, 2 * s + 1)

                def f_mlp(l, c):
                    if c < HC:
                        table_of(ACT.Gelu)
                        r = HCN[c]
                        act.wait_ge(*bank_filled(("w1", l, c, 1)))
                        t, free = bank_to_read(("w1", l, c, 1))
                        A(ge[0:r, c, :], t[0:r, :], ACT.Gelu, bias=col(f"b1{l}", HC + c, r)).then_inc(S["f_gelu"], 1)
                        act.wait_ge(S["f_gelu"], upto(g, "f_gelu", l * HC + c + 1))
                        act.sem_inc(free, 1)

                def f_end():
                    table_of(ACT.Silu)
                    act.wait_ge(S["f_res2"], upto(g, "f_res2", DEPTH))
                    A(gate_f, yT[:, :], ACT.Silu).then_inc(S["f_silu"], 1)

                def a_proj():
                    act.wait_ge(*bank_filled("a_lat"))
                    t, free = bank_to_read("a_lat")
                    A(lat[0:LATENT, :], t[0:LATENT, :], ACT.Identity, bias=col("bl", 0, LATENT))\
                        .then_inc(S["latent"], 1)
                    act.wait_ge(S["latent"], upto(g, "latent", 1))
                    act.sem_inc(free, 1)

                def a_kv():
                    if gc is not None:
                        act.wait_ge(S["out_stored"], upto(gc, "out_stored", 16))
                    for i in range(2):
                        act.wait_ge(S["a_q32"], upto(g, "a_q32", i + 1))
                        A(parts[:, i, 0, :], f32op[:, i, :], ACT.Identity).then_inc(S["a_part0"], 1)
                        act.wait_ge(S["a_rest1"], upto(g, "a_rest1", i + 1))
                        A(parts[:, i, 1, :], rest[:, i, :], ACT.Identity).then_inc(S["a_part1"], 1)

                def a_maxT():
                    act.wait_ge(*bank_filled("maxT"))
                    t, free = bank_to_read("maxT")
                    A(mx, t[0:AH, :], ACT.Identity).then_inc(S["m_rows"], 1)
                    act.wait_ge(S["m_rows"], upto(g, "m_rows", 1))
                    act.sem_inc(free, 1)
                    A(mparts[:, 0, :], mx, ACT.Identity).then_inc(S["m_part0"], 1)
                    act.wait_ge(S["m_rest1"], upto(g, "m_rest1", 1))
                    A(mparts[:, 1, :], mrest, ACT.Identity).then_inc(S["m_part1"], 1)

                def a_exp(s):
                    for n in (2 * s, 2 * s + 1):
                        if n < UNITS:
                            log_exp()
                            act.wait_ge(S["exp_filled"], upto(g, "exp_filled", n + 1))
                            if n >= NPT:
                                act.wait_ge(S["a_pv"], upto(g, "a_pv", n - NPT + 1))
                            A(PT[:, n % NPT, :, :].rearrange("p c q -> p (c q)"), EXPB[n % 2][:, :], ACT.Exp,
                              scale=ADH ** -0.5).then_inc(S["a_exp"], 1)

                def a_out(part):
                    if part == 1:
                        return
                    act.wait_ge(*bank_filled("a_oT"))
                    t, free = bank_to_read("a_oT")
                    A(aoT, t[:, :], ACT.Identity).then_inc(S["a_oT"], 1)
                    act.wait_ge(S["a_oT"], upto(g, "a_oT", 1))
                    act.sem_inc(free, 1)

                def c_ln(part):
                    if part == 0:
                        act.wait_ge(S["c_centered"], upto(gc, "c_centered", 1))
                        A(csqr[:, :], ccen[:, :], ACT.Square).then_inc(S["c_squared"], 1)
                        return
                    log_exp()
                    act.wait_ge(*bank_filled("c_var"))
                    t, free = bank_to_read("c_var")
                    A(crst[:, :], t[:, :], ACT.Ln, bias=EPS).then_inc(S["c_log"], 1)
                    act.wait_ge(S["c_log"], upto(gc, "c_log", 1))
                    act.sem_inc(free, 1)
                    A(crst[:, :], crst[:, :], ACT.Exp, scale=-0.5).then_inc(S["c_rstd"], 1)

                def c_dt(part):
                    log_exp()
                    if part == 0:
                        act.wait_ge(S["dt_raw"], upto(gc, "dt_raw", 1))
                        A(dt_e, dt_raw, ACT.Abs).then_inc(S["dt_abs"], 1)
                        act.wait_ge(S["dt_abs"], upto(gc, "dt_abs", 1))
                        A(dt_e, dt_e, ACT.Exp, scale=-1.0).then_inc(S["dt_exp"], 1)
                        return
                    for bb in range(NB):
                        act.wait_ge(S["g_negmax"], upto(gc, "g_negmax", bb + 1))
                        A(gex[:, bb, :], lg_[:, bb, :], ACT.Exp, bias=gsm[:, bb, 0:1]).then_inc(S["g_exp"], 1)

                def c_conv(half):
                    for j in range(2 * half, 2 * half + 2):
                        act.wait_ge(*bank_filled(("m_xbc", j)))
                        t, free = bank_to_read(("m_xbc", j))
                        A(cin[:, j, :, TAPS - 1:], t[:, :].rearrange("p (b t) -> p b t", b=NB), ACT.Identity)\
                            .then_inc(S["conv_in"], 1)
                        act.wait_ge(S["conv_in"], upto(gc, "conv_in", j + 1))
                        act.sem_inc(free, 1)
                    if half == 0:
                        log_exp()
                        act.wait_ge(S["dt_a"], upto(gc, "dt_a", 1))
                        A(dt_dA, dt_dA, ACT.Exp).then_inc(S["dA"], 1)

                def c_z():
                    table_of(ACT.Silu)
                    for j in range(2):
                        act.wait_ge(*bank_filled(("m_z", j)))
                        t, free = bank_to_read(("m_z", j))
                        A(zs[:, j, :], t[:, :], ACT.Silu).then_inc(S["z_silu"], 1)
                        act.wait_ge(S["z_silu"], upto(gc, "z_silu", j + 1))
                        act.sem_inc(free, 1)
                    for j in range(XBC):
                        act.wait_ge(S["conv"], upto(gc, "conv", TAPS * (j + 1)))
                        A(cs[:, j, :], cs[:, j, :], ACT.Silu).then_inc(S["conv_silu"], 1)

                def c_rows():
                    for bb in range(NB):
                        act.wait_ge(*bank_filled(("m_cb", bb)))
                        t, free = bank_to_read(("m_cb", bb))
                        A(cbp[:, bb, :], t[:, 0:384], ACT.Identity).then_inc(S["cb_prod"], 1)
                        act.wait_ge(S["cb_prod"], upto(gc, "cb_prod", bb + 1))
                        act.sem_inc(free, 1)

                def c_norm():
                    log_exp()
                    act.wait_ge(S["y_gated"], upto(gc, "y_gated", NB))
                    A(ysq[:, :, :], AO[:, :, :], ACT.Square).then_inc(S["y_squared"], 1)
                    act.wait_ge(*bank_filled("m_ss"))
                    t, free = bank_to_read("m_ss")
                    A(crst[:, :], t[:, :], ACT.Ln, bias=EPS, scale=0.5).then_inc(S["y_log"], 1)
                    act.wait_ge(S["y_log"], upto(gc, "y_log", 1))
                    act.sem_inc(free, 1)
                    A(crst[:, :], crst[:, :], ACT.Exp, scale=-0.5).then_inc(S["y_rstd"], 1)

                def c_expert(half):
                    table_of(ACT.Gelu)
                    for e in range(half * NE // 2, (half + 1) * NE // 2):
                        if e >= 2:
                            act.wait_ge(S["mixed"], upto(gc, "mixed", e - 1))
                        act.wait_ge(*bank_filled(("expert", e)))
                        t, free = bank_to_read(("expert", e))
                        A(eg[:, e % 2, :], t[:, :], ACT.Gelu, bias=col("eb", e)).then_inc(S["expert"], 1)
                        act.wait_ge(S["expert"], upto(gc, "expert", e + 1))
                        act.sem_inc(free, 1)

                def c_end():
                    table_of(ACT.Silu)
                    act.wait_ge(S["mixed"], upto(gc, "mixed", NE))
                    A(gate_c, gate_c, ACT.Silu).then_inc(S["c_silu"], 1)
                    act.wait_ge(*bank_filled("outT"))
                    t, free = bank_to_read("outT")
                    A(out_rows[:, :, :].rearrange("p t d -> p (t d)"), t[:, :], ACT.Identity)\
                        .then_inc(S["out_rows"], 1)
                    act.wait_ge(S["out_rows"], upto(gc, "out_rows", 1))
                    act.sem_inc(free, 1)

                return {"first_x": first_x, "c_weights": c_weights, "next_x": next_x, "f_proj": f_proj,
                        "f_norms": f_norms, "f_v": f_v, "f_att": f_att,
                        "f_ln": f_ln, "f_mlp": f_mlp, "f_end": f_end, "a_proj": a_proj, "a_kv": a_kv,
                        "a_maxT": a_maxT, "a_exp": a_exp, "a_out": a_out, "c_ln": c_ln, "c_dt": c_dt,
                        "c_conv": c_conv, "c_z": c_z, "c_rows": c_rows, "c_norm": c_norm,
                        "c_expert": c_expert, "c_end": c_end}

            run_trips(act, "act_trip", steps)

        @block.vector
        def _(dve):
            dve.wait_ge(weights_in[0], 16)
            dve.wait_ge(tables_in, 16)
            for l in range(DEPTH):
                for k, scale in enumerate(("qs", "qsr", "ks", "ksr")):
                    dve.tensor_scalar(rope[:, l, k, :], rope0[:, k, :], col(scale, l), None, ALU.mult)\
                        .then_inc(setup, 1)
            dve.wait_ge(setup, SETUP)
            dve.wait_ge(consts, CONSTS)
            for b in range(NBANK):
                dve.sem_inc(work_read[b], 1)
            TS, TT, STT = dve.tensor_scalar, dve.tensor_tensor, dve.scalar_tensor_tensor

            def rows2(t):
                return t.rearrange("p (b t) -> p b t", b=NB)

            def table(l, k):
                return rope[:, l, k, :].unsqueeze(1).to_broadcast([128, NB, SEQ])

            def steps(g, gc, gn):
                def shift(gx, k, src):
                    s3 = rows2(src)
                    dve.tensor_copy(hT[0:64, :, :], s3[0:64, :, :])
                    dve.tensor_copy(hT[64:128, :, 1:], s3[64:128, :, 0:SEQ - 1]).then_inc(S["shifted"], 1)
                    dve.wait_ge(S["shifted"], upto(gx, "shifted", k))

                def c_weights():
                    dve.wait_ge(weights_in[1 + DEPTH], 16)
                    for j in range(2):
                        TS(outp[:, j, :], outp[:, j, :], col("nw", j), None, ALU.mult).then_inc(c_setup, 1)
                    dve.wait_ge(c_setup, C_SETUP - 1)
                    TS(neg_a, neg_a, -1.0, None, ALU.mult).then_inc(c_setup, 1)
                    dve.wait_ge(c_setup, C_SETUP)

                def x_norm(gx, part):
                    if part == 0:
                        return
                    if part == 1:
                        dve.wait_ge(S["xT"], upto(gx, "xT", 1))
                        dve.wait_ge(*bank_filled(("x_mean", gx is g)))
                        t, free = bank_to_read(("x_mean", gx is g))
                        TT(ccen[:, :], xT[:, :], t[:, :], ALU.subtract).then_inc(S["x_centered"], 1)
                        dve.wait_ge(S["x_centered"], upto(gx, "x_centered", 1))
                        dve.sem_inc(free, 1)
                        return
                    dve.wait_ge(S["x_rstd"], upto(gx, "x_rstd", 1))
                    TT(xn[:, :], ccen[:, :], crst[:, :], ALU.mult).then_inc(S["xn"], 1)
                    dve.wait_ge(S["xn"], upto(gx, "xn", 1))
                    shift(gx, 1, xn[:, :])

                def first_x(part):
                    x_norm(g, part)

                def next_x(part):
                    if gn is not None:
                        if gc is not None and part == 0:
                            dve.wait_ge(S["out_rows"], upto(gc, "out_rows", 1))
                        x_norm(gn, part)

                def k_squares(l, p):
                    k = l * FP + p
                    if k >= 2:
                        dve.wait_ge(S["k_final"], upto(g, "k_final", k - 1))
                    dve.wait_ge(*bank_filled(("k_norm", l, p)))
                    t, free = bank_to_read(("k_norm", l, p))
                    TS(kn[:, p % 2, :], t[:, :], 1e-24, None, ALU.max).then_inc(S["k_norm2"], 1)
                    dve.wait_ge(S["k_norm2"], upto(g, "k_norm2", l * FP + p + 1))
                    dve.sem_inc(free, 1)

                def k_final(l, p):
                    k = l * FP + p
                    dve.wait_ge(S["k_rnorm"], upto(g, "k_rnorm", k + 1))
                    dve.wait_ge(S["k_rot"], upto(g, "k_rot", k + 1))
                    TT(KR[:, p, :], KR[:, p, :], kn[:, p % 2, :], ALU.mult).then_inc(S["k_final"], 1)

                def f_proj(l, p):
                    k = l * FP + p
                    if p == 0 and gc is None:
                        dve.wait_ge(weights_in[1 + l], 16)
                    for name, c, ca, sa, rot, R in (("fq", 0, "q_cos", "q_sin", "q_rot", QR),
                                                    ("fk", 2, "k_cos", "k_sin", "k_rot", KR)):
                        b = 0 if c == 0 else 1
                        dve.wait_ge(*bank_filled((name, l, p)))
                        t, free = bank_to_read((name, l, p))
                        TT(rows2(R[:, p, :]), rows2(t[:, :]), table(l, c), ALU.mult).then_inc(S[ca], 1)
                        dve.wait_ge(*bank_filled((name + "r", l, p)))
                        t, free = bank_to_read((name + "r", l, p))
                        if k > 0:
                            dve.wait_ge(S[rot], upto(g, rot, k))
                        TT(rows2(sinp[:, b, :]), rows2(t[:, :]), table(l, c + 1), ALU.mult).then_inc(S[sa], 1)
                        dve.wait_ge(S[sa], upto(g, sa, k + 1))
                        dve.sem_inc(free, 1)
                    if p > 0:
                        k_squares(l, p - 1)
                    if p > 1:
                        k_final(l, p - 2)

                def f_norms(l, part):
                    if part == 1:
                        k_final(l, FP - 2)
                        return
                    k_squares(l, FP - 1)
                    dve.wait_ge(*bank_filled(("q_norm", l)))
                    t, free = bank_to_read(("q_norm", l))
                    TS(qn[:, :, :].rearrange("p t h -> p (t h)"), t[:, 0:NT * FH], 1e-24, None, ALU.max)\
                        .then_inc(S["q_norm2"], 1)
                    dve.wait_ge(S["q_norm2"], upto(g, "q_norm2", l + 1))
                    dve.sem_inc(free, 1)

                def f_v(l, half):
                    if half == 1:
                        k_final(l, FP - 1)

                def masked(l, n):
                    bb, h, _, _ = funit(n)
                    t, free = bank_to_read(("f_s", l, n))
                    for u, a, e in ((0, 0, 128), (1, 128, SW)):
                        m = dve.tensor_tensor_reduce(MS[:, n % NMS, a:e], t[:, a:e], wt("band")[:, a:e],
                                                     qn[:, 2 * bb + u, h:h + 1], -3.0e38, ALU.add, ALU.max,
                                                     fmx[:, n, u:u + 1])
                    m.then_inc(S["f_masked"], 1)

                def f_att(l, s):
                    if s == 0:
                        dve.wait_ge(S["q_rnorm"], upto(g, "q_rnorm", l + 1))
                    if s < FUNITS // 2:
                        n = 2 * s
                        k = l * FUNITS + n
                        if n >= NMS:
                            dve.wait_ge(S["f_probsT"], upto(g, "f_probsT", k + 2 - NMS))
                        dve.wait_ge(*bank_filled(("f_s", l, n)))
                        dve.sem_inc(spacer, 1)
                        masked(l, n)
                        for j in (n, n + 1):
                            t, free = bank_to_read(("f_s", l, j))
                            dve.wait_ge(S["f_masked"], upto(g, "f_masked", l * FUNITS + j + 1))
                            dve.sem_inc(free, 1)
                            if j == n:
                                dve.wait_ge(*bank_filled(("f_s", l, n + 1)))
                            TS(fnm[:, j, :], fmx[:, j, :], -1.0, None, ALU.mult).then_inc(S["f_negmax"], 1)
                            if j == n:
                                masked(l, n + 1)
                    if 1 <= s < FUNITS // 2 + 1:
                        for j in (2 * s - 2, 2 * s - 1):
                            dve.wait_ge(S["f_exp"], upto(g, "f_exp", l * FUNITS + j + 1))
                            dve.reciprocal(frs[:, j, :], fsum[:, j, :]).then_inc(S["f_rsum"], 1)
                        for j in (2 * s - 2, 2 * s - 1):
                            dve.wait_ge(S["f_rsum"], upto(g, "f_rsum", l * FUNITS + j + 1))
                            P = MS[:, j % NMS, :]
                            TS(P[:, 0:128], P[:, 0:128], frs[:, j, 0:1], None, ALU.mult)
                            TS(P[:, 128:SW], P[:, 128:SW], frs[:, j, 1:2], None, ALU.mult).then_inc(S["f_probs"], 1)

                def f_wo(l):
                    src = xn if l == 0 else yT
                    dve.wait_ge(*bank_filled(("f_wo", l)))
                    t, free = bank_to_read(("f_wo", l))
                    TT(yT[:, :], t[:, :], src[:, :], ALU.add).then_inc(S["f_res1"], 1)
                    dve.wait_ge(S["f_res1"], upto(g, "f_res1", l + 1))
                    dve.sem_inc(free, 1)
                    shift(g, 2 * l + 2, yT[:, :])

                def f_ln(l, part):
                    if part == 0:
                        dve.wait_ge(*bank_filled(("mean", l)))
                        t, free = bank_to_read(("mean", l))
                        TT(cen[:, :], hT[:, :, :].rearrange("p b t -> p (b t)"), t[:, :], ALU.subtract)\
                            .then_inc(S["ln_centered"], 1)
                        dve.wait_ge(S["ln_centered"], upto(g, "ln_centered", l + 1))
                        dve.sem_inc(free, 1)
                        return
                    dve.wait_ge(S["ln_rstd"], upto(g, "ln_rstd", l + 1))
                    TT(hn[:, :], cen[:, :], rst[:, :], ALU.mult).then_inc(S["ln_done"], 1)
                    dve.wait_ge(S["ln_done"], upto(g, "ln_done", l + 1))
                    TS(hn[:, :], hn[:, :], col(f"lg{l}"), col(f"lb{l}"), ALU.mult, ALU.add).then_inc(S["f_affine"], 1)

                def f_mlp(l, c):
                    if c < HC:
                        r = HCN[c]
                        dve.wait_ge(S["f_gelu"], upto(g, "f_gelu", l * HC + c + 1))
                        dve.wait_ge(*bank_filled(("w1", l, c, 0)))
                        t, free = bank_to_read(("w1", l, c, 0))
                        STT(out=hid[0:r, c, :], in0=t[0:r, :], scalar=col(f"b1{l}", c, r), in1=ge[0:r, c, :],
                            op0=ALU.add, op1=ALU.mult).then_inc(S["f_hidden"], 1)
                        dve.wait_ge(S["f_hidden"], upto(g, "f_hidden", l * HC + c + 1))
                        dve.sem_inc(free, 1)
                        return
                    dve.wait_ge(*bank_filled(("w2", l)))
                    t, free = bank_to_read(("w2", l))
                    STT(out=yT[:, :], in0=t[:, :], scalar=col(f"b2{l}"), in1=yT[:, :], op0=ALU.add,
                        op1=ALU.add).then_inc(S["f_res2"], 1)
                    dve.wait_ge(S["f_res2"], upto(g, "f_res2", l + 1))
                    dve.sem_inc(free, 1)
                    if l + 1 < DEPTH:
                        shift(g, 2 * l + 3, yT[:, :])

                def f_end():
                    dve.wait_ge(S["f_silu"], upto(g, "f_silu", 1))
                    dve.wait_ge(*bank_filled("a_out"))
                    t, free = bank_to_read("a_out")
                    STT(out=s_out[:, :], in0=t[:, :], scalar=col("bo"), in1=gate_f, op0=ALU.add,
                        op1=ALU.mult).then_inc(S["f_gated"], 1)
                    dve.wait_ge(S["f_gated"], upto(g, "f_gated", 1))
                    dve.sem_inc(free, 1)
                    dve.wait_ge(S["x_kept"], upto(g, "x_kept", 1))
                    TT(x1T[:, :], s_out[:, :], x1T[:, :], ALU.add).then_inc(S["x1"], 1)

                def split(i):
                    dve.wait_ge(*bank_filled(("a_proj", i)))
                    t, free = bank_to_read(("a_proj", i))
                    TS(f32op[:, i, :], t[:, :], col(("bq", "bk")[i]), None, ALU.add).then_inc(S["a_q32"], 1)
                    dve.wait_ge(S["a_q32"], upto(g, "a_q32", i + 1))
                    dve.sem_inc(free, 1)

                def split_rest(i):
                    dve.wait_ge(S["a_part0"], upto(g, "a_part0", i + 1))
                    TT(rest[:, i, :], f32op[:, i, :], parts[:, i, 0, :], ALU.subtract).then_inc(S["a_rest1"], 1)
                    dve.wait_ge(S["a_part1"], upto(g, "a_part1", i + 1))
                    TT(parts[:, i, 2, :], rest[:, i, :], parts[:, i, 1, :], ALU.subtract).then_inc(S["a_part2"], 1)

                def a_proj():
                    split(0)

                def a_kv():
                    split(1)
                    dve.wait_ge(*bank_filled("a_v"))
                    t, free = bank_to_read("a_v")
                    dve.tensor_copy(VA[:, :, 0:AH * VW].rearrange("p t (h w) -> p t h w", h=AH)[:, :, :, 0:ADH],
                                    t[:, :].rearrange("p (t h d) -> p t h d", t=NT, h=AH)).then_inc(S["a_v"], 1)
                    split_rest(0)
                    split_rest(1)
                    dve.wait_ge(S["a_v"], upto(g, "a_v", 1))
                    dve.sem_inc(free, 1)

                def a_max(s):
                    for n in (2 * s, 2 * s + 1):
                        bb, h, _, _ = unit(n)
                        dve.wait_ge(S["max_filled"], upto(g, "max_filled", n + 1))
                        dve.tensor_reduce(nmax[:, 2 * bb:2 * bb + 2, (h % 2) * AP + h // 2],
                                          MAXB[n % 2][:, :].rearrange("p (a k) -> p a k", a=2), AXX, ALU.max,
                                          negate=True).then_inc(S["neg_max"], 1)

                def a_maxT():
                    dve.wait_ge(S["m_part0"], upto(g, "m_part0", 1))
                    TT(mrest, mx, mparts[:, 0, :], ALU.subtract).then_inc(S["m_rest1"], 1)
                    dve.wait_ge(S["m_part1"], upto(g, "m_part1", 1))
                    TT(mparts[:, 2, :], mrest, mparts[:, 1, :], ALU.subtract).then_inc(S["m_part2"], 1)

                def a_exp(s):
                    if s % 2 == 0 and 2 <= s <= 2 * GROUPS:
                        r = (s - 2) // 2
                        dve.wait_ge(S["a_pv"], upto(g, "a_pv", 4 * r + 4))
                        dve.tensor_copy(heads4[:, r % 2, :], MAXB[r % 2][:, 0:SEQ]).then_inc(S["a_heads"], 1)
                    if s % 2 == 1 and s >= 3:
                        r = (s - 3) // 2
                        bb, h0 = 4 * r // AH, 4 * r % AH
                        dve.wait_ge(*bank_filled(("a_heads", r)))
                        t, free = bank_to_read(("a_heads", r))
                        o = t[:, 0:256].rearrange("p (a h d) -> p a h d", a=2, h=4)
                        dve.reciprocal(arsum[:, r % 2, :, :], o[:, :, :, ADH]).then_inc(S["a_rsum"], 1)
                        dve.wait_ge(S["a_rsum"], upto(g, "a_rsum", r + 1))
                        TT(AN[:, 2 * bb:2 * bb + 2, h0:h0 + 4, :], o[:, :, :, 0:ADH],
                           arsum[:, r % 2, :, :].unsqueeze(3).to_broadcast([128, 2, 4, ADH]), ALU.mult)\
                            .then_inc(S["a_norm"], 1)
                        dve.wait_ge(S["a_norm"], upto(g, "a_norm", r + 1))
                        dve.sem_inc(free, 1)

                def c_ln(part):
                    if part == 0:
                        dve.wait_ge(*bank_filled("c_mean"))
                        t, free = bank_to_read("c_mean")
                        TT(ccen[:, :], x1T[:, :], t[:, :], ALU.subtract).then_inc(S["c_centered"], 1)
                        dve.wait_ge(S["c_centered"], upto(gc, "c_centered", 1))
                        dve.sem_inc(free, 1)
                        return
                    dve.wait_ge(S["c_rstd"], upto(gc, "c_rstd", 1))
                    TT(cxn[:, :], ccen[:, :], crst[:, :], ALU.mult).then_inc(S["c_xn"], 1)

                def c_dt(part):
                    if part == 1:
                        gate_logits()
                        return
                    dve.wait_ge(*bank_filled("m_dt"))
                    t, free = bank_to_read("m_dt")
                    heads = [128, NT, MH]
                    TT(dt_raw, t[:, 0:NT * MH].rearrange("p (t h) -> p t h", t=NT),
                       wt("dtb").unsqueeze(1).to_broadcast(heads), ALU.add).then_inc(S["dt_raw"], 1)
                    dve.wait_ge(S["dt_raw"], upto(gc, "dt_raw", 1))
                    dve.sem_inc(free, 1)
                    dve.wait_ge(S["c_xn"], upto(gc, "c_xn", 1))
                    dve.tensor_reduce(pool[:, :], rows2(cxn[:, :]), AXX, ALU.add).then_inc(S["pooled"], 1)
                    dve.wait_ge(S["pooled"], upto(gc, "pooled", 1))
                    for bb in range(NB):
                        TS(poolb[:, bb, :], pool[:, bb:bb + 1].to_broadcast([128, 128]), 1.0 / SEQ, None, ALU.mult)\
                            .then_inc(S["pool_rows"], 1)

                def gate_logits():
                    dve.wait_ge(*bank_filled("logits"))
                    t, free = bank_to_read("logits")
                    TT(lg_[:, :, :], t[:, 0:NB * NE].rearrange("p (b e) -> p b e", b=NB),
                       wt("gb").unsqueeze(1).to_broadcast([128, NB, NE]), ALU.add).then_inc(S["logits"], 1)
                    dve.wait_ge(S["logits"], upto(gc, "logits", 1))
                    dve.sem_inc(free, 1)
                    for bb in range(NB):
                        dve.max(top[:, bb, :], lg_[:, bb, :]).then_inc(S["top"], 1)
                    for bb in range(NB):
                        dve.wait_ge(S["top"], upto(gc, "top", bb + 1))
                        TS(gsm[:, bb, 0:1], top[:, bb, 0:1], -1.0, None, ALU.mult).then_inc(S["g_negmax"], 1)
                        TS(gkp[:, bb, :], lg_[:, bb, :], top[:, bb, 1:2], None, ALU.is_ge).then_inc(S["g_keep"], 1)

                def softplus():
                    TS(dt_pos, dt_raw, 0.0, None, ALU.max)
                    dve.wait_ge(S["dt_exp"], upto(gc, "dt_exp", 1))
                    TS(dt_w, dt_e, 2.0, None, ALU.add).then_inc(S["dt_step"], 1)
                    dve.wait_ge(S["dt_step"], upto(gc, "dt_step", 1))
                    dve.reciprocal(dt_w, dt_w).then_inc(S["dt_step"], 1)
                    dve.wait_ge(S["dt_step"], upto(gc, "dt_step", 2))
                    TT(dt_w, dt_w, dt_e, ALU.mult).then_inc(S["dt_step"], 1)
                    dve.wait_ge(S["dt_step"], upto(gc, "dt_step", 3))
                    TT(dt_w2, dt_w, dt_w, ALU.mult).then_inc(S["dt_step"], 1)
                    for k, c in enumerate(SERIES):
                        dve.wait_ge(S["dt_step"], upto(gc, "dt_step", 4 + k))
                        if k == 0:
                            TS(dt_p, dt_w2, c, None, ALU.mult).then_inc(S["dt_step"], 1)
                        else:
                            STT(out=dt_p, in0=dt_p, scalar=c, in1=dt_w2, op0=ALU.add, op1=ALU.mult)\
                                .then_inc(S["dt_step"], 1)
                    dve.wait_ge(S["dt_step"], upto(gc, "dt_step", 4 + len(SERIES)))
                    STT(out=dt_p, in0=dt_p, scalar=1.0, in1=dt_w, op0=ALU.add, op1=ALU.mult).then_inc(S["dt_step"], 1)
                    dve.wait_ge(S["dt_step"], upto(gc, "dt_step", 5 + len(SERIES)))
                    STT(out=dt_, in0=dt_p, scalar=2.0, in1=dt_pos, op0=ALU.mult, op1=ALU.add).then_inc(S["dt"], 1)
                    dve.wait_ge(S["dt"], upto(gc, "dt", 1))
                    TT(dt_dA, dt_, neg_a.unsqueeze(1).to_broadcast([128, NT, MH]), ALU.mult).then_inc(S["dt_a"], 1)

                def gates():
                    for bb in range(NB):
                        dve.wait_ge(S["g_exp"], upto(gc, "g_exp", bb + 1))
                        dve.wait_ge(S["g_keep"], upto(gc, "g_keep", bb + 1))
                        dve.tensor_tensor_reduce(gkp[:, bb, :], gkp[:, bb, :], gex[:, bb, :], 1.0, 0.0, ALU.mult,
                                                 ALU.add, gsm[:, bb, 1:2]).then_inc(S["g_sum"], 1)
                    for bb in range(NB):
                        dve.wait_ge(S["g_sum"], upto(gc, "g_sum", bb + 1))
                        dve.reciprocal(gsm[:, bb, 2:3], gsm[:, bb, 1:2]).then_inc(S["g_rsum"], 1)
                    for bb in range(NB):
                        dve.wait_ge(S["g_rsum"], upto(gc, "g_rsum", bb + 1))
                        TS(gt[:, bb, :], gkp[:, bb, :], gsm[:, bb, 2:3], None, ALU.mult).then_inc(S["gates"], 1)

                def c_conv(half):
                    if half == 0:
                        softplus()
                        gates()
                    for j in range(2 * half, 2 * half + 2):
                        dve.wait_ge(S["conv_in"], upto(gc, "conv_in", j + 1))
                        for k in range(TAPS):
                            a = cin[:, j, :, k:k + SEQ]
                            if k == 0:
                                TS(cv[:, j, :, :], a, col("cw", j * TAPS), col("cb", j), ALU.mult, ALU.add)\
                                    .then_inc(S["conv"], 1)
                            else:
                                dve.wait_ge(S["conv"], upto(gc, "conv", j * TAPS + k))
                                STT(out=cv[:, j, :, :], in0=a, scalar=col("cw", j * TAPS + k), in1=cv[:, j, :, :],
                                    op0=ALU.mult, op1=ALU.add).then_inc(S["conv"], 1)

                def c_rows():
                    for j in range(NT):
                        dve.wait_ge(*bank_filled(("m_xt", j)))
                        t, free = bank_to_read(("m_xt", j))
                        TT(xd[:, j, :, :], t[:, 0:DI].rearrange("p (h d) -> p h d", h=MH),
                           dt_[:, j, :].unsqueeze(2).to_broadcast([128, MH, MDH]), ALU.mult).then_inc(S["xdt"], 1)
                        dve.wait_ge(S["xdt"], upto(gc, "xdt", j + 1))
                        dve.sem_inc(free, 1)

                def c_head(n):
                    if n > 0 and n % MH == 0:
                        y_of(n // MH - 1)
                    if n == NB * MH:
                        return
                    bb, h = n // MH, n % MH
                    dve.wait_ge(S["cb_prod"], upto(gc, "cb_prod", bb + 1))
                    dve.wait_ge(*bank_filled(("m_dA", n)))
                    t, free = bank_to_read(("m_dA", n))
                    dve.tensor_tensor_scan(dec[:, n % 2, 0:256], t[:, 0:256], step, 0.0, ALU.mult, ALU.add)
                    dve.tensor_tensor_scan(dec[:, n % 2, 256:384], t[:, 128:256], ident, 0.0,
                                           ALU.mult, ALU.add).then_inc(S["decay"], 1)
                    dve.wait_ge(S["decay"], upto(gc, "decay", n + 1))
                    dve.sem_inc(free, 1)
                    if n >= 2:
                        dve.wait_ge(S["weights_used"], upto(gc, "weights_used", n - 1))
                    TT(wgt[:, n % 2, :], dec[:, n % 2, :], cbp[:, bb, :], ALU.mult).then_inc(S["weights"], 1)

                def y_of(bb):
                    dve.wait_ge(S["z_silu"], upto(gc, "z_silu", 2))
                    dve.wait_ge(S["weights_used"], upto(gc, "weights_used", (bb + 1) * MH))
                    for j in range(2):
                        m = STT(out=ym[:, j, bb, :], in0=rows2(cs[:, j, :])[:, bb, :], scalar=col("dsk", j),
                                in1=YB[:, j * SEQ:j * SEQ + SEQ], op0=ALU.mult, op1=ALU.add)
                    m.then_inc(S["y_skip"], 1)
                    dve.wait_ge(S["y_skip"], upto(gc, "y_skip", bb + 1))
                    TT(ym[:, :, bb, :], ym[:, :, bb, :],
                       zs[:, :, bb * SEQ:bb * SEQ + SEQ], ALU.mult).then_inc(S["y_gated"], 1)

                def c_norm():
                    dve.wait_ge(S["y_rstd"], upto(gc, "y_rstd", 1))
                    dve.wait_ge(*bank_filled("m_out"))
                    t, free = bank_to_read("m_out")
                    TT(s_out[:, :], t[:, :], crst[:, :], ALU.mult).then_inc(S["mamba_out"], 1)
                    dve.wait_ge(S["mamba_out"], upto(gc, "mamba_out", 1))
                    dve.sem_inc(free, 1)
                    TT(s_out[:, :], s_out[:, :], cxn[:, :], ALU.add).then_inc(S["mamba_out"], 1)

                def c_expert(half):
                    for e in range(half * NE // 2, (half + 1) * NE // 2):
                        if e == 0:
                            dve.wait_ge(S["gates"], upto(gc, "gates", NB))
                        dve.wait_ge(S["expert"], upto(gc, "expert", e + 1))
                        if e > 0:
                            dve.wait_ge(S["mixed"], upto(gc, "mixed", e))
                        for bb in range(NB):
                            a = rows2(eg[:, e % 2, :])[:, bb, :]
                            if e == 0:
                                m = TS(mix[:, bb, :], a, gt[:, bb, e:e + 1], None, ALU.mult)
                            else:
                                m = STT(out=mix[:, bb, :], in0=a, scalar=gt[:, bb, e:e + 1], in1=mix[:, bb, :],
                                        op0=ALU.mult, op1=ALU.add)
                        m.then_inc(S["mixed"], 1)

                def c_end():
                    dve.wait_ge(S["c_silu"], upto(gc, "c_silu", 1))
                    dve.wait_ge(S["mamba_out"], upto(gc, "mamba_out", 2))
                    TT(s_out[:, :], s_out[:, :], gate_c, ALU.mult).then_inc(S["c_gated"], 1)
                    dve.wait_ge(S["c_gated"], upto(gc, "c_gated", 1))
                    TT(x2T[:, :], s_out[:, :], x1T[:, :], ALU.add).then_inc(S["x2"], 1)

                return {"first_x": first_x, "c_weights": c_weights, "next_x": next_x, "f_proj": f_proj,
                        "f_norms": f_norms, "f_v": f_v, "f_att": f_att,
                        "f_wo": f_wo, "f_ln": f_ln, "f_mlp": f_mlp, "f_end": f_end, "a_proj": a_proj,
                        "a_kv": a_kv, "a_max": a_max, "a_maxT": a_maxT, "a_exp": a_exp, "c_ln": c_ln,
                        "c_dt": c_dt, "c_conv": c_conv, "c_rows": c_rows, "c_head": c_head, "c_norm": c_norm,
                        "c_expert": c_expert, "c_end": c_end}

            run_trips(dve, "dve_trip", steps)

        @block.gpsimd
        def _(gp):
            for n, (dst, value) in enumerate((
                    (KS[:, :, :], 1.0), (lat[:, :], 1.0), (VA[:, :, :], 1.0), (hT[:, :, :], 0.0),
                    (cin[:, :, :, :], 0.0), (EPS, 1e-5), (HALF_SHIFT, LN_SHIFT / 2),
                    (HALF_SHIFT8, LN_SHIFT / 2 + LN_8))):
                gp.memset(dst, value).then_inc(consts, 1)
            assert n + 1 == CONSTS

            def steps(g, gc, gn):
                def f_proj(l, p):
                    k = l * FP + p
                    gp.wait_ge(S["q_sin"], upto(g, "q_sin", k + 1))
                    gp.wait_ge(S["q_cos"], upto(g, "q_cos", k + 1))
                    gp.tensor_tensor(QR[:, p, :], QR[:, p, :], sinp[:, 0, :], ALU.add).then_inc(S["q_rot"], 1)
                    gp.wait_ge(S["k_sin"], upto(g, "k_sin", k + 1))
                    gp.wait_ge(S["k_cos"], upto(g, "k_cos", k + 1))
                    gp.tensor_tensor(KR[:, p, :], KR[:, p, :], sinp[:, 1, :], ALU.add).then_inc(S["k_rot"], 1)

                def keep_x():
                    gp.wait_ge(S["xT"], upto(g, "xT", 1))
                    if gc is not None:
                        gp.wait_ge(S["x2"], upto(gc, "x2", 1))
                        gp.sem_inc(spacer, 1)
                    gp.tensor_copy(x1T[:, :], xT[:, :]).then_inc(S["x_kept"], 1)

                return {"f_proj": f_proj, "keep_x": keep_x}

            run_trips(gp, "pool_trip", steps)

        @block.sync
        def _(sp):
            for i, (a, e) in enumerate(spans):
                sp.dma_start(W[:, a:e], w[:, a:e]).then_inc(weights_in[i], 16)
                if i == 0:
                    sp.dma_start(x_rows[:, :, :], x[0]).then_inc(S["x_loaded"], 16)
                    sp.dma_start(rope0, tables).then_inc(tables_in, 16)
            sp.wait_ge(consts, CONSTS)

            def steps(g, gc, gn):
                def a_kv():
                    if gn is not None:
                        sp.wait_ge(S["xT"], upto(g, "xT", 1))
                        sp.dma_start(x_rows[:, :, :], x[gn]).then_inc(S["x_loaded"], 16)
                    for i, (dst, which, name) in enumerate(((QS, Q_PART, "q_spread"), (KS, K_PART, "k_spread"))):
                        for part in range(NPART):
                            ready = ("a_part0", "a_part1", "a_part2")[part]
                            sp.wait_ge(S[ready], upto(g, ready, i + 1))
                            for r, part_r in enumerate(which):
                                if part_r == part:
                                    for lo in (0, 64):
                                        sp.dma_start(dst[lo + r * ADH:lo + r * ADH + ADH, :, :],
                                                     parts[lo:lo + 64, i, part, :]).then_inc(S[name], 16)

                def a_maxT():
                    for part in range(NPART):
                        ready = ("m_part0", "m_part1", "m_part2")[part]
                        sp.wait_ge(S[ready], upto(g, ready, 1))
                        for i in range(2):
                            row = 64 * i + QROWS + part
                            sp.dma_start(QS[row:row + 1, :, :], mparts[i * AP:i * AP + AP, part, :])\
                                .then_inc(S["m_spread"], 16)

                def c_end():
                    sp.wait_ge(S["out_rows"], upto(gc, "out_rows", 1))
                    sp.dma_start(out[gc], out_rows[:, :, :]).then_inc(S["out_stored"], 16)

                def stored():
                    sp.wait_ge(S["out_stored"], upto(gc, "out_stored", 16))

                return {"a_kv": a_kv, "a_maxT": a_maxT, "c_end": c_end,
                        "f_end": stored if gc is not None else (lambda: None)}

            run_trips(sp, "sp_trip", steps)
            sp.wait_ge(S["out_stored"], NG * PER["out_stored"])


CONSTS = 8
SETUP = DEPTH * 4
C_SETUP = 2 + 1 + 1


def rotary_tables():
    import numpy as np

    half = np.arange(0, FDH, 2, dtype=np.float32)
    freqs = np.arange(SEQ, dtype=np.float32)[:, None] * (np.float32(1.0) / np.float32(10000.0) ** (half / FDH))[None, :]
    base = (half + 0.4 * FDH) / (1.4 * FDH)
    power = (np.arange(SEQ, dtype=np.float32) - SEQ // 2) / float(WIN // 2)
    scale = (base[None, :].astype(np.float64) ** power[:, None]).T
    cos, sin = np.cos(freqs.astype(np.float64)).T, np.sin(freqs.astype(np.float64)).T
    return np.stack([np.tile(cos * scale, (4, 1)), np.concatenate([-sin * scale, sin * scale] * 2),
                     np.tile(cos / scale, (4, 1)), np.concatenate([-sin / scale, sin / scale] * 2)],
                    1).astype(np.float32)


def host_layout(v):
    import numpy as np

    place, _, width = layout()
    w = np.zeros((128, width), np.float32)

    def put(name, a):
        at, n = place[name]
        a = np.asarray(a)
        w[:a.shape[0], at:at + n] = a

    def colv(a):
        return np.asarray(a).reshape(-1, 1)

    put("ident", np.eye(128))
    put("mean", np.full((128, 128), 1.0 / D))
    r = np.arange(128)
    put("block", (r[:, None] // 64 == r[None, :] // 64) * 1.0)
    put("heads", (r[:, None, None] // 64 + 2 * np.arange(FP)[None, :, None] == np.arange(FH)[None, None, :])
        .reshape(128, FP * FH) * 1.0)
    gap0 = r[:, None] - r[None, :]
    gap1 = 128 + r[:, None] - (64 + np.arange(192)[None, :])
    gap = np.concatenate([gap0, gap1], 1)
    put("band", np.where((gap < 0) | (gap > WIN), -1e30, 0.0))

    def by_pair(a):
        a = np.asarray(a)
        return a.reshape(a.shape[0], AP, 2, ADH).transpose(0, 2, 3, 1).reshape(a.shape[0], D)

    put("wq", by_pair(v["L0_attn_Wq"]))
    put("bq", by_pair(np.asarray(v["L0_attn_bq"]).reshape(1, D)).reshape(D, 1))
    put("wl", v["L0_attn_Wl"])
    put("bl", colv(v["L0_attn_bl"]))
    put("wk", by_pair(v["L0_attn_Wk"]))
    put("bk", by_pair(np.asarray(v["L0_attn_bk"]).reshape(1, D)).reshape(D, 1))
    put("wv", np.concatenate([np.asarray(v["L0_attn_Wv"]), np.asarray(v["L0_attn_bv"]).reshape(1, D)]))
    put("wo", v["L0_attn_Wo"])
    put("bo", colv(v["L0_attn_bo"]))

    def swap(a):
        a = np.asarray(a)
        return a.reshape(a.shape[0], -1, 2, FDH // 2)[:, :, ::-1].reshape(a.shape)

    def twice(a):
        return np.concatenate([a, a])

    for name, src in (("qs", "L0_ffn_q_scale"), ("ks", "L0_ffn_k_scale")):
        s = np.asarray(v[src])
        put(name, twice(s.T))
        put(name + "r", twice(swap(s).T))
    for l in range(DEPTH):
        qkv = np.asarray(v["L0_ffn_wqkv"])[l]
        q, k, vv = qkv[:, :INNER], qkv[:, INNER:2 * INNER], qkv[:, 2 * INNER:]
        put(f"fq{l}", q)
        put(f"fqr{l}", swap(q))
        put(f"fk{l}", k)
        put(f"fkr{l}", swap(k))
        put(f"fv{l}", vv)
        put(f"fo{l}", np.asarray(v["L0_ffn_wo"])[l].reshape(FP, 128, D).transpose(1, 0, 2).reshape(128, FP * D))
        put(f"w1{l}", np.asarray(v["L0_ffn_w1"])[l])
        w2 = np.zeros((128, HC, D), np.float32)
        b1 = np.zeros((128, 2 * HC), np.float32)
        for c in range(HC):
            w2[:HCN[c], c] = np.asarray(v["L0_ffn_w2"])[l][c * HCW:c * HCW + HCN[c]]
            for part in range(2):
                a = part * HID + c * HCW
                b1[:HCN[c], part * HC + c] = np.asarray(v["L0_ffn_b1"])[l][a:a + HCN[c]]
        put(f"w2{l}", w2.reshape(128, HC * D))
        put(f"b1{l}", b1)
        put(f"lg{l}", colv(np.asarray(v["L0_ffn_ln_g"])[l]))
        put(f"lb{l}", colv(np.asarray(v["L0_ffn_ln_b"])[l]))
        put(f"b2{l}", colv(np.asarray(v["L0_ffn_b2"])[l]))
    put("inp", np.asarray(v["L1_attn_in_proj_w"]).T)
    put("cw", np.asarray(v["L1_attn_conv_w"]).reshape(XBC, 128, TAPS).transpose(1, 0, 2).reshape(128, XBC * TAPS))
    put("cb", np.asarray(v["L1_attn_conv_b"]).reshape(XBC, 128).T)
    put("dtb", np.broadcast_to(np.asarray(v["L1_attn_dt_bias"]).reshape(1, MH), (128, MH)))
    put("alog", np.broadcast_to(np.asarray(v["L1_attn_A_log"]).reshape(1, MH), (128, MH)))
    put("dsk", np.repeat(np.asarray(v["L1_attn_D"]), MDH).reshape(2, 128).T)
    put("nw", np.asarray(v["L1_attn_norm_w"]).reshape(2, 128).T)
    put("outp", np.asarray(v["L1_attn_out_proj_w"]).T.reshape(2, 128, D).transpose(1, 0, 2).reshape(128, 2 * D))
    put("gw", np.asarray(v["L1_ffn_gate_w"]).T)
    put("gb", np.broadcast_to(np.asarray(v["L1_ffn_gate_b"]).reshape(1, NE), (128, NE)))
    put("ew", np.asarray(v["L1_ffn_expert_w"]).transpose(2, 0, 1).reshape(D, NE * D))
    put("eb", np.asarray(v["L1_ffn_expert_b"]).T)
    return w


def kernel(**inputs):
    import numpy as np
    import concourse.bacc as bacc
    from concourse.bass_utils import run_bass_kernel_spmd

    nc = bacc.Bacc("TRN2", target_bir_lowering=False, num_devices=1)
    w = host_layout(inputs)
    x = np.ascontiguousarray(np.asarray(inputs["L0_attn_x"]).reshape(NG, NT, 128, D).transpose(0, 2, 1, 3))
    xd = nc.dram_tensor("x", x.shape, F32, kind="ExternalInput").ap()
    wd = nc.dram_tensor("w", w.shape, F32, kind="ExternalInput").ap()
    od = nc.dram_tensor("out", x.shape, F32, kind="ExternalOutput").ap()
    tables = rotary_tables()
    td = nc.dram_tensor("tables", tables.shape, F32, kind="ExternalInput").ap()
    build(nc, xd, wd, td, od)
    r = run_bass_kernel_spmd(nc, [{"x": x, "w": w, "tables": tables}], core_ids=[0])
    got = np.asarray(r.results[0]["out"])
    return np.ascontiguousarray(got.transpose(0, 2, 1, 3)).reshape(BATCH, SEQ, D)
```
